# Optimizing a Trainium2 kernel written in Bass

```python
import numpy as np
import jax
import jax.numpy as jnp

def _softmax(x, axis=-1):
    return jax.nn.softmax(x, axis=axis)

def _gelu(x):
    return jax.nn.gelu(x, approximate=True)

def _silu(x):
    return jax.nn.silu(x)

def _sigmoid(x):
    return jax.nn.sigmoid(x)

def _layernorm(x, axis=-1, eps=1e-05):
    m = jnp.mean(x, axis=axis, keepdims=True)
    v = jnp.var(x, axis=axis, keepdims=True)
    return (x - m) / jnp.sqrt(v + eps)

def _scatter_add(tgt, idx, src, axis=0):
    return tgt.at[idx].add(src)

def _segment_sum(src, seg, n):
    return jax.ops.segment_sum(src, seg, n)
kernel_name = 'mk_decoder_preln_d2_seqx_r4_bd7a96'

def setup_inputs(seed: int=0):
    np.random.seed(seed)
    _w = jnp.asarray

    def _rec_inputs():
        import jax
        import jax.numpy as jnp
        _rk = jax.random.key(seed)
        x = -0.0002928 + 1 * jax.random.normal(jax.random.fold_in(_rk, 1), (16, 256, 256), jnp.float32)
        _lenS = 256 - jax.random.randint(jax.random.fold_in(_rk, 7), (16,), 0, max(1, 256 // 4) + 1, jnp.int32)
        _lenS2 = 77 - jax.random.randint(jax.random.fold_in(_rk, 8), (16,), 0, max(1, 77 // 4) + 1, jnp.int32)
        _ctx_1024P = jax.random.normal(jax.random.fold_in(_rk, 11), (16, 16, 256), jnp.float32)
        _ctx_1024c = jax.random.dirichlet(jax.random.fold_in(_rk, 511), 0.3 * jnp.ones((16,), jnp.float32), (16, 77))
        _ctx_1024t = jnp.einsum('bsk,bkd->bsd', _ctx_1024c, _ctx_1024P)
        _ctx_1024t = _ctx_1024t * jax.lax.rsqrt(jnp.mean(jnp.square(_ctx_1024t)) + 1e-12) * 0.953939
        ctx_1024 = -1.39393e-06 + 0.999914 * (_ctx_1024t + 0.3 * jax.random.normal(jax.random.fold_in(_rk, 611), (16, 77, 256), jnp.float32))
        _validS = jnp.arange(256)[None, :] < _lenS[:, None]
        _validS2 = jnp.arange(77)[None, :] < _lenS2[:, None]
        _causal = jnp.tril(jnp.ones((256, 256), dtype=bool))
        mask_Bx1xSxS2_ff0 = jnp.where(jnp.ones((16, 1, 256, 77), dtype=bool), 0.0, -1000000000.0).astype(jnp.float32)
        mask_SxS2_ik0 = jnp.where(jnp.broadcast_to(_validS2[0:1, :], (256, 77)), 0, 1).astype(jnp.int32)
        return (x, ctx_1024, mask_Bx1xSxS2_ff0, mask_SxS2_ik0)
    x, ctx_1024, mask_Bx1xSxS2_ff0, mask_SxS2_ik0 = _rec_inputs()

    def _L0_attn_setup():
        import jax, jax.numpy as jnp
        import numpy as np
        EPS = 1e-05
        NUM_HEADS = 16

        def _linear_attention(x, Wq, Wk, Wv, Wo, bo):
            B, L, E = x.shape
            H = NUM_HEADS
            D = E // H
            q = (x @ Wq.T).reshape(B, L, H, D)
            k = (x @ Wk.T).reshape(B, L, H, D)
            v = (x @ Wv.T).reshape(B, L, H, D)
            phi_q = jax.nn.elu(q) + 1.0
            phi_k = jax.nn.elu(k) + 1.0
            pq = jnp.moveaxis(phi_q, 1, 0)
            pk = jnp.moveaxis(phi_k, 1, 0)
            vt = jnp.moveaxis(v, 1, 0)
            S0 = jnp.zeros((B, H, D, D), x.dtype)
            z0 = jnp.zeros((B, H, D), x.dtype)

            def step(carry, inp):
                S, z = carry
                pq_t, pk_t, v_t = inp
                S = S + pk_t[..., :, None] * v_t[..., None, :]
                z = z + pk_t
                num = jnp.einsum('bhd,bhde->bhe', pq_t, S)
                den = jnp.sum(pq_t * z, axis=-1, keepdims=True) + EPS
                return ((S, z), num / den)
            (_, _), out = jax.lax.scan(step, (S0, z0), (pq, pk, vt))
            out = jnp.moveaxis(out, 0, 1).reshape(B, L, E)
            return out @ Wo.T + bo
        key = jax.random.key(seed)
        ks = jax.random.split(key, 6)
        B, L, E = (4, 1024, 256)
        s = 1.0 / np.sqrt(E)
        return {'x': jax.random.normal(ks[0], (B, L, E), jnp.float32), 'Wq': jax.random.normal(ks[1], (E, E), jnp.float32) * s, 'Wk': jax.random.normal(ks[2], (E, E), jnp.float32) * s, 'Wv': jax.random.normal(ks[3], (E, E), jnp.float32) * s, 'Wo': jax.random.normal(ks[4], (E, E), jnp.float32) * s, 'bo': jnp.zeros((E,), jnp.float32)}
    _L0_attn_all = _L0_attn_setup()
    _L0_attn_in = {k: v for k, v in _L0_attn_all.items() if k in ('Wq', 'Wk', 'Wv', 'Wo', 'bo')}
    del _L0_attn_all

    def _L0_xattn_setup():
        import jax, jax.numpy as jnp
        import numpy as np
        HIDDEN = 256
        NUM_HEADS = 16
        HEAD_DIM = HIDDEN // NUM_HEADS
        B, F, T = (2, 512, 512)
        key = jax.random.key(seed)
        ks = jax.random.split(key, 6)
        return {'query_input': jax.random.normal(ks[0], (B, F, HIDDEN), dtype=jnp.float32), 'source_input': jax.random.normal(ks[1], (B, T, HIDDEN), dtype=jnp.float32), 'bias': jnp.zeros((B, 1, F, T), dtype=jnp.float32), 'wq': jax.random.normal(ks[2], (HIDDEN, NUM_HEADS, HEAD_DIM), dtype=jnp.float32) * (1.0 / np.sqrt(HIDDEN)), 'wk': jax.random.normal(ks[3], (HIDDEN, NUM_HEADS, HEAD_DIM), dtype=jnp.float32) * (1.0 / np.sqrt(HIDDEN)), 'wv': jax.random.normal(ks[4], (HIDDEN, NUM_HEADS, HEAD_DIM), dtype=jnp.float32) * (1.0 / np.sqrt(HIDDEN)), 'wo': jax.random.normal(ks[5], (NUM_HEADS, HEAD_DIM, HIDDEN), dtype=jnp.float32) * (1.0 / np.sqrt(HIDDEN))}
    _L0_xattn_all = _L0_xattn_setup()
    _L0_xattn_in = {k: v for k, v in _L0_xattn_all.items() if k in ('wq', 'wk', 'wv', 'wo')}
    del _L0_xattn_all

    def _L0_ffn_setup():
        import jax, jax.numpy as jnp
        import numpy as np
        D_MODEL = 256
        D_FF = 512
        NUM_EXPERTS = 16
        TOP_K = 2
        CAPACITY_FACTOR = 1.25
        BATCH, SEQ = (4, 512)
        key = jax.random.key(seed)
        k0, k1, k2, k3 = jax.random.split(key, 4)
        x = jax.random.normal(k0, (BATCH, SEQ, D_MODEL), jnp.float32)
        gate_w = jax.random.normal(k1, (NUM_EXPERTS, D_MODEL), jnp.float32) / np.float32(np.sqrt(D_MODEL))
        w1 = jax.random.normal(k2, (NUM_EXPERTS, D_MODEL, D_FF), jnp.float32) / np.float32(np.sqrt(D_MODEL))
        w2 = jax.random.normal(k3, (NUM_EXPERTS, D_FF, D_MODEL), jnp.float32) / np.float32(np.sqrt(D_FF))
        return {'x': x, 'gate_w': gate_w, 'w1': w1, 'w2': w2}
    _L0_ffn_all = _L0_ffn_setup()
    _L0_ffn_in = {k: v for k, v in _L0_ffn_all.items() if k in ('gate_w', 'w1', 'w2')}
    del _L0_ffn_all

    def _L1_attn_setup():
        import jax, jax.numpy as jnp
        import numpy as np
        B, T = (4, 512)
        D_MODEL = 256
        N_HEADS = 8
        HEAD_DIM = 64
        KV_LRANK = 64

        def _orthogonalize_per_head(w):
            chunks = w.reshape(N_HEADS, HEAD_DIM, D_MODEL)

            def ns(m):
                A = m @ m.T
                Bm = 1.5 * jnp.eye(HEAD_DIM, dtype=m.dtype) - 0.5 * A
                return Bm @ m
            return jax.vmap(ns)(chunks).reshape(w.shape)
        key = jax.random.key(seed)
        ks = jax.random.split(key, 6)

        def lin(k, out_dim, in_dim):
            bound = 1.0 / np.sqrt(in_dim)
            return jax.random.uniform(k, (out_dim, in_dim), jnp.float32, -bound, bound)
        Wq = _orthogonalize_per_head(lin(ks[0], N_HEADS * HEAD_DIM, D_MODEL))
        return {'x': jax.random.normal(ks[1], (B, T, D_MODEL), jnp.float32), 'Wq': Wq, 'Wkv_down': lin(ks[2], KV_LRANK, D_MODEL), 'Wk_up': lin(ks[3], N_HEADS * HEAD_DIM, KV_LRANK), 'Wv_up': lin(ks[4], N_HEADS * HEAD_DIM, KV_LRANK), 'Wo': lin(ks[5], D_MODEL, N_HEADS * HEAD_DIM)}
    _L1_attn_all = _L1_attn_setup()
    _L1_attn_in = {k: v for k, v in _L1_attn_all.items() if k in ('Wq', 'Wkv_down', 'Wk_up', 'Wv_up', 'Wo')}
    del _L1_attn_all

    def _L1_xattn_setup():
        import jax, jax.numpy as jnp
        import numpy as np
        B, S, D = (4, 1024, 256)
        NUM_Q_HEADS = 16
        D_K = D // NUM_Q_HEADS
        INIT_SCALE = 0.02
        key = jax.random.key(seed)
        ks = jax.random.split(key, 11)
        s = INIT_SCALE
        return {'Q': jax.random.normal(ks[0], (B, S, D), dtype=jnp.float32), 'K': jax.random.normal(ks[1], (B, S, D), dtype=jnp.float32), 'V': jax.random.normal(ks[2], (B, S, D), dtype=jnp.float32), 'Wq': jax.random.normal(ks[3], (D, D), dtype=jnp.float32) * s, 'bq': jnp.zeros((D,), jnp.float32), 'Wk': jax.random.normal(ks[4], (D, D), dtype=jnp.float32) * s, 'bk': jnp.zeros((D,), jnp.float32), 'Wv': jax.random.normal(ks[5], (D, D), dtype=jnp.float32) * s, 'bv': jnp.zeros((D,), jnp.float32), 'Wo': jax.random.normal(ks[6], (D, D), dtype=jnp.float32) * s, 'bo': jnp.zeros((D,), jnp.float32), 'mask': jnp.tril(jnp.ones((S, S), dtype=jnp.int32))}
    _L1_xattn_all = _L1_xattn_setup()
    _L1_xattn_in = {k: v for k, v in _L1_xattn_all.items() if k in ('Wq', 'bq', 'Wk', 'bk', 'Wv', 'bv', 'Wo', 'bo')}
    del _L1_xattn_all

    def _L1_ffn_setup():
        import jax, jax.numpy as jnp
        import numpy as np
        BLOCK = 32
        W_BITS = 4
        ACT_BITS = 16

        def act_qdq(x):
            qmax = 2.0 ** (ACT_BITS - 1) - 1.0
            scale = jnp.maximum(jnp.max(jnp.abs(x)) / qmax, 1e-12)
            return jnp.clip(jnp.round(x / scale), -qmax - 1.0, qmax) * scale

        def fixed_qdq_u16(x):
            scale = 1.0 / 65536.0
            return jnp.clip(jnp.round(x / scale), 0.0, 65535.0) * scale

        def lpbq_dequant(w):
            O, I = w.shape
            qmax = 2.0 ** (W_BITS - 1) - 1.0
            wb = w.reshape(O, I // BLOCK, BLOCK)
            s = jnp.maximum(jnp.max(jnp.abs(wb), axis=-1, keepdims=True) / qmax, 1e-12)
            wq = jnp.clip(jnp.round(wb / s), -qmax - 1.0, qmax) * s
            return wq.reshape(O, I)
        key = jax.random.key(seed)
        k1, k2, k3, k4 = jax.random.split(key, 4)
        B, S, H, I = (2, 1024, 256, 768)
        x = jax.random.normal(k1, (B, S, H), jnp.float32)
        w_gate = jax.random.normal(k2, (I, H), jnp.float32) * 0.02
        w_up = jax.random.normal(k3, (I, H), jnp.float32) * 0.02
        w_down = jax.random.normal(k4, (H, I), jnp.float32) * 0.02
        return {'x': x, 'w_gate': w_gate, 'w_up': w_up, 'w_down': w_down}
    _L1_ffn_all = _L1_ffn_setup()
    _L1_ffn_in = {k: v for k, v in _L1_ffn_all.items() if k in ('w_gate', 'w_up', 'w_down')}
    del _L1_ffn_all
    return {'x': x, 'ctx_1024': ctx_1024, 'mask_Bx1xSxS2_ff0': mask_Bx1xSxS2_ff0, 'mask_SxS2_ik0': mask_SxS2_ik0, 'L0_attn_Wq': _L0_attn_in['Wq'], 'L0_attn_Wk': _L0_attn_in['Wk'], 'L0_attn_Wv': _L0_attn_in['Wv'], 'L0_attn_Wo': _L0_attn_in['Wo'], 'L0_attn_bo': _L0_attn_in['bo'], 'L0_xattn_wq': _L0_xattn_in['wq'], 'L0_xattn_wk': _L0_xattn_in['wk'], 'L0_xattn_wv': _L0_xattn_in['wv'], 'L0_xattn_wo': _L0_xattn_in['wo'], 'L0_ffn_gate_w': _L0_ffn_in['gate_w'], 'L0_ffn_w1': _L0_ffn_in['w1'], 'L0_ffn_w2': _L0_ffn_in['w2'], 'L1_attn_Wq': _L1_attn_in['Wq'], 'L1_attn_Wkv_down': _L1_attn_in['Wkv_down'], 'L1_attn_Wk_up': _L1_attn_in['Wk_up'], 'L1_attn_Wv_up': _L1_attn_in['Wv_up'], 'L1_attn_Wo': _L1_attn_in['Wo'], 'L1_xattn_Wq': _L1_xattn_in['Wq'], 'L1_xattn_bq': _L1_xattn_in['bq'], 'L1_xattn_Wk': _L1_xattn_in['Wk'], 'L1_xattn_bk': _L1_xattn_in['bk'], 'L1_xattn_Wv': _L1_xattn_in['Wv'], 'L1_xattn_bv': _L1_xattn_in['bv'], 'L1_xattn_Wo': _L1_xattn_in['Wo'], 'L1_xattn_bo': _L1_xattn_in['bo'], 'L1_ffn_w_gate': _L1_ffn_in['w_gate'], 'L1_ffn_w_up': _L1_ffn_in['w_up'], 'L1_ffn_w_down': _L1_ffn_in['w_down']}

def reference(x, ctx_1024, mask_Bx1xSxS2_ff0, mask_SxS2_ik0, L0_attn_Wq, L0_attn_Wk, L0_attn_Wv, L0_attn_Wo, L0_attn_bo, L0_xattn_wq, L0_xattn_wk, L0_xattn_wv, L0_xattn_wo, L0_ffn_gate_w, L0_ffn_w1, L0_ffn_w2, L1_attn_Wq, L1_attn_Wkv_down, L1_attn_Wk_up, L1_attn_Wv_up, L1_attn_Wo, L1_xattn_Wq, L1_xattn_bq, L1_xattn_Wk, L1_xattn_bk, L1_xattn_Wv, L1_xattn_bv, L1_xattn_Wo, L1_xattn_bo, L1_ffn_w_gate, L1_ffn_w_up, L1_ffn_w_down):
    import jax
    import jax.numpy as jnp

    def _L0_attn_ref(x, Wq, Wk, Wv, Wo, bo):
        import jax, jax.numpy as jnp
        import numpy as np
        EPS = 1e-05
        NUM_HEADS = 16

        def _linear_attention(x, Wq, Wk, Wv, Wo, bo):
            B, L, E = x.shape
            H = NUM_HEADS
            D = E // H
            q = (x @ Wq.T).reshape(B, L, H, D)
            k = (x @ Wk.T).reshape(B, L, H, D)
            v = (x @ Wv.T).reshape(B, L, H, D)
            phi_q = jax.nn.elu(q) + 1.0
            phi_k = jax.nn.elu(k) + 1.0
            pq = jnp.moveaxis(phi_q, 1, 0)
            pk = jnp.moveaxis(phi_k, 1, 0)
            vt = jnp.moveaxis(v, 1, 0)
            S0 = jnp.zeros((B, H, D, D), x.dtype)
            z0 = jnp.zeros((B, H, D), x.dtype)

            def step(carry, inp):
                S, z = carry
                pq_t, pk_t, v_t = inp
                S = S + pk_t[..., :, None] * v_t[..., None, :]
                z = z + pk_t
                num = jnp.einsum('bhd,bhde->bhe', pq_t, S)
                den = jnp.sum(pq_t * z, axis=-1, keepdims=True) + EPS
                return ((S, z), num / den)
            (_, _), out = jax.lax.scan(step, (S0, z0), (pq, pk, vt))
            out = jnp.moveaxis(out, 0, 1).reshape(B, L, E)
            return out @ Wo.T + bo
        return _linear_attention(x, Wq, Wk, Wv, Wo, bo)

    def _L0_xattn_ref(query_input, source_input, bias, wq, wk, wv, wo):
        import jax, jax.numpy as jnp
        import numpy as np
        HIDDEN = 256
        NUM_HEADS = 16
        HEAD_DIM = HIDDEN // NUM_HEADS
        B, F, T = (2, 512, 512)
        q = jnp.einsum('bfd,dnh->bfnh', query_input, wq)
        k = jnp.einsum('btd,dnh->btnh', source_input, wk)
        v = jnp.einsum('btd,dnh->btnh', source_input, wv)
        q = q * HEAD_DIM ** (-0.5)
        logits = jnp.einsum('btnh,bfnh->bnft', k, q) + bias
        weights = jax.nn.softmax(logits, axis=-1)
        attn = jnp.einsum('bnft,btnh->bfnh', weights, v)
        return jnp.einsum('bfnh,nhd->bfd', attn, wo)

    def _L0_ffn_ref(x, gate_w, w1, w2):
        import jax, jax.numpy as jnp
        import numpy as np
        D_MODEL = 256
        D_FF = 512
        NUM_EXPERTS = 16
        TOP_K = 2
        CAPACITY_FACTOR = 1.25
        BATCH, SEQ = (4, 512)
        B, S, d = x.shape
        T = B * S
        E, K = (NUM_EXPERTS, TOP_K)
        capacity = int(CAPACITY_FACTOR * T * K / E)
        xf = x.reshape(T, d)
        logits = xf @ gate_w.T
        probs = jax.nn.sigmoid(logits)
        top_vals, sel = jax.lax.top_k(probs, K)
        weights = top_vals / (top_vals.sum(-1, keepdims=True) + 1e-06)
        flat_sel = sel.reshape(-1)
        onehot = jax.nn.one_hot(flat_sel, E, dtype=jnp.int32)
        ranks = jnp.take_along_axis(jnp.cumsum(onehot, axis=0), flat_sel[:, None], axis=1)[:, 0] - 1
        valid = ranks < capacity
        sentinel = E * capacity
        slot = jnp.where(valid, flat_sel * capacity + ranks, sentinel)
        x_rep = jnp.repeat(xf, K, axis=0)
        padded = jnp.zeros((sentinel + 1, d), xf.dtype).at[slot].set(x_rep)
        padded = padded[:sentinel].reshape(E, capacity, d)
        h = jax.nn.gelu(jnp.einsum('ecd,edf->ecf', padded, w1), approximate=False)
        out_padded = jnp.einsum('ecf,efd->ecd', h, w2).reshape(sentinel, d)
        gathered = out_padded[jnp.minimum(slot, sentinel - 1)]
        gathered = jnp.where(valid[:, None], gathered, jnp.zeros((), xf.dtype))
        out = (gathered * weights.reshape(-1)[:, None]).reshape(T, K, d).sum(axis=1)
        return out.reshape(B, S, d)

    def _L1_attn_ref(x, Wq, Wkv_down, Wk_up, Wv_up, Wo):
        import jax, jax.numpy as jnp
        import numpy as np
        B, T = (4, 512)
        D_MODEL = 256
        N_HEADS = 8
        HEAD_DIM = 64
        KV_LRANK = 64

        def _orthogonalize_per_head(w):
            chunks = w.reshape(N_HEADS, HEAD_DIM, D_MODEL)

            def ns(m):
                A = m @ m.T
                Bm = 1.5 * jnp.eye(HEAD_DIM, dtype=m.dtype) - 0.5 * A
                return Bm @ m
            return jax.vmap(ns)(chunks).reshape(w.shape)
        b, t, _ = x.shape
        q = (x @ Wq.T).reshape(b, t, N_HEADS, HEAD_DIM)
        kv_latent = x @ Wkv_down.T
        k = (kv_latent @ Wk_up.T).reshape(b, t, N_HEADS, HEAD_DIM)
        v = (kv_latent @ Wv_up.T).reshape(b, t, N_HEADS, HEAD_DIM)
        scale = HEAD_DIM ** (-0.5)
        scores = jnp.einsum('bqhd,bkhd->bhqk', q, k) * scale
        attn = jax.nn.softmax(scores, axis=-1)
        out = jnp.einsum('bhqk,bkhd->bqhd', attn, v)
        out = out.reshape(b, t, N_HEADS * HEAD_DIM)
        return out @ Wo.T

    def _L1_xattn_ref(Q, K, V, Wq, bq, Wk, bk, Wv, bv, Wo, bo, mask):
        import jax, jax.numpy as jnp
        import numpy as np
        B, S, D = (4, 1024, 256)
        NUM_Q_HEADS = 16
        D_K = D // NUM_Q_HEADS
        INIT_SCALE = 0.02
        q = Q @ Wq + bq
        k = K @ Wk + bk
        v = V @ Wv + bv
        scale = 1.0 / np.sqrt(D_K).astype(np.float32)
        scores = jnp.einsum('bqd,bkd->bqk', q, k) * scale
        scores = jnp.where(mask == 0, jnp.asarray(-1000000000.0, scores.dtype), scores)
        probs = jax.nn.softmax(scores, axis=-1)
        attn = jnp.einsum('bqk,bkd->bqd', probs, v)
        return attn @ Wo + bo

    def _L1_ffn_ref(x, w_gate, w_up, w_down):
        import jax, jax.numpy as jnp
        import numpy as np
        BLOCK = 32
        W_BITS = 4
        ACT_BITS = 16

        def act_qdq(x):
            qmax = 2.0 ** (ACT_BITS - 1) - 1.0
            scale = jnp.maximum(jnp.max(jnp.abs(x)) / qmax, 1e-12)
            return jnp.clip(jnp.round(x / scale), -qmax - 1.0, qmax) * scale

        def fixed_qdq_u16(x):
            scale = 1.0 / 65536.0
            return jnp.clip(jnp.round(x / scale), 0.0, 65535.0) * scale

        def lpbq_dequant(w):
            O, I = w.shape
            qmax = 2.0 ** (W_BITS - 1) - 1.0
            wb = w.reshape(O, I // BLOCK, BLOCK)
            s = jnp.maximum(jnp.max(jnp.abs(wb), axis=-1, keepdims=True) / qmax, 1e-12)
            wq = jnp.clip(jnp.round(wb / s), -qmax - 1.0, qmax) * s
            return wq.reshape(O, I)
        x = act_qdq(x)
        up = act_qdq(x @ lpbq_dequant(w_up).T)
        gate = act_qdq(x @ lpbq_dequant(w_gate).T)
        sig = fixed_qdq_u16(jax.nn.sigmoid(gate))
        gate = act_qdq(gate * sig)
        o = act_qdq(gate * up)
        return o @ lpbq_dequant(w_down).T
    x = x + _L0_attn_ref(_layernorm(x, axis=-1), L0_attn_Wq, L0_attn_Wk, L0_attn_Wv, L0_attn_Wo, L0_attn_bo)
    x = x + _L0_xattn_ref(_layernorm(x, axis=-1), ctx_1024, mask_Bx1xSxS2_ff0, L0_xattn_wq, L0_xattn_wk, L0_xattn_wv, L0_xattn_wo)
    x = x + _L0_ffn_ref(_layernorm(x, axis=-1), L0_ffn_gate_w, L0_ffn_w1, L0_ffn_w2)
    x = x + _L1_attn_ref(_layernorm(x, axis=-1), L1_attn_Wq, L1_attn_Wkv_down, L1_attn_Wk_up, L1_attn_Wv_up, L1_attn_Wo)
    x = x + _L1_xattn_ref(_layernorm(x, axis=-1), ctx_1024, ctx_1024, L1_xattn_Wq, L1_xattn_bq, L1_xattn_Wk, L1_xattn_bk, L1_xattn_Wv, L1_xattn_bv, L1_xattn_Wo, L1_xattn_bo, mask_SxS2_ik0)
    x = x + _L1_ffn_ref(_layernorm(x, axis=-1), L1_ffn_w_gate, L1_ffn_w_up, L1_ffn_w_down)
    return x

_drawn_inputs = setup_inputs


def setup_inputs(seed=0):
    import zlib

    import numpy as np

    out = dict(_drawn_inputs(seed))
    spreads = {'L0_attn_bo': (0.0, 0.1),
     'L1_xattn_bq': (0.0, 0.8),
     'L1_xattn_bk': (0.0, 0.8),
     'L1_xattn_bv': (0.0, 0.308),
     'L1_xattn_bo': (0.0, 0.1)}
    factors = {'L1_attn_Wq': 8.0, 'L1_attn_Wk_up': 8.0, 'L1_xattn_Wq': 4.733, 'L1_xattn_Wk': 4.651}
    for name, (base, spread) in spreads.items():
        noise = np.random.default_rng([zlib.crc32(name.encode()), seed]).standard_normal(out[name].shape)
        drawn = base * np.exp(spread * noise) if base else spread * noise
        out[name] = jnp.asarray(drawn.astype(out[name].dtype))
    for name, factor in factors.items():
        out[name] = (out[name] * factor).astype(out[name].dtype)
    return out
```

```python
import numpy as np
import concourse.bass as bass
from concourse import mybir
from collections import namedtuple
from contextlib import ExitStack

F32 = mybir.dt.float32
BF16 = mybir.dt.bfloat16
I32 = mybir.dt.int32
U32 = mybir.dt.uint32
I16 = mybir.dt.int16
U16 = mybir.dt.uint16
ALU = mybir.AluOpType
ACT = mybir.ActivationFunctionType
AX = mybir.AxisListType
RMAX = bass.bass_isa.ReduceOp.max

B, S, D = 16, 256, 256
S2 = 77
H, HD = 16, 16
T = 512
NT = T // 128
NB = T // S
NG = B * S // T
E, TOPK = 16, 2
CAP = int(1.25 * B * S * TOPK / E)
SLOTS = E * CAP
FF0 = 512
H1, HD1 = 8, 64
LR = 64
FF1 = 768
FC = FF1 // 128
BLK = 32
LN_EPS = 1e-5
DEN_EPS = 1e-5
QMAX = 32767.0
WMAX = 7.0


def signals(nc, ctx, names):
    return namedtuple("Signals", names)(*[ctx.enter_context(nc.semaphore(name)) for name in names.split()])


def clear(nc, q):
    numbers = sorted(s.num for s in q)
    while numbers:
        run = 1
        while run < len(numbers) and numbers[run] == numbers[0] + run:
            run += 1
        nc.gpsimd.sem_clear(range(numbers[0], numbers[0] + run))
        numbers = numbers[run:]
    nc.all_engine_barrier()


def bcast(ap, axis, n):
    shape = list(ap.shape)
    shape.insert(axis, n)
    return ap.unsqueeze(axis).broadcast_to(shape)


class Norm:

    def __init__(self, nc, ctx, tag):
        sb = lambda name, shape: ctx.enter_context(nc.sbuf_tensor(f"{tag}_{name}", shape, F32))
        self.stats = sb("stats", [128, NT, 6])
        self.mv = sb("mean_var", [128, NT, 2])
        self.ve = sb("var_eps", [128, NT])
        self.rstd = sb("rstd", [128, NT])
        self.power = sb("power", [128, NT])
        self.h = sb("h", [128, NT, D])

    def vector(self, v, q, src, n):
        for j in range(NT):
            v.bn_stats(self.stats[:, j, :], src[:, j, :]).then_inc(q.ln_stats, 1)
        v.wait_ge(q.ln_stats, NT * (n + 1))
        for j in range(NT):
            v.bn_aggr(self.mv[:, j, :], self.stats[:, j, :]).then_inc(q.ln_moments, 1)
        v.wait_ge(q.ln_moments, NT * (n + 1))
        v.tensor_scalar(self.ve[:, :], self.mv[:, :, 1], LN_EPS, None, ALU.add).then_inc(q.ln_var, 1)
        v.wait_ge(q.ln_rstd, n + 1)
        for j in range(NT):
            v.tensor_scalar(self.h[:, j, :], src[:, j, :], self.mv[:, j, 0:1], self.rstd[:, j:j + 1],
                            ALU.subtract, ALU.mult).then_inc(q.ln_h, 1)

    def gpsimd(self, g, q, n):
        g.wait_ge(q.ln_var, n + 1)
        g.tensor_tensor(self.rstd[:, :], self.ve[:, :], self.power[:, :], ALU.pow).then_inc(q.ln_rstd, 1)

    def tensor(self, p, q, n, banks, ident):
        for j in range(NT):
            p.wait_ge(q.ln_h, NT * n + j + 1)
            for c in range(2):
                t = p.transpose(banks[c][:, 128 * j:128 * j + 128], self.h[:, j, 128 * c:128 * c + 128], ident)
        t.then_inc(q.hT_psum, 1)

    def scalar(self, a, q, n, banks, hT):
        a.wait_ge(q.hT_psum, n + 1)
        for c in range(2):
            a.activation(hT[:, c, :], banks[c][:, :], ACT.Copy).then_inc(q.hT_ready, 1)


def fill_selector(g, q, out, conditions):
    n = q[1]
    g.memset(out, 1.0).then_inc(q[0], 1)
    n += 1
    for base, mult, pattern, op in conditions:
        g.wait_ge(q[0], n)
        g.affine_select(out=out, in_=out, pattern=pattern, base=base, channel_multiplier=mult,
                        compare_op=op, fill=0.0).then_inc(q[0], 1)
        n += 1
    q[1] = n
    return n


def layer0(nc, ctx, c, io, dr):
    st = ExitStack()
    with st:
        def sb(name, shape, dt=F32):
            return st.enter_context(nc.sbuf_tensor("a_" + name, shape, dt))
        P = c.banks
        ident = c.ident[:, :]
        wq, wk, wv, wo = (sb(n, [128, 2, D]) for n in ("wq", "wk", "wv", "wo"))
        xwq, xwk, xwv, xwo = (sb(n, [128, 2, D]) for n in ("xwq", "xwk", "xwv", "xwo"))
        wg = sb("wg", [128, 2, E])
        bo = sb("bo", [128, D])
        causal = sb("causal", [128, 384])
        headsel = sb("headsel", [128, 8])
        before = sb("before", [128, 128], BF16)
        ones = sb("ones", [128, 128], BF16)
        eid = sb("eid", [128, E])
        carry = sb("carry", [128, E])
        left = sb("left", [128, 1])
        zeros = sb("zeros", [128, 2048])

        norm0, norm, norm2 = Norm(nc, st, "a0"), Norm(nc, st, "a1"), Norm(nc, st, "a2")
        xin = sb("xin", [128, NT, D])
        x1 = sb("x1", [128, NT, D])
        x2 = sb("x2", [128, NT, D])
        hT0 = sb("hT0", [128, 2, T])
        hT = sb("hT", [128, 2, T])
        eq = sb("eq", [128, 2, T])
        ek = sb("ek", [128, 2, T])
        pq = sb("pq", [128, 2, T])
        pk = sb("pk", [128, 2, T])
        kbd = sb("kbd", [128, NB, 2, 8, S])
        vpad = sb("vpad", [128, NT, H, 32])
        A = sb("A", [128, 8, 384])
        oT = sb("oT", [128, 4, T])
        rden = sb("rden", [128, NT, H])
        den = sb("den", [128, NT, H])
        at = sb("at", [128, NT, D])
        aT = sb("aT", [128, 2, T])

        ctxT = sb("ctxT", [128, 2, NB, S2])
        amask = sb("amask", [128, NT, S2])
        xqT = sb("xqT", [128, 2, T])
        xkbd = sb("xkbd", [128, NB, 2, 8, S2])
        xvpad = sb("xvpad", [S2, NB, H, 32])
        L = sb("L", [128, 3, H, S2])
        Lm = sb("Lm", [128, NT, H])
        L2 = sb("L2", [128, 3, H, S2])
        PT = kbd[0:S2, :, :, :, :].rearrange("k b u h t -> k b (u h) t")

        lg = sb("lg", [128, NT, E])
        top = sb("top", [128, NT, 8])
        topi = sb("topi", [128, NT, 8], U32)
        topf = sb("topf", [128, NT, TOPK])
        oh = sb("oh", [128, TOPK, NT, E])
        M = sb("M", [128, NT, E], BF16)
        rank = sb("rank", [128, NT, E])
        pick = sb("pick", [128, TOPK, NT, E])
        r = sb("r", [128, TOPK, NT])
        valid = sb("valid", [128, TOPK, NT])
        slot = sb("slot", [128, TOPK, NT])
        drop = sb("drop", [128, TOPK, NT])
        slot_s = sb("slot_s", [128, TOPK, NT], I32)
        slot_g = sb("slot_g", [128, TOPK, NT], I32)
        prob = sb("prob", [128, TOPK, NT])
        psum2 = sb("psum2", [128, NT])
        wt = sb("wt", [128, TOPK, NT])

        with ExitStack() as once:
            q = signals(nc, once, "a_w a_const a_dve")
            with nc.Block() as block:
                @block.sync
                def _(s):
                    n = 0
                    for dst, src in ((wq, io["L0_attn_Wq"]), (wk, io["L0_attn_Wk"]), (wv, io["L0_attn_Wv"]),
                                     (wo, io["L0_attn_Wo"]), (xwq, io["L0_xattn_wq"]), (xwk, io["L0_xattn_wk"]),
                                     (xwv, io["L0_xattn_wv"]), (xwo, io["L0_xattn_wo"]), (wg, io["L0_ffn_gate_w"])):
                        s.dma_start(dst[:, :, :], src.rearrange("(c p) n -> p c n", p=128)).then_inc(q.a_w, 16)
                        n += 16
                    s.dma_start(bo[:, :], io["L0_attn_bo"].unsqueeze(0).broadcast_to([128, D])).then_inc(q.a_w, 16)
                    n += 16
                    s.wait_ge(q.a_w, n)

                @block.vector
                def _(v):
                    v.memset(zeros[:, :], 0.0).then_inc(q.a_dve, 1)
                    v.memset(vpad[:, :, :, :], 0.0).then_inc(q.a_dve, 1)
                    v.memset(xvpad[:, :, :, :], 0.0).then_inc(q.a_dve, 1)
                    v.memset(carry[:, :], 0.0).then_inc(q.a_dve, 1)
                    v.memset(ones[:, :], 1.0).then_inc(q.a_dve, 1)
                    v.wait_ge(q.a_dve, 5)
                    v.memset(vpad[:, :, :, HD:HD + 1], 1.0).then_inc(q.a_dve, 1)
                    v.memset(xvpad[:, :, :, HD:HD + 1], 1.0).then_inc(q.a_dve, 1)

                @block.gpsimd
                def _(g):
                    k = [q.a_const, 0]
                    fill_selector(g, k, headsel[:, :], [(0, 1, [[-16, 8]], ALU.is_ge), (15, -1, [[16, 8]], ALU.is_ge)])
                    fill_selector(g, k, causal[:, 0:128], [(0, -1, [[1, 128]], ALU.is_ge)])
                    g.memset(causal[:, 128:256], 1.0)
                    fill_selector(g, k, causal[:, 256:384], [(0, -1, [[1, 128]], ALU.is_ge)])
                    fill_selector(g, k, before[:, :], [(0, -1, [[1, 128]], ALU.is_gt)])
                    g.iota(eid[:, :], [[1, E]], base=0, channel_multiplier=0, allow_small_or_imprecise_dtypes=True)
                    for m in (norm0, norm, norm2):
                        g.memset(m.power[:, :], -0.5)
            clear(nc, q)

        q = signals(nc, st, "x_in ctx_in next_in ln_stats ln_moments ln_var ln_rstd ln_h hT_psum hT_ready q_psum k_psum "
                            "v_psum eq_ready ek_ready eq_min ek_min pq_ready pk_ready kbd_ready kbd1_ready v_ready s_psum A_ready "
                            "o_psum oT_ready tok_psum den_ready rden_ready at_ready aT_psum aT_ready proj_psum xb_ready x1_ready "
                            "xk_psum xv_psum xq_psum xkbd_ready xv_ready xq_ready l_psum L_ready Lm_ready L2_ready "
                            "exp_ready pt_psum PT_ready x2_ready gate_psum lg_ready top_ready topi_ready router "
                            "eneg rank_psum slots_ready stored kept zeroed")
        scattered = c.scattered
        x_rows = io["x"].rearrange("(i j p) n -> i p j n", p=128, j=NT)
        y_rows = dr["x_a"].rearrange("(i j p) n -> i p j n", p=128, j=NT)
        ctx_cols = io["ctxT"].rearrange("(i b) (c p) k -> i c p b k", b=NB, p=128)
        mask_rows = io["mask_Bx1xSxS2_ff0"].rearrange("(i j p) k -> i p j k", p=128, j=NT)
        slot_rows = dr["slots_in"].rearrange("(a p r) n -> a p (r n)", p=128, r=8)

        def router_scalar(a):
            a.wait_ge(q.top_ready, NT)
            a.activation(prob[:, :, :], top[:, :, 0:TOPK].rearrange("p j k -> p k j"), ACT.Exp, scale=-1.0).then_inc(q.eneg, 1)

        def router_logits(p):
            for j in range(NT):
                for u in range(2):
                    t = p.matmul(P[6][:, E * j:E * j + E], hT[:, u, 128 * j:128 * j + 128], wg[:, u, :], start=(u == 0), stop=(u == 1))
            t.then_inc(q.gate_psum, 1)

        def router_choose(v):
            v.wait_ge(q.gate_psum, 1)
            v.tensor_copy(lg[:, :, :], P[6][:, 0:NT * E].rearrange("p (j e) -> p j e", e=E)).then_inc(q.lg_ready, 1)
            v.wait_ge(q.lg_ready, 1)
            for j in range(NT):
                v.max(top[:, j, :], lg[:, j, :]).then_inc(q.top_ready, 1)
            v.wait_ge(q.top_ready, NT)
            for j in range(NT):
                v.max_index(topi[:, j, :], top[:, j, :], lg[:, j, :]).then_inc(q.topi_ready, 1)
            v.wait_ge(q.topi_ready, NT)
            v.tensor_copy(topf[:, :, :], topi[:, :, 0:TOPK]).then_inc(q.router, 1)
            v.wait_ge(q.router, 1)
            for k in range(TOPK):
                v.tensor_tensor(oh[:, k, :, :], bcast(eid[:, :], 1, NT), bcast(topf[:, :, k], 2, E), ALU.is_equal).then_inc(q.router, 1)
            v.wait_ge(q.router, 3)
            v.tensor_tensor(M[:, :, :], oh[:, 0, :, :], oh[:, 1, :, :], ALU.add).then_inc(q.kept, 1)

        def router_rank(p):
            p.wait_ge(q.kept, 1)
            for j in range(NT + 1):
                if j < NT:
                    p.matmul(P[6][:, E * j:E * j + E], before[:, :], M[:, j, :], start=True, stop=(j == 0))
                for k in range(j):
                    t = p.matmul(P[6][:, E * j:E * j + E], ones[:, :], M[:, k, :], start=(j == NT and k == 0), stop=(k == j - 1))
            t.then_inc(q.rank_psum, 1)

        def router_place(v):
            steps = [3]

            def step(ins):
                ins.then_inc(q.router, 1)
                steps[0] += 1
                v.wait_ge(q.router, steps[0])

            v.wait_ge(q.eneg, 1)
            step(v.tensor_scalar(prob[:, :, :], prob[:, :, :], 1.0, None, ALU.add))
            step(v.reciprocal(prob[:, :, :], prob[:, :, :]))
            step(v.tensor_tensor(psum2[:, :], prob[:, 0, :], prob[:, 1, :], ALU.add))
            step(v.tensor_scalar(psum2[:, :], psum2[:, :], 1e-6, None, ALU.add))
            step(v.reciprocal(psum2[:, :], psum2[:, :]))
            step(v.tensor_tensor(wt[:, :, :], prob[:, :, :], bcast(psum2[:, :], 1, TOPK), ALU.mult))
            v.wait_ge(q.rank_psum, 1)
            step(v.tensor_tensor(rank[:, :, :], P[6][:, 0:NT * E].rearrange("p (j e) -> p j e", e=E), bcast(carry[:, :], 1, NT), ALU.add))
            step(v.tensor_tensor(carry[:, :], P[6][:, NT * E:NT * E + E], carry[:, :], ALU.add))
            for k in range(TOPK):
                step(v.tensor_tensor(pick[:, k, :, :], oh[:, k, :, :], rank[:, :, :], ALU.mult))
            step(v.tensor_reduce(r[:, :, :], pick[:, :, :, :], AX.X, ALU.add))
            step(v.tensor_scalar(valid[:, :, :], r[:, :, :], float(CAP), None, ALU.is_lt))
            step(v.scalar_tensor_tensor(slot[:, :, :], topf[:, :, :].rearrange("p j k -> p k j"), float(CAP), r[:, :, :], ALU.mult, ALU.add))
            step(v.tensor_scalar(drop[:, :, :], valid[:, :, :], -float(4 * SLOTS), float(4 * SLOTS), ALU.mult, ALU.add))
            step(v.tensor_tensor(slot[:, :, :], slot[:, :, :], drop[:, :, :], ALU.add))
            step(v.tensor_copy(slot_s[:, :, :], slot[:, :, :]))
            step(v.tensor_scalar(slot_g[:, :, :], slot[:, :, :], float(SLOTS - 1), None, ALU.min))
            v.tensor_tensor(wt[:, :, :], wt[:, :, :], valid[:, :, :], ALU.mult).then_inc(q.slots_ready, 1)

        def router_scatter(g):
            g.wait_ge(q.slots_ready, 1)
            for k in range(TOPK):
                for j in range(NT):
                    g.indirect_dma_start(out=dr["slots_in"], out_offset=bass.IndirectOffsetOnAxis(ap=slot_s[:, k, j:j + 1], axis=0),
                                         in_=norm2.h[:, j, :], in_offset=None,
                                         bounds_check=SLOTS - 1, oob_is_err=False).then_inc(scattered, 16)

        def router_store(s, i):
            s.wait_ge(q.slots_ready, 1)
            s.dma_start(dr["slot_g"][i], slot_g[:, :, :].rearrange("p k j -> p (k j)")).then_inc(q.stored, 16)
            s.dma_start(dr["wt"][i], wt[:, :, :].rearrange("p k j -> p (k j)")).then_inc(q.stored, 16)

        with nc.Block() as block:
            @block.sync
            def _(s):
                s.dma_start(xin[:, :, :], x_rows[0]).then_inc(q.x_in, 16)

            @block.vector
            def _(v):
                v.wait_ge(q.x_in, 16)
                norm0.vector(v, q, xin, 0)

            @block.gpsimd
            def _(g):
                norm0.gpsimd(g, q, 0)

            @block.tensor
            def _(p):
                norm0.tensor(p, q, 0, P[6:8], ident)

            @block.scalar
            def _(a):
                norm0.scalar(a, q, 0, P[6:8], hT0)
        clear(nc, q)

        def group(i, first):
            N1 = 0 if first else 1
            with nc.Block() as block:
                @block.sync
                def _(s):
                    for u in range(2):
                        s.dma_start(ctxT[:, u, :, :], ctx_cols[i, u]).then_inc(q.ctx_in, 16)
                    s.dma_start(amask[:, :, :], mask_rows[i]).then_inc(q.ctx_in, 16)
                    if first:
                        for a in range(SLOTS // 1024):
                            s.dma_start(slot_rows[a], zeros[:, :]).then_inc(q.zeroed, 16)
                    else:
                        router_store(s, i - 1)
                    s.wait_ge(q.x1_ready, NT)
                    s.dma_start(xin[:, :, :], x_rows[(i + 1) % NG]).then_inc(q.next_in, 16)
                    s.wait_ge(q.x2_ready, NT)
                    s.dma_start(y_rows[i], x2[:, :, :]).then_inc(q.stored, 16)
                    if first:
                        s.wait_ge(q.zeroed, 16 * (SLOTS // 1024))
                    s.wait_ge(q.stored, 16 if first else 48)

                @block.gpsimd
                def _(g):
                    if not first:
                        norm2.gpsimd(g, q, 0)
                    for j in range(NT):
                        g.tensor_tensor(xin[:, j, :], xin[:, j, :], bo[:, :], ALU.add).then_inc(q.xb_ready, 1)
                    for u in range(2):
                        g.wait_ge(q.pk_ready, u + 1)
                        g.tensor_tensor(kbd[:, 1, u, :, :], bcast(pk[:, u, S:2 * S], 1, 8), bcast(headsel[:, :], 2, S),
                                        ALU.mult).then_inc(q.kbd1_ready, 1)
                    if not first:
                        router_scatter(g)
                    norm.gpsimd(g, q, N1)
                    for j in range(NT):
                        g.wait_ge(q.Lm_ready, j + 1)
                        if j >= 3:
                            g.wait_ge(q.pt_psum, 4 * (j - 2))
                        g.tensor_tensor(L2[:, j % 3, :, :], L[:, j % 3, :, :],
                                        bcast(Lm[:, j, :], 2, S2), ALU.subtract).then_inc(q.L2_ready, 1)
                    norm0.gpsimd(g, q, N1 + 1)
                    if not first:
                        g.wait_ge(scattered, 16 * TOPK * NT * i)
                        g.tensor_tensor(left[:, :], norm.power[:, 0:1], norm.power[:, 0:1], ALU.add)

                @block.tensor
                def _(p):
                    def attend_back(n):
                        tb = (6, 7) if n == 0 else (4, 5)
                        for j in range(NT):
                            if j % 2 == 0:
                                p.wait_ge(q.oT_ready, 8 * n + 4 * (j // 2) + 4)
                            if j >= 2:
                                p.wait_ge(q.at_ready, NT * n + j - 1)
                            for u in range(4):
                                t = p.transpose(P[tb[j % 2]][:, 128 * u:128 * u + 128], oT[:, u, 128 * j:128 * j + 128], ident)
                            t.then_inc(q.tok_psum, 1)
                        if n == 1:
                            norm0.tensor(p, q, N1 + 1, P[6:8], ident)
                        for j in range(NT):
                            p.wait_ge(q.at_ready, NT * n + j + 1)
                            for u in range(2):
                                t = p.transpose(P[u][:, 128 * j:128 * j + 128], at[:, j, 128 * u:128 * u + 128], ident)
                        t.then_inc(q.aT_psum, 1)
                        p.wait_ge(q.aT_ready, 2 * n + 2)
                        w = wo if n == 0 else xwo
                        for j in range(NT):
                            for u in range(2):
                                t = p.matmul(P[2 + j // 2][:, D * (j % 2):D * (j % 2) + D], aT[:, u, 128 * j:128 * j + 128],
                                             w[:, u, :], start=(u == 0), stop=(u == 1))
                            t.then_inc(q.proj_psum, 1)

                    for w, b0, done in ((wk, 4, q.k_psum), (wq, 2, q.q_psum)):
                        for m in range(2):
                            for u in range(2):
                                t = p.matmul(P[b0 + m][:, :], w[:, u, 128 * m:128 * m + 128], hT0[:, u, :], start=(u == 0), stop=(u == 1))
                            t.then_inc(done, 1)
                    for j in range(NT):
                        for u in range(2):
                            t = p.matmul(P[6 + j // 2][:, D * (j % 2):D * (j % 2) + D], hT0[:, u, 128 * j:128 * j + 128], wv[:, u, :],
                                         start=(u == 0), stop=(u == 1))
                        t.then_inc(q.v_psum, 1)
                    if not first:
                        norm2.tensor(p, q, 0, P[0:2], ident)
                        p.wait_ge(q.hT_ready, 2)
                    p.wait_ge(q.pk_ready, 2)
                    p.wait_ge(q.pq_ready, 2)

                    def lin_values(m):
                        b, u = m // 4, m % 4
                        if m >= 2:
                            p.wait_ge(q.oT_ready, m - 1)
                        for s in range(2):
                            for hh in range(4):
                                n = 4 * m + hh
                                p.wait_ge(q.A_ready, n + 1)
                                cols = slice(0, 256) if s == 0 else slice(256, 384)
                                t = p.matmul(P[4 + m % 2][32 * hh:32 * hh + 32, 128 * s:256], vpad[:, 2 * b + s, 4 * u + hh, :],
                                             A[:, n % 8, cols], start=(s == 0), stop=(s == 1), tile_position=(0, 32 * hh),
                                             skip_group_check=True)
                        t.then_inc(q.o_psum, 1)

                    for n in range(NB * H + 2):
                        if n < NB * H:
                            b, h = n // H, n % H
                            u = h // 8
                            if h % 8 == 0:
                                p.wait_ge(q.kbd1_ready if b else q.kbd_ready, u + 1)
                            if n >= 4:
                                p.wait_ge(q.A_ready, n - 3)
                            p.matmul(P[n % 4][:, 0:256], kbd[:, b, u, h % 8, 0:128], pq[:, u, S * b:S * b + S], start=True, stop=True)
                            p.matmul(P[n % 4][:, 256:384], kbd[:, b, u, h % 8, 128:256], pq[:, u, S * b + 128:S * b + 256],
                                     start=True, stop=True).then_inc(q.s_psum, 1)
                        if n == 3:
                            p.wait_ge(q.v_ready, NT)
                        if n == 4 and not first:
                            router_logits(p)
                        if n == 14 and not first:
                            router_rank(p)
                        if n >= 5 and n % 4 == 1:
                            lin_values((n - 5) // 4)
                    p.wait_ge(q.ctx_in, 48)
                    p.wait_ge(q.A_ready, NB * H)
                    for m in range(2):
                        for u in range(2):
                            t = p.matmul(P[2][:, 154 * m:154 * m + 154], xwk[:, u, 128 * m:128 * m + 128],
                                         ctxT[:, u, :, :].rearrange("p b k -> p (b k)"), start=(u == 0), stop=(u == 1))
                    t.then_inc(q.xk_psum, 1)
                    for b in range(NB):
                        for u in range(2):
                            t = p.matmul(P[3][0:S2, D * b:D * b + D], ctxT[:, u, b, :], xwv[:, u, :], start=(u == 0), stop=(u == 1))
                    t.then_inc(q.xv_psum, 1)
                    if not first:
                        p.wait_ge(q.slots_ready, 1)
                    p.wait_ge(q.xkbd_ready, 4)
                    p.wait_ge(q.xv_ready, NB)
                    attend_back(0)
                    norm.tensor(p, q, N1, P[0:2], ident)
                    p.wait_ge(q.hT_ready, 2 * N1 + 2)
                    p.wait_ge(q.at_ready, NT)
                    for m in range(2):
                        for u in range(2):
                            t = p.matmul(P[6 + m][:, :], xwq[:, u, 128 * m:128 * m + 128], hT[:, u, :], start=(u == 0), stop=(u == 1))
                        t.then_inc(q.xq_psum, 1)
                    p.wait_ge(q.xq_ready, 2)
                    p.wait_ge(q.x1_ready, NT)

                    def x_scores(j):
                        for u in range(4):
                            n = 4 * j + u
                            if n >= 4:
                                p.wait_ge(q.L_ready, n - 3)
                            p.matmul(P[n % 4][:, 0:308], xqT[:, u // 2, 128 * j:128 * j + 128],
                                     xkbd[:, j // 2, u // 2, 4 * (u % 2):4 * (u % 2) + 4, :].rearrange("p h k -> p (h k)"),
                                     start=True, stop=True).then_inc(q.l_psum, 1)

                    def x_turn(j):
                        p.wait_ge(q.exp_ready, j + 1)
                        for u in range(4):
                            n = 4 * j + u
                            if n >= 2:
                                p.wait_ge(q.PT_ready, n - 1)
                            for hh in range(4):
                                t = p.transpose(P[4 + n % 2][0:S2, 128 * hh:128 * hh + 128], L2[:, j % 3, 4 * u + hh, :], ident)
                            t.then_inc(q.pt_psum, 1)

                    def x_values(b):
                        p.wait_ge(q.PT_ready, 8 * b + 8)
                        for u in range(4):
                            m = 4 * b + u
                            if m >= 2:
                                p.wait_ge(q.oT_ready, 8 + m - 1)
                            for hh in range(4):
                                t = p.matmul(P[6 + m % 2][32 * hh:32 * hh + 32, 0:256], xvpad[:, b, 4 * u + hh, :],
                                             PT[:, b, 4 * u + hh, :], start=True, stop=True, tile_position=(0, 32 * hh))
                            t.then_inc(q.o_psum, 1)

                    x_scores(0)
                    x_scores(1)
                    for j in range(NT):
                        if j + 2 < NT:
                            x_scores(j + 2)
                        x_turn(j)
                        if j == 2:
                            x_values(0)
                    x_values(1)
                    p.wait_ge(q.L_ready, 16)
                    p.wait_ge(q.PT_ready, 16)
                    attend_back(1)

                @block.scalar
                def _(a):
                    for m in range(2):
                        a.wait_ge(q.k_psum, m + 1)
                        a.activation(ek[:, m, :], P[4 + m][:, :], ACT.Exp).then_inc(q.ek_ready, 1)
                    for m in range(2):
                        a.wait_ge(q.q_psum, m + 1)
                        a.activation(eq[:, m, :], P[2 + m][:, :], ACT.Exp).then_inc(q.eq_ready, 1)
                    for j in range(NT):
                        a.wait_ge(q.v_psum, 2 * (j // 2) + 2)
                        a.activation(vpad[:, j, :, 0:HD], P[6 + j // 2][:, D * (j % 2):D * (j % 2) + D].rearrange("p (h d) -> p h d", d=HD),
                                     ACT.Copy).then_inc(q.v_ready, 1)
                    if not first:
                        norm2.scalar(a, q, 0, P[0:2], hT)
                    for m in range(8):
                        if m == 1 and not first:
                            router_scalar(a)
                        a.wait_ge(q.o_psum, m + 1)
                        a.activation(oT[:, m % 4, S * (m // 4):S * (m // 4) + S], P[4 + m % 2][:, 0:256], ACT.Copy).then_inc(q.oT_ready, 1)
                    a.wait_ge(q.xv_psum, 1)
                    for b in range(NB):
                        a.activation(xvpad[:, b, :, 0:HD], P[3][0:S2, D * b:D * b + D].rearrange("p (h d) -> p h d", d=HD),
                                     ACT.Copy).then_inc(q.xv_ready, 1)
                    a.wait_ge(q.aT_psum, 1)
                    for u in range(2):
                        a.activation(aT[:, u, :], P[u][:, :], ACT.Copy).then_inc(q.aT_ready, 1)
                    norm.scalar(a, q, N1, P[0:2], hT)
                    for m in range(2):
                        a.wait_ge(q.xq_psum, m + 1)
                        a.activation(xqT[:, m, :], P[6 + m][:, :], ACT.Copy, scale=HD ** -0.5).then_inc(q.xq_ready, 1)

                    def outputs(b):
                        for u in range(4):
                            m = 4 * b + u
                            a.wait_ge(q.o_psum, 8 + m + 1)
                            a.activation(oT[:, u, S * b:S * b + S], P[6 + m % 2][:, 0:256], ACT.Copy).then_inc(q.oT_ready, 1)

                    def exponents(j):
                        a.wait_ge(q.L2_ready, j + 1)
                        a.activation(L2[:, j % 3, :, :], L2[:, j % 3, :, :], ACT.Exp).then_inc(q.exp_ready, 1)

                    exponents(0)
                    for j in range(NT):
                        if j + 1 < NT:
                            exponents(j + 1)
                        for u in range(4):
                            n = 4 * j + u
                            a.wait_ge(q.pt_psum, n + 1)
                            a.activation(PT[:, j // 2, 4 * u:4 * u + 4, 128 * (j % 2):128 * (j % 2) + 128],
                                         P[4 + n % 2][0:S2, :].rearrange("p (h t) -> p h t", h=4), ACT.Copy).then_inc(q.PT_ready, 1)
                        if j == 2:
                            outputs(0)
                    outputs(1)
                    norm0.scalar(a, q, N1 + 1, P[6:8], hT0)
                    a.wait_ge(q.aT_psum, 2)
                    for u in range(2):
                        a.activation(aT[:, u, :], P[u][:, :], ACT.Copy).then_inc(q.aT_ready, 1)

                @block.vector
                def _(v):
                    def divide(n, eps):
                        tb = (6, 7) if n == 0 else (4, 5)
                        for j in range(NT):
                            v.wait_ge(q.tok_psum, NT * n + j + 1)
                            o = P[tb[j % 2]][:, :].rearrange("p (h d) -> p h d", d=32)
                            v.tensor_scalar(den[:, j, :], o[:, :, HD], eps, None, ALU.add).then_inc(q.den_ready, 1)
                            v.wait_ge(q.den_ready, NT * n + j + 1)
                            v.reciprocal(rden[:, j, :], den[:, j, :]).then_inc(q.rden_ready, 1)
                            v.wait_ge(q.rden_ready, NT * n + j + 1)
                            v.tensor_tensor(at[:, j, :].rearrange("p (h d) -> p h d", d=HD), o[:, :, 0:HD],
                                            bcast(rden[:, j, :], 2, HD), ALU.mult).then_inc(q.at_ready, 1)

                    if not first:
                        norm2.vector(v, q, x2, 0)
                    for m in range(2):
                        v.wait_ge(q.ek_ready, m + 1)
                        v.tensor_scalar(ek[:, m, :], ek[:, m, :], 1.0, None, ALU.min).then_inc(q.ek_min, 1)
                        v.wait_ge(q.ek_min, m + 1)
                        v.scalar_tensor_tensor(pk[:, m, :], P[4 + m][:, :], 0.0, ek[:, m, :], ALU.max, ALU.add).then_inc(q.pk_ready, 1)
                    for m in range(2):
                        v.wait_ge(q.eq_ready, m + 1)
                        v.tensor_scalar(eq[:, m, :], eq[:, m, :], 1.0, None, ALU.min).then_inc(q.eq_min, 1)
                        v.wait_ge(q.eq_min, m + 1)
                        v.scalar_tensor_tensor(pq[:, m, :], P[2 + m][:, :], 0.0, eq[:, m, :], ALU.max, ALU.add).then_inc(q.pq_ready, 1)
                        v.wait_ge(q.pk_ready, m + 1)
                        v.tensor_tensor(kbd[:, 0, m, :, :], bcast(pk[:, m, 0:S], 1, 8), bcast(headsel[:, :], 2, S),
                                        ALU.mult).then_inc(q.kbd_ready, 1)
                    for n in range(NB * H):
                        v.wait_ge(q.s_psum, n + 1)
                        if n >= 8:
                            v.wait_ge(q.o_psum, n // 4 - 1)
                        v.tensor_tensor(A[:, n % 8, :], P[n % 4][:, 0:384], causal[:, :], ALU.mult).then_inc(q.A_ready, 1)
                        if n == 5 and not first:
                            router_choose(v)
                        if n == 18 and not first:
                            router_place(v)
                    v.wait_ge(q.xk_psum, 1)
                    for b in range(NB):
                        for u in range(2):
                            v.tensor_tensor(xkbd[:, b, u, :, :], bcast(P[2][:, 154 * u + 77 * b:154 * u + 77 * b + 77], 1, 8),
                                            bcast(headsel[:, :], 2, S2), ALU.mult).then_inc(q.xkbd_ready, 1)
                    divide(0, DEN_EPS)
                    v.wait_ge(q.xb_ready, NT)
                    for j in range(NT):
                        v.wait_ge(q.proj_psum, 2 * (j // 2) + 2)
                        v.tensor_tensor(x1[:, j, :], P[2 + j // 2][:, D * (j % 2):D * (j % 2) + D], xin[:, j, :], ALU.add).then_inc(q.x1_ready, 1)
                    v.wait_ge(q.x1_ready, NT)
                    norm.vector(v, q, x1, N1)
                    for j in range(NT):
                        for u in range(4):
                            n = 4 * j + u
                            v.wait_ge(q.l_psum, n + 1)
                            if u == 0 and j >= 3:
                                v.wait_ge(q.L2_ready, j - 2)
                            v.tensor_tensor(L[:, j % 3, 4 * u:4 * u + 4, :], P[n % 4][:, 0:308].rearrange("p (h k) -> p h k", h=4),
                                            bcast(amask[:, j, :], 1, 4), ALU.add).then_inc(q.L_ready, 1)
                        v.wait_ge(q.L_ready, 4 * j + 4)
                        v.tensor_reduce(Lm[:, j, :], L[:, j % 3, :, :], AX.X, ALU.max).then_inc(q.Lm_ready, 1)
                    v.wait_ge(q.next_in, 16)
                    norm0.vector(v, q, xin, N1 + 1)
                    divide(1, 0.0)
                    for j in range(NT):
                        v.wait_ge(q.proj_psum, NT + 2 * (j // 2) + 2)
                        v.tensor_tensor(x2[:, j, :], P[2 + j // 2][:, D * (j % 2):D * (j % 2) + D], x1[:, j, :], ALU.add).then_inc(q.x2_ready, 1)
            clear(nc, q)

        group(0, True)
        with nc.Fori(1, NG) as i:
            group(i, False)

        with nc.Block() as block:
            @block.vector
            def _(v):
                norm2.vector(v, q, x2, 0)
                router_choose(v)
                router_place(v)

            @block.tensor
            def _(p):
                norm2.tensor(p, q, 0, P[0:2], ident)
                p.wait_ge(q.hT_ready, 2)
                router_logits(p)
                router_rank(p)

            @block.scalar
            def _(a):
                norm2.scalar(a, q, 0, P[0:2], hT)
                router_scalar(a)

            @block.gpsimd
            def _(g):
                norm2.gpsimd(g, q, 0)
                router_scatter(g)
                g.wait_ge(scattered, 16 * TOPK * NT * NG)

            @block.sync
            def _(s):
                router_store(s, NG - 1)
                s.wait_ge(q.stored, 32)
        clear(nc, q)


def experts(nc, ctx, c, io, dr):
    st = ExitStack()
    with st:
        def sb(name, shape, dt=F32):
            return st.enter_context(nc.sbuf_tensor("b_" + name, shape, dt))
        P = c.banks
        ident = c.ident[:, :]
        RT = CAP // 128
        HC = CAP // 2
        w1 = [sb(f"w1_{k}", [128, 2, FF0]) for k in range(2)]
        w2 = [sb(f"w2_{k}", [128, 4, D]) for k in range(2)]
        X = [sb(f"X_{k}", [128, RT, D]) for k in range(2)]
        XT = sb("XT", [128, 2, CAP])
        G = sb("G", [128, 4, CAP])
        Y = sb("Y", [128, RT, D])
        w1_d = io["L0_ffn_w1"].rearrange("e (c p) f -> e p c f", p=128)
        w2_d = io["L0_ffn_w2"].rearrange("e (c p) d -> e p c d", p=128)
        in_d = dr["slots_in"].rearrange("(e j p) d -> e p j d", p=128, j=RT)
        out_d = dr["slots_out"].rearrange("(e j p) d -> e p j d", p=128, j=RT)

        def load(s, e, k, done):
            s.dma_start(w1[k][:, :, :], w1_d[e]).then_inc(done, 16)
            s.dma_start(w2[k][:, :, :], w2_d[e]).then_inc(done, 16)
            s.dma_start(X[k][:, :, :], in_d[e]).then_inc(done, 16)

        with ExitStack() as once:
            q = signals(nc, once, "b_first")
            with nc.Block() as block:
                @block.sync
                def _(s):
                    load(s, 0, 0, q.b_first)
                    s.wait_ge(q.b_first, 48)
            clear(nc, q)

        q = signals(nc, st, "b_in b_next xT_psum xT_ready g_psum g_ready y_psum y_ready b_out b_stored")

        def pair(e0, more):
            with nc.Block() as block:
                @block.sync
                def _(s):
                    load(s, e0 + 1, 1, q.b_in)
                    s.wait_ge(q.y_ready, RT)
                    s.dma_start(out_d[e0], Y[:, :, :]).then_inc(q.b_stored, 16)
                    if more:
                        load(s, e0 + 2, 0, q.b_next)
                    s.wait_ge(q.y_ready, 2 * RT)
                    s.dma_start(out_d[e0 + 1], Y[:, :, :]).then_inc(q.b_stored, 16)
                    s.wait_ge(q.b_stored, 32)
                    if more:
                        s.wait_ge(q.b_next, 48)

                @block.tensor
                def _(p):
                    for k in range(2):
                        if k:
                            p.wait_ge(q.b_in, 48)
                        for j in range(RT):
                            if j >= 2 or k:
                                p.wait_ge(q.xT_ready, RT * k + j - 1)
                            for u in range(2):
                                t = p.transpose(P[j % 2][:, 128 * u:128 * u + 128], X[k][:, j, 128 * u:128 * u + 128], ident)
                            t.then_inc(q.xT_psum, 1)
                        p.wait_ge(q.xT_ready, RT * (k + 1))
                        for n in range(8):
                            f, m = n // 2, n % 2
                            if n >= 2 or k:
                                p.wait_ge(q.g_ready, 8 * k + n - 1)
                            for u in range(2):
                                t = p.matmul(P[2 + n % 2][:, 0:HC], w1[k][:, u, 128 * f:128 * f + 128], XT[:, u, HC * m:HC * m + HC],
                                             start=(u == 0), stop=(u == 1))
                            t.then_inc(q.g_psum, 1)
                        p.wait_ge(q.g_ready, 8 * (k + 1))
                        for j in range(RT):
                            n = RT * k + j
                            if n >= 4:
                                p.wait_ge(q.y_ready, n - 3)
                            for f in range(4):
                                t = p.matmul(P[4 + n % 4][:, 0:D], G[:, f, 128 * j:128 * j + 128], w2[k][:, f, :], start=(f == 0), stop=(f == 3))
                            t.then_inc(q.y_psum, 1)

                @block.scalar
                def _(a):
                    for k in range(2):
                        for n in range(8):
                            f, m = n // 2, n % 2
                            a.wait_ge(q.g_psum, 8 * k + n + 1)
                            if k and n == 0:
                                a.wait_ge(q.y_psum, RT)
                            a.activation(G[:, f, HC * m:HC * m + HC], P[2 + n % 2][:, 0:HC], ACT.Gelu).then_inc(q.g_ready, 1)

                @block.vector
                def _(v):
                    for k in range(2):
                        for j in range(RT):
                            n = RT * k + j
                            v.wait_ge(q.xT_psum, n + 1)
                            if k and j == 0:
                                v.wait_ge(q.g_psum, 8)
                            v.tensor_copy(XT[:, :, 128 * j:128 * j + 128], P[j % 2][:, 0:256].rearrange("p (c t) -> p c t", c=2)).then_inc(q.xT_ready, 1)
                        for j in range(RT):
                            n = RT * k + j
                            v.wait_ge(q.y_psum, n + 1)
                            if k and j == 0:
                                v.wait_ge(q.b_stored, 16)
                            v.tensor_copy(Y[:, j, :], P[4 + n % 4][:, 0:D]).then_inc(q.y_ready, 1)
            clear(nc, q)

        with nc.Fori(0, E // 2 - 1) as i:
            pair(2 * i, True)
        pair(E - 2, False)


def layer1(nc, ctx, c, io, dr):
    st = ExitStack()
    with st:
        def sb(name, shape, dt=F32):
            return st.enter_context(nc.sbuf_tensor("c_" + name, shape, dt))
        P = c.banks
        ident = c.ident[:, :]
        HW = H1 * HD1
        NP = H1 // 2
        wq = sb("wq", [128, 2, HW])
        wdn = sb("wdn", [128, 2, LR])
        wku = sb("wku", [128, HW])
        wvu = sb("wvu", [128, HW])
        wo = sb("wo", [128, NP, D])
        xwq, xwk, xwv, xwo = (sb(n, [128, 2, D]) for n in ("xwq", "xwk", "xwv", "xwo"))
        bq, bqs, bk = (sb(n, [128, 2]) for n in ("bq", "bqs", "bk"))
        bv = sb("bv", [128, D])
        bo = sb("bo", [128, D])
        imask = sb("imask", [128, NB, S2], I32)
        keep = sb("keep", [128, NB, S2])
        pen = sb("pen", [128, NB, S2])

        norm0, norm, norm2 = Norm(nc, st, "c0"), Norm(nc, st, "c1"), Norm(nc, st, "c2")
        slot = sb("slot", [128, TOPK * NT], I32)
        wt = sb("wt", [128, TOPK * NT])
        rows = sb("rows", [128, TOPK, NT, D])
        arrived = sb("arrived", [128, 1])
        xin = sb("xin", [128, NT, D])
        x3 = sb("x3", [128, NT, D])
        x4 = sb("x4", [128, NT, D])
        x5 = sb("x5", [128, NT, D])
        hT0 = sb("hT0", [128, 2, T])
        hT = sb("hT", [128, 2, T])
        qT = sb("qT", [128, NP, T])
        latT = sb("latT", [128, T])
        kz = sb("kz", [128, H1, T])
        vs = sb("vs", [128, NT, HW])
        nmax = sb("nmax", [128, NB * H1, 2])
        sums = sb("sums", [128, NB * H1, 2])
        rsum = sb("rsum", [128, NB * H1, 2])
        pr = sb("pr", [128, 4, 2, S])
        PT = sb("PT", [128, 4, 2, S])
        aT = sb("aT", [128, NP, T])
        ctxT = sb("ctxT", [128, 2, NB, S2])
        xqT = sb("xqT", [128, 2, T])
        xkT = sb("xkT", [128, 2, NB, S2])
        xv = sb("xv", [S2, NB, D])
        L = sb("L", [128, NT, S2])
        xm = sb("xm", [128, NT])
        xs = sb("xs", [128, NT])
        xr = sb("xr", [128, NT])
        xPT = sb("xPT", [S2, T])
        xaT = sb("xaT", [128, 2, T])
        amax = sb("amax", [128, 1])

        with ExitStack() as once:
            q = signals(nc, once, "c_w c_dve")
            with nc.Block() as block:
                @block.sync
                def _(s):
                    n = 0
                    for dst, src in ((wq[:, :, :], io["L1_attn_Wq"].rearrange("(c p) n -> p c n", p=128)),
                                     (wdn[:, :, :], io["L1_attn_Wkv_down"].rearrange("(c p) n -> p c n", p=128)),
                                     (wo[:, :, :], io["L1_attn_Wo"].rearrange("(c p) n -> p c n", p=128)),
                                     (xwq[:, :, :], io["L1_xattn_Wq"].rearrange("(c p) n -> p c n", p=128)),
                                     (xwk[:, :, :], io["L1_xattn_Wk"].rearrange("(c p) n -> p c n", p=128)),
                                     (xwv[:, :, :], io["L1_xattn_Wv"].rearrange("(c p) n -> p c n", p=128)),
                                     (xwo[:, :, :], io["L1_xattn_Wo"].rearrange("(c p) n -> p c n", p=128)),
                                     (wku[0:LR, :], io["L1_attn_Wk_up"]),
                                     (wvu[0:LR, :], io["L1_attn_Wv_up"]),
                                     (bv[:, :], io["L1_xattn_bv"].unsqueeze(0).broadcast_to([128, D])),
                                     (bo[:, :], io["L1_xattn_bo"].unsqueeze(0).broadcast_to([128, D])),
                                     (imask[:, :, :], io["mask_SxS2_ik0"].rearrange("(j p) k -> p j k", p=128))):
                        s.dma_start(dst, src).then_inc(q.c_w, 16)
                        n += 16
                    for dst, src in ((bq, io["L1_xattn_bq"]), (bk, io["L1_xattn_bk"])):
                        for u in range(2):
                            s.dma_start(dst[:, u:u + 1], src[128 * u:128 * u + 128].unsqueeze(1)).then_inc(q.c_w, 16)
                            n += 16
                    s.wait_ge(q.c_w, n)

                @block.gpsimd
                def _(g):
                    for m in (norm0, norm, norm2):
                        g.memset(m.power[:, :], -0.5)

                @block.vector
                def _(v):
                    v.memset(wku[LR:128, :], 0.0)
                    v.memset(wvu[LR:128, :], 0.0)
                    v.memset(latT[LR:128, :], 0.0)
                    v.memset(kz[:, :, :], 0.0)
                    v.memset(c.amax[:, :], 0.0)
                    v.wait_ge(q.c_w, 16 * 16)
                    v.tensor_scalar(bqs[:, :], bq[:, :], HD ** -0.5, None, ALU.mult)
                    v.tensor_scalar(keep[:, :, :], imask[:, :, :], 0.0, None, ALU.not_equal).then_inc(q.c_dve, 1)
                    v.wait_ge(q.c_dve, 1)
                    v.tensor_scalar(pen[:, :, :], keep[:, :, :], 1.0, 1e9, ALU.subtract, ALU.mult).then_inc(q.c_dve, 1)
            clear(nc, q)

        q = signals(nc, st, "r_in x_in ctx_in rows_in mixed ln_stats ln_moments ln_var ln_rstd ln_h hT_psum hT_ready q_psum qT_ready lat_psum "
                         "lat_ready k_psum kz_ready v_psum v_ready s_psum nmax_ready exp_ready rsum_ready pr_ready pt_psum PT_ready "
                         "a_psum aT_ready proj_psum x4_ready xb_ready xk_psum xv_psum xk_ready xv_ready xq_psum xq_ready l_psum "
                         "L_kept L_ready xm_ready xe_ready xr_ready xp_ready xpt_psum xPT_ready xa_psum xaT_ready xproj_psum "
                         "x5_ready amax_part amax_ready stored")
        gathered = c.gathered
        NH = NB * H1
        SB = (0, 1, 6, 7)

        def fetch(s, i):
            s.dma_start(slot[:, :], dr["slot_g"][i]).then_inc(q.r_in, 16)
            s.dma_start(wt[:, :], dr["wt"][i]).then_inc(q.x_in, 16)
            s.dma_start(xin[:, :, :], dr["x_a"].rearrange("(i j p) n -> i p j n", p=128, j=NT)[i]).then_inc(q.x_in, 16)

        def gather(g):
            g.wait_ge(q.r_in, 16)
            for k in range(TOPK):
                for j in range(NT):
                    g.indirect_dma_start(out=rows[:, k, j, :], out_offset=None, in_=dr["slots_out"],
                                         in_offset=bass.IndirectOffsetOnAxis(ap=slot[:, NT * k + j:NT * k + j + 1], axis=0),
                                         bounds_check=SLOTS - 1, oob_is_err=False).then_inc(gathered, 16)

        def gathers_done(g, n):
            g.wait_ge(gathered, 16 * TOPK * NT * n)
            g.tensor_tensor(arrived[:, :], norm.power[:, 0:1], norm.power[:, 0:1], ALU.add).then_inc(q.rows_in, 1)

        def mix(v):
            v.wait_ge(q.x_in, 32)
            v.wait_ge(q.rows_in, 1)
            for j in range(NT):
                v.scalar_tensor_tensor(x3[:, j, :], rows[:, 0, j, :], wt[:, j:j + 1], xin[:, j, :], ALU.mult, ALU.add).then_inc(q.mixed, 1)
            v.wait_ge(q.mixed, NT)
            for j in range(NT):
                v.scalar_tensor_tensor(x3[:, j, :], rows[:, 1, j, :], wt[:, NT + j:NT + j + 1], x3[:, j, :], ALU.mult, ALU.add).then_inc(q.mixed, 1)
            v.wait_ge(q.mixed, 2 * NT)

        def last_norm(v):
            norm2.vector(v, q, x5, 0)
            v.wait_ge(q.ln_h, NT)
            v.tensor_reduce(amax[:, :], norm2.h[:, :, :].rearrange("p j n -> p (j n)"), AX.X, ALU.max, apply_absolute_value=True).then_inc(q.amax_part, 1)
            v.wait_ge(q.amax_part, 1)
            v.tensor_tensor(c.amax[:, :], c.amax[:, :], amax[:, :], ALU.max).then_inc(q.amax_ready, 1)

        def keep_input(a, i):
            a.wait_ge(q.hT_psum, 1)
            for u in range(2):
                a.activation(c.hT_all[:, u, bass.ts(i, T)], P[u][:, :], ACT.Copy).then_inc(q.hT_ready, 1)

        with nc.Block() as block:
            @block.sync
            def _(s):
                fetch(s, 0)

            @block.gpsimd
            def _(g):
                gather(g)
                gathers_done(g, 1)
                norm0.gpsimd(g, q, 0)

            @block.vector
            def _(v):
                mix(v)
                norm0.vector(v, q, x3, 0)

            @block.tensor
            def _(p):
                norm0.tensor(p, q, 0, P[4:6], ident)

            @block.scalar
            def _(a):
                norm0.scalar(a, q, 0, P[4:6], hT0)
        clear(nc, q)

        def group(i, first):
            N1 = 0 if first else 1
            with nc.Block() as block:
                @block.sync
                def _(s):
                    fetch(s, (i + 1) % NG)
                    for u in range(2):
                        s.dma_start(ctxT[:, u, :, :], io["ctxT"].rearrange("(i b) (c p) k -> i c p b k", b=NB, p=128)[i, u]).then_inc(q.ctx_in, 16)
                    s.wait_ge(q.x5_ready, NT)
                    s.dma_start(dr["x_c"].rearrange("(i j p) n -> i p j n", p=128, j=NT)[i], x5[:, :, :]).then_inc(q.stored, 16)
                    s.wait_ge(q.stored, 16)

                @block.gpsimd
                def _(g):
                    gather(g)
                    if not first:
                        norm2.gpsimd(g, q, 0)
                    for n in range(NH):
                        g.wait_ge(q.rsum_ready, n + 1)
                        for u in range(2):
                            g.tensor_scalar(pr[:, n % 4, u, :], pr[:, n % 4, u, :], rsum[:, n, u:u + 1], 1.0,
                                            ALU.mult, ALU.mult).then_inc(q.pr_ready, 1)
                    norm.gpsimd(g, q, N1)
                    gathers_done(g, i + 2)
                    norm0.gpsimd(g, q, N1 + 1)
                    g.wait_ge(q.ln_h, NT * (N1 + 1))
                    for j in range(NT):
                        g.tensor_tensor(x4[:, j, :], x4[:, j, :], bo[:, :], ALU.add).then_inc(q.xb_ready, 1)

                @block.tensor
                def _(p):
                    for u in range(2):
                        t = p.matmul(P[6][0:LR, :], wdn[:, u, :], hT0[:, u, :], start=(u == 0), stop=(u == 1))
                    t.then_inc(q.lat_psum, 1)
                    for m in range(NP):
                        for u in range(2):
                            t = p.matmul(P[2 + m][:, :], wq[:, u, 128 * m:128 * m + 128], hT0[:, u, :], start=(u == 0), stop=(u == 1))
                        t.then_inc(q.q_psum, 1)
                    if not first:
                        norm2.tensor(p, q, 0, P[0:2], ident)
                        p.wait_ge(q.hT_ready, 2)
                    p.wait_ge(q.lat_ready, 1)
                    for m in range(NP):
                        p.matmul(P[(7, 0, 1, 6)[m]][:, :], wku[:, 128 * m:128 * m + 128], latT[:, :], start=True, stop=True).then_inc(q.k_psum, 1)
                    for j in range(NT):
                        p.wait_ge(q.qT_ready, j + 1)
                        p.matmul(P[2 + j][:, :], latT[:, 128 * j:128 * j + 128], wvu[:, :], start=True, stop=True).then_inc(q.v_psum, 1)
                    p.wait_ge(q.kz_ready, H1)

                    def scores(n):
                        b, h = n // H1, n % H1
                        if n >= 4:
                            p.wait_ge(q.exp_ready, 2 * (n - 3))
                        for u in range(2):
                            t = p.matmul(P[SB[n % 4]][:, S * u:S * u + S], qT[:, h // 2, S * b + 128 * u:S * b + 128 * u + 128],
                                         kz[:, h, S * b:S * b + S], start=True, stop=True)
                        t.then_inc(q.s_psum, 1)

                    def turn(n):
                        p.wait_ge(q.pr_ready, 2 * n + 2)
                        if n == 0:
                            p.wait_ge(q.v_ready, 2)
                        if n >= 2:
                            p.wait_ge(q.PT_ready, n - 1)
                        for k in range(2):
                            for u in range(2):
                                t = p.transpose(P[2 + n % 2][:, S * k + 128 * u:S * k + 128 * u + 128],
                                                pr[:, n % 4, u, 128 * k:128 * k + 128], ident)
                        t.then_inc(q.pt_psum, 1)

                    def values(m):
                        b, g = m // NP, m % NP
                        p.wait_ge(q.PT_ready, 2 * m + 2)
                        if m == 0:
                            p.wait_ge(q.v_ready, NT)
                        if m >= 2:
                            p.wait_ge(q.aT_ready, m - 1)
                        for k in range(2):
                            for e in range(2):
                                h = 2 * g + e
                                t = p.matmul(P[4 + m % 2][HD1 * e:HD1 * e + HD1, 0:S], vs[:, 2 * b + k, HD1 * h:HD1 * h + HD1],
                                             PT[:, (2 * m + e) % 4, k, :], start=(k == 0), stop=(k == 1),
                                             tile_position=(0, HD1 * e), skip_group_check=True)
                        t.then_inc(q.a_psum, 1)

                    for n in range(NH + 4):
                        if n < NH:
                            scores(n)
                        if 0 <= n - 3 < NH:
                            turn(n - 3)
                        if n >= 5 and n % 2:
                            values((n - 5) // 2)
                    p.wait_ge(q.aT_ready, 2 * NP)
                    for j in range(NT):
                        for m in range(NP):
                            t = p.matmul(P[6 + j // 2][:, D * (j % 2):D * (j % 2) + D], aT[:, m, 128 * j:128 * j + 128], wo[:, m, :],
                                         start=(m == 0), stop=(m == NP - 1))
                        t.then_inc(q.proj_psum, 1)

                    p.wait_ge(q.ctx_in, 32)
                    p.wait_ge(q.PT_ready, NH)
                    for m in range(2):
                        for u in range(2):
                            t = p.matmul(P[2][:, 154 * m:154 * m + 154], xwk[:, u, 128 * m:128 * m + 128],
                                         ctxT[:, u, :, :].rearrange("p b k -> p (b k)"), start=(u == 0), stop=(u == 1))
                    t.then_inc(q.xk_psum, 1)
                    for b in range(NB):
                        for u in range(2):
                            t = p.matmul(P[3][0:S2, D * b:D * b + D], ctxT[:, u, b, :], xwv[:, u, :], start=(u == 0), stop=(u == 1))
                    t.then_inc(q.xv_psum, 1)
                    norm.tensor(p, q, N1, P[0:2], ident)
                    p.wait_ge(q.hT_ready, 2 * N1 + 2)
                    for m in range(2):
                        for u in range(2):
                            t = p.matmul(P[4 + m][:, :], xwq[:, u, 128 * m:128 * m + 128], hT[:, u, :], start=(u == 0), stop=(u == 1))
                        t.then_inc(q.xq_psum, 1)
                    p.wait_ge(q.xq_ready, 2)
                    p.wait_ge(q.xk_ready, 2)
                    for j in range(NT):
                        for u in range(2):
                            t = p.matmul(P[6][:, S2 * j:S2 * j + S2], xqT[:, u, 128 * j:128 * j + 128], xkT[:, u, j // 2, :],
                                         start=(u == 0), stop=(u == 1))
                    t.then_inc(q.l_psum, 1)
                    norm0.tensor(p, q, N1 + 1, P[4:6], ident)
                    for j in range(NT):
                        p.wait_ge(q.xp_ready, j + 1)
                        t = p.transpose(P[7][0:S2, 128 * j:128 * j + 128], L[:, j, :], ident)
                    t.then_inc(q.xpt_psum, 1)
                    p.wait_ge(q.xPT_ready, 1)
                    p.wait_ge(q.xv_ready, NB)
                    for u in range(2):
                        for b in range(NB):
                            t = p.matmul(P[u][:, S * b:S * b + S], xv[:, b, 128 * u:128 * u + 128], xPT[:, S * b:S * b + S], start=True, stop=True)
                        t.then_inc(q.xa_psum, 1)
                    p.wait_ge(q.xaT_ready, 2)
                    for j in range(NT):
                        for u in range(2):
                            t = p.matmul(P[2 + j // 2][:, D * (j % 2):D * (j % 2) + D], xaT[:, u, 128 * j:128 * j + 128], xwo[:, u, :],
                                         start=(u == 0), stop=(u == 1))
                        t.then_inc(q.xproj_psum, 1)

                @block.scalar
                def _(a):
                    a.wait_ge(q.lat_psum, 1)
                    a.activation(latT[0:LR, :], P[6][0:LR, :], ACT.Copy).then_inc(q.lat_ready, 1)
                    for m in range(NP):
                        a.wait_ge(q.q_psum, m + 1)
                        a.activation(qT[:, m, :], P[2 + m][:, :], ACT.Copy, scale=HD1 ** -0.5).then_inc(q.qT_ready, 1)
                    if not first:
                        keep_input(a, i - 1)
                    for j in range(NT):
                        a.wait_ge(q.v_psum, j + 1)
                        a.activation(vs[:, j, :], P[2 + j][:, :], ACT.Copy).then_inc(q.v_ready, 1)

                    def heads(m):
                        a.wait_ge(q.a_psum, m + 1)
                        a.activation(aT[:, m % NP, S * (m // NP):S * (m // NP) + S], P[4 + m % 2][:, 0:S], ACT.Copy).then_inc(q.aT_ready, 1)

                    for n in range(NH):
                        a.wait_ge(q.nmax_ready, n + 1)
                        if n >= 4:
                            a.wait_ge(q.pt_psum, n - 3)
                        for u in range(2):
                            a.activation(pr[:, n % 4, u, :], P[SB[n % 4]][:, S * u:S * u + S], ACT.Exp, bias=nmax[:, n, u:u + 1],
                                         accum_out=sums[:, n, u:u + 1]).then_inc(q.exp_ready, 1)
                        if n >= 7 and n % 2:
                            heads((n - 7) // 2)
                    heads(NH // 2 - 3)
                    heads(NH // 2 - 2)
                    heads(NH // 2 - 1)
                    a.wait_ge(q.xk_psum, 1)
                    for m in range(2):
                        a.activation(xkT[:, m, :, :].rearrange("p b k -> p (b k)"), P[2][:, 154 * m:154 * m + 154], ACT.Identity,
                                     bias=bk[:, m:m + 1]).then_inc(q.xk_ready, 1)
                    norm.scalar(a, q, N1, P[0:2], hT)
                    for m in range(2):
                        a.wait_ge(q.xq_psum, m + 1)
                        a.activation(xqT[:, m, :], P[4 + m][:, :], ACT.Identity, bias=bqs[:, m:m + 1], scale=HD ** -0.5).then_inc(q.xq_ready, 1)
                    norm0.scalar(a, q, N1 + 1, P[4:6], hT0)
                    a.wait_ge(q.xm_ready, 1)
                    for j in range(NT):
                        a.activation(L[:, j, :], L[:, j, :], ACT.Exp, bias=xm[:, j:j + 1], accum_out=xs[:, j:j + 1]).then_inc(q.xe_ready, 1)
                    a.wait_ge(q.xpt_psum, 1)
                    a.activation(xPT[:, :], P[7][0:S2, :], ACT.Copy).then_inc(q.xPT_ready, 1)
                    for u in range(2):
                        a.wait_ge(q.xa_psum, u + 1)
                        a.activation(xaT[:, u, :], P[u][:, :], ACT.Copy).then_inc(q.xaT_ready, 1)
                @block.vector
                def _(v):
                    if not first:
                        last_norm(v)
                    for m in range(NP):
                        v.wait_ge(q.k_psum, m + 1)
                        for e in range(2):
                            rows_ = slice(HD1 * e, HD1 * e + HD1)
                            v.tensor_copy(kz[rows_, 2 * m + e, :], P[(7, 0, 1, 6)[m]][rows_, :]).then_inc(q.kz_ready, 1)

                    def maxima(n):
                        v.wait_ge(q.s_psum, n + 1)
                        v.tensor_reduce(nmax[:, n, :], P[SB[n % 4]][:, :].rearrange("p (u k) -> p u k", u=2), AX.X, ALU.max,
                                        negate=True).then_inc(q.nmax_ready, 1)

                    def invert(n):
                        v.wait_ge(q.exp_ready, 2 * n + 2)
                        v.reciprocal(rsum[:, n, :], sums[:, n, :]).then_inc(q.rsum_ready, 1)

                    def by_key(n):
                        v.wait_ge(q.pt_psum, n + 1)
                        if n >= 4:
                            v.wait_ge(q.a_psum, n // 2 - 1)
                        v.tensor_copy(PT[:, n % 4, :, :].rearrange("p k t -> p (k t)"), P[2 + n % 2][:, :]).then_inc(q.PT_ready, 1)

                    for n in range(NH + 3):
                        if n < NH:
                            maxima(n)
                        if 0 <= n - 1 < NH:
                            invert(n - 1)
                        if n >= 3:
                            by_key(n - 3)
                    for j in range(NT):
                        v.wait_ge(q.proj_psum, 2 * (j // 2) + 2)
                        v.tensor_tensor(x4[:, j, :], P[6 + j // 2][:, D * (j % 2):D * (j % 2) + D], x3[:, j, :], ALU.add).then_inc(q.x4_ready, 1)
                    v.wait_ge(q.x4_ready, NT)
                    norm.vector(v, q, x4, N1)
                    v.wait_ge(q.xv_psum, 1)
                    for b in range(NB):
                        v.tensor_tensor(xv[:, b, :], P[3][0:S2, D * b:D * b + D], bv[0:S2, :], ALU.add).then_inc(q.xv_ready, 1)
                    mix(v)
                    norm0.vector(v, q, x3, N1 + 1)
                    v.wait_ge(q.l_psum, 1)
                    l = P[6][:, 0:NT * S2].rearrange("p (b r k) -> p b r k", b=NB, r=NB)
                    l3 = L[:, :, :].rearrange("p (b r) k -> p b r k", b=NB)
                    v.tensor_tensor(l3, l, bcast(keep[:, :, :], 1, NB), ALU.mult).then_inc(q.L_kept, 1)
                    v.wait_ge(q.L_kept, 1)
                    v.tensor_tensor(l3, l3, bcast(pen[:, :, :], 1, NB), ALU.add).then_inc(q.L_ready, 1)
                    v.wait_ge(q.L_ready, 1)
                    v.tensor_reduce(xm[:, :], L[:, :, :], AX.X, ALU.max, negate=True).then_inc(q.xm_ready, 1)
                    v.wait_ge(q.xe_ready, NT)
                    v.reciprocal(xr[:, :], xs[:, :]).then_inc(q.xr_ready, 1)
                    v.wait_ge(q.xr_ready, 1)
                    for j in range(NT):
                        v.tensor_scalar(L[:, j, :], L[:, j, :], xr[:, j:j + 1], None, ALU.mult).then_inc(q.xp_ready, 1)
                    v.wait_ge(q.xb_ready, NT)
                    for j in range(NT):
                        v.wait_ge(q.xproj_psum, 2 * (j // 2) + 2)
                        v.tensor_tensor(x5[:, j, :], P[2 + j // 2][:, D * (j % 2):D * (j % 2) + D], x4[:, j, :], ALU.add).then_inc(q.x5_ready, 1)
            clear(nc, q)

        group(0, True)
        with nc.Fori(1, NG) as i:
            group(i, False)

        with nc.Block() as block:
            @block.vector
            def _(v):
                last_norm(v)

            @block.gpsimd
            def _(g):
                norm2.gpsimd(g, q, 0)

            @block.tensor
            def _(p):
                norm2.tensor(p, q, 0, P[0:2], ident)

            @block.scalar
            def _(a):
                keep_input(a, NG - 1)
        clear(nc, q)


def feed_forward(nc, ctx, c, io, dr, out):
    st = ExitStack()
    with st:
        def sb(name, shape, dt=F32):
            return st.enter_context(nc.sbuf_tensor("d_" + name, shape, dt))
        P = c.banks
        ident = c.ident[:, :]
        NTOK = B * S
        NW = 48
        wuT = sb("wuT", [128, 2, FF1])
        wgT = sb("wgT", [128, 2, FF1])
        wdT = sb("wdT", [128, FC, D])
        raw = sb("raw", [128, FC, NTOK])
        mx = sb("mx", [128, 1])
        gmx = sb("gmx", [128, 1])
        cur = sb("cur", [128, 2 * FC])
        cur1 = sb("cur1", [128, 1])
        scale = {k: sb("scale_" + k, [128, 1]) for k in "xugao"}
        inv = {k: sb("inv_" + k, [128, 1]) for k in "xugao"}

        with ExitStack() as once:
            q = signals(nc, once, "d_w w_steps wt_psum wt_ready")
            W = once.enter_context(nc.sbuf_tensor("w_rows", [128, 3, NW, BLK], F32))
            Wi = once.enter_context(nc.sbuf_tensor("w_int", [128, 3, NW, BLK], I16))
            wa = once.enter_context(nc.sbuf_tensor("w_amax", [128, 3, NW], F32))
            wi = once.enter_context(nc.sbuf_tensor("w_inv", [128, 3, NW], F32))
            with nc.Block() as block:
                @block.sync
                def _(s):
                    for k, (name, r) in enumerate((("L1_ffn_w_up", FC), ("L1_ffn_w_gate", FC), ("L1_ffn_w_down", 2))):
                        s.dma_start(W[:, k, :, :].rearrange("p a b -> p (a b)").rearrange("p (r n) -> p r n", r=r),
                                    io[name].rearrange("(r p) n -> p r n", p=128)).then_inc(q.d_w, 16)
                    s.wait_ge(q.d_w, 48)

                @block.vector
                def _(v):
                    n = [0]

                    def step(ins):
                        ins.then_inc(q.w_steps, 1)
                        n[0] += 1
                        v.wait_ge(q.w_steps, n[0])

                    v.wait_ge(q.d_w, 48)
                    step(v.tensor_reduce(wa[:, :, :], W[:, :, :, :], AX.X, ALU.max, apply_absolute_value=True))
                    step(v.tensor_scalar(wa[:, :, :], wa[:, :, :], 1.0 / WMAX, 1e-12, ALU.mult, ALU.max))
                    step(v.reciprocal(wi[:, :, :], wa[:, :, :]))
                    for k in range(3):
                        step(v.tensor_tensor(Wi[:, k, :, :], W[:, k, :, :], bcast(wi[:, k, :], 2, BLK), ALU.mult))
                    step(v.tensor_scalar(Wi[:, :, :, :], Wi[:, :, :, :], WMAX, -WMAX - 1.0, ALU.min, ALU.max))
                    for k in range(3):
                        step(v.tensor_tensor(W[:, k, :, :], Wi[:, k, :, :], bcast(wa[:, k, :], 2, BLK), ALU.mult))

                @block.tensor
                def _(p):
                    p.wait_ge(q.w_steps, 10)
                    n = 0
                    for k in range(3):
                        w = W[:, k, :, :].rearrange("p a b -> p (a b)")
                        nr, ncol = (FC, 2) if k < 2 else (2, FC)
                        for col in range(ncol):
                            for r in range(nr):
                                if n % 2 == 0 and n >= 16:
                                    p.wait_ge(q.wt_ready, n // 2 - 7)
                                width = 128 * ncol
                                t = p.transpose(P[(n // 2) % 8][:, 128 * (n % 2):128 * (n % 2) + 128],
                                                w[:, width * r + 128 * col:width * r + 128 * col + 128], ident)
                                if n % 2:
                                    t.then_inc(q.wt_psum, 1)
                                n += 1

                @block.scalar
                def _(a):
                    n = 0
                    for k, dst in enumerate((wuT, wgT, wdT)):
                        nr, ncol = (FC, 2) if k < 2 else (2, FC)
                        for col in range(ncol):
                            for r in range(0, nr, 2):
                                a.wait_ge(q.wt_psum, n + 1)
                                a.activation(dst[:, col, 128 * r:128 * r + 256], P[n % 8][:, 0:256], ACT.Copy).then_inc(q.wt_ready, 1)
                                n += 1
            clear(nc, q)

        def make_scale(k, src):
            with ExitStack() as once:
                q = signals(nc, once, "all_max scale_steps")
                with nc.Block() as block:
                    @block.gpsimd
                    def _(g):
                        g.partition_all_reduce(gmx[:, :], src[:, :], 128, RMAX).then_inc(q.all_max, 1)

                    @block.vector
                    def _(v):
                        v.wait_ge(q.all_max, 1)
                        v.tensor_scalar(scale[k][:, :], gmx[:, :], 1.0 / QMAX, 1e-12, ALU.mult, ALU.max).then_inc(q.scale_steps, 1)
                        v.wait_ge(q.scale_steps, 1)
                        v.reciprocal(inv[k][:, :], scale[k][:, :]).then_inc(q.scale_steps, 1)
                        v.memset(mx[:, :], 0.0)
                clear(nc, q)

        def quantise_input():
            with ExitStack() as once:
                q = signals(nc, once, "xi_ready xq_ready")
                xi = raw[:, 0:1, :].bitcast(I16)
                with nc.Block() as block:
                    @block.vector
                    def _(v):
                        for u in range(2):
                            part = xi[:, 0, NTOK * u:NTOK * u + NTOK]
                            v.tensor_scalar(part, c.hT_all[:, u, :], inv["x"][:, :], None, ALU.mult).then_inc(q.xi_ready, 1)
                        for u in range(2):
                            part = xi[:, 0, NTOK * u:NTOK * u + NTOK]
                            v.wait_ge(q.xi_ready, u + 1)
                            v.tensor_scalar(c.hT_all[:, u, :], part, scale["x"][:, :], None, ALU.mult).then_inc(q.xq_ready, 1)
                clear(nc, q)

        def project(tag, wT, up):
            with ExitStack() as once:
                q = signals(nc, once, f"up_ready_{tag} r_psum_{tag} raw_ready_{tag} cur_ready_{tag} cur1_ready_{tag} mx_ready_{tag}")
                up_ready, r_psum, raw_ready, cur_ready, cur1_ready, mx_ready = q
                N = 2 * FC
                with nc.Fori(0, NG // 2) as i:
                    with nc.Block() as block:
                        @block.vector
                        def _(v):
                            if up is not None:
                                for k in range(2):
                                    at = bass.ts(2 * i + k, T)
                                    v.tensor_scalar(up[:, :, at], raw[:, :, at], inv["u"][:, :], None, ALU.mult).then_inc(up_ready, 1)
                            for n in range(N):
                                v.wait_ge(raw_ready, n + 1)
                                v.tensor_reduce(cur[:, n:n + 1], P[n % 8][:, :], AX.X, ALU.max, apply_absolute_value=True).then_inc(cur_ready, 1)
                            v.wait_ge(cur_ready, N)
                            v.tensor_reduce(cur1[:, :], cur[:, :], AX.X, ALU.max).then_inc(cur1_ready, 1)
                            v.wait_ge(cur1_ready, 1)
                            v.tensor_tensor(mx[:, :], mx[:, :], cur1[:, :], ALU.max).then_inc(mx_ready, 1)

                        @block.tensor
                        def _(p):
                            for n in range(N):
                                k, f = n // FC, n % FC
                                if n >= 8:
                                    p.wait_ge(cur_ready, n - 7)
                                for u in range(2):
                                    t = p.matmul(P[n % 8][:, :], wT[:, u, 128 * f:128 * f + 128], c.hT_all[:, u, bass.ts(2 * i + k, T)],
                                                 start=(u == 0), stop=(u == 1))
                                t.then_inc(r_psum, 1)

                        @block.scalar
                        def _(a):
                            for n in range(N):
                                k, f = n // FC, n % FC
                                if up is not None and f == 0:
                                    a.wait_ge(up_ready, k + 1)
                                a.wait_ge(r_psum, n + 1)
                                a.activation(raw[:, f, bass.ts(2 * i + k, T)], P[n % 8][:, :], ACT.Copy).then_inc(raw_ready, 1)
                    clear(nc, q)

        TP = T // 2
        NPC = 4

        def carve(tiles, width):
            room = c.hT_all[:, :, :].rearrange("p c t -> p (c t)")
            at, out = 0, {}
            for k, dt in tiles:
                words = FC * width // (1 if dt == F32 else 2)
                part = room[:, at:at + words]
                out[k] = (part if dt == F32 else part.bitcast(dt)).rearrange("p (f t) -> p f t", f=FC)
                at += words
            assert at <= 2 * B * S
            return out

        def magnitude(v, n, r, part, total, done):
            v.tensor_reduce(cur[:, n:n + 1], r, AX.XY, ALU.max, apply_absolute_value=True).then_inc(part, 1)
            if n == NPC - 1:
                v.wait_ge(part, NPC)
                v.tensor_reduce(cur1[:, :], cur[:, 0:NPC], AX.X, ALU.max).then_inc(total, 1)
                v.wait_ge(total, 1)
                v.tensor_tensor(mx[:, :], mx[:, :], cur1[:, :], ALU.max).then_inc(done, 1)

        make_scale("x", c.amax)
        quantise_input()
        project("up", wuT, None)
        make_scale("u", mx)
        up = sb("up", [128, FC, NTOK], I16)
        project("gate", wgT, up)
        make_scale("g", mx)

        with ExitStack() as once:
            q = signals(nc, once, "gi_ready sig_ready gf_ready sq_ready act_ready g_part g_total g_done")
            tl = carve([(n + str(k), dt) for k in range(2) for n, dt in (("sig", F32), ("gi", I16), ("sq", U16))], TP)
            with nc.Fori(0, NTOK // (TP * NPC)) as i:
                with nc.Block() as block:
                    @block.vector
                    def _(v):
                        for n in range(NPC):
                            k, r = n % 2, raw[:, :, bass.ts(NPC * i + n, TP)]
                            v.wait_ge(q.sig_ready, n + 1)
                            v.tensor_scalar(tl[f"sq{k}"], tl[f"sig{k}"], 65536.0, None, ALU.mult).then_inc(q.sq_ready, 1)
                            v.wait_ge(q.sq_ready, n + 1)
                            v.wait_ge(q.gf_ready, n + 1)
                            v.scalar_tensor_tensor(r, tl[f"sq{k}"], 1.0 / 65536.0, r, ALU.mult, ALU.mult).then_inc(q.act_ready, 1)
                            v.wait_ge(q.act_ready, n + 1)
                            magnitude(v, n, r, q.g_part, q.g_total, q.g_done)

                    @block.scalar
                    def _(a):
                        for n in range(NPC):
                            k, r = n % 2, raw[:, :, bass.ts(NPC * i + n, TP)]
                            a.activation(tl[f"gi{k}"], r, ACT.Copy, scale=inv["g"][:, :]).then_inc(q.gi_ready, 1)
                            if n >= 2:
                                a.wait_ge(q.sq_ready, n - 1)
                            a.wait_ge(q.gi_ready, n + 1)
                            a.activation(tl[f"sig{k}"], tl[f"gi{k}"], ACT.Sigmoid, scale=scale["g"][:, :]).then_inc(q.sig_ready, 1)
                            a.activation(r, tl[f"gi{k}"], ACT.Copy, scale=scale["g"][:, :]).then_inc(q.gf_ready, 1)
                clear(nc, q)
        make_scale("a", mx)

        with ExitStack() as once:
            q = signals(nc, once, "ai_ready uf_ready prod_ready p_part p_total p_done")
            tl = carve([(n + str(k), dt) for k in range(2) for n, dt in (("uf", F32), ("ai", I16))], TP)
            with nc.Fori(0, NTOK // (TP * NPC)) as i:
                with nc.Block() as block:
                    @block.vector
                    def _(v):
                        for n in range(NPC):
                            k, r = n % 2, raw[:, :, bass.ts(NPC * i + n, TP)]
                            v.wait_ge(q.ai_ready, n + 1)
                            v.wait_ge(q.uf_ready, n + 1)
                            v.scalar_tensor_tensor(r, tl[f"ai{k}"], scale["a"][:, :], tl[f"uf{k}"], ALU.mult, ALU.mult).then_inc(q.prod_ready, 1)
                            v.wait_ge(q.prod_ready, n + 1)
                            magnitude(v, n, r, q.p_part, q.p_total, q.p_done)

                    @block.scalar
                    def _(a):
                        for n in range(NPC):
                            k, r = n % 2, raw[:, :, bass.ts(NPC * i + n, TP)]
                            if n >= 2:
                                a.wait_ge(q.prod_ready, n - 1)
                            a.activation(tl[f"ai{k}"], r, ACT.Copy, scale=inv["a"][:, :]).then_inc(q.ai_ready, 1)
                            a.activation(tl[f"uf{k}"], up[:, :, bass.ts(NPC * i + n, TP)], ACT.Copy, scale=scale["u"][:, :]).then_inc(q.uf_ready, 1)
                clear(nc, q)
        make_scale("o", mx)

        with ExitStack() as once:
            q = signals(nc, once, "xf_in0 xf_in1 oi_ready of_ready y_psum y_ready y_out")
            tl = carve((("of0", F32), ("of1", F32), ("oi", I16)), T)
            xin = [once.enter_context(nc.sbuf_tensor(f"x_tile{k}", [128, NT, D], F32)) for k in range(2)]
            with nc.Fori(0, NG // 2) as i:
                with nc.Block() as block:
                    @block.sync
                    def _(s):
                        for k, arrived in ((0, q.xf_in0), (1, q.xf_in1)):
                            s.dma_start(xin[k][:, :, :], dr["x_c"].rearrange("(i j p) n -> i p j n", p=128, j=NT)[2 * i + k]).then_inc(arrived, 16)
                        for k in range(2):
                            s.wait_ge(q.y_ready, NT * (k + 1))
                            s.dma_start(out.rearrange("(i j p) n -> i p j n", p=128, j=NT)[2 * i + k], xin[k][:, :, :]).then_inc(q.y_out, 16)
                        s.wait_ge(q.y_out, 32)

                    @block.scalar
                    def _(a):
                        for k in range(2):
                            if k:
                                a.wait_ge(q.of_ready, 1)
                            a.activation(tl["oi"], raw[:, :, bass.ts(2 * i + k, T)], ACT.Copy, scale=inv["o"][:, :]).then_inc(q.oi_ready, 1)

                    @block.vector
                    def _(v):
                        for k in range(2):
                            v.wait_ge(q.oi_ready, k + 1)
                            v.tensor_scalar(tl[f"of{k}"], tl["oi"], scale["o"][:, :], None, ALU.mult).then_inc(q.of_ready, 1)
                        for k, arrived in ((0, q.xf_in0), (1, q.xf_in1)):
                            v.wait_ge(arrived, 16)
                            for j in range(NT):
                                n = NT * k + j
                                v.wait_ge(q.y_psum, n + 1)
                                v.tensor_tensor(xin[k][:, j, :], P[n][:, 0:D], xin[k][:, j, :], ALU.add).then_inc(q.y_ready, 1)

                    @block.tensor
                    def _(p):
                        for k in range(2):
                            p.wait_ge(q.of_ready, k + 1)
                            for j in range(NT):
                                for f in range(FC):
                                    t = p.matmul(P[NT * k + j][:, 0:D], tl[f"of{k}"][:, f, 128 * j:128 * j + 128], wdT[:, f, :],
                                                 start=(f == 0), stop=(f == FC - 1))
                                t.then_inc(q.y_psum, 1)
                clear(nc, q)


class Common:
    pass


def program(nc, io, dr, out):
    ctx = ExitStack()
    with ctx:
        c = Common()
        c.banks = [ctx.enter_context(nc.psum_tensor(f"bank{k}", [128, 512], F32)) for k in range(8)]
        c.scattered = ctx.enter_context(nc.semaphore("scattered"))
        c.gathered = ctx.enter_context(nc.semaphore("gathered"))
        c.ident = ctx.enter_context(nc.sbuf_tensor("ident", [128, 128], F32))
        with ExitStack() as once:
            q = signals(nc, once, "ident_made")
            with nc.Block() as block:
                @block.gpsimd
                def _(g):
                    g.memset(c.ident[:, :], 0.0).then_inc(q.ident_made, 1)
                    g.wait_ge(q.ident_made, 1)
                    g.affine_select(out=c.ident[:, :], in_=c.ident[:, :], pattern=[[-1, 128]], base=0, channel_multiplier=1,
                                    compare_op=ALU.not_equal, fill=1.0).then_inc(q.ident_made, 1)
            clear(nc, q)
        layer0(nc, ctx, c, io, dr)
        experts(nc, ctx, c, io, dr)
        c.hT_all = ctx.enter_context(nc.sbuf_tensor("hT_all", [128, 2, B * S], F32))
        c.amax = ctx.enter_context(nc.sbuf_tensor("amax_all", [128, 1], F32))
        layer1(nc, ctx, c, io, dr)
        feed_forward(nc, ctx, c, io, dr, out)


def kernel(**inputs):
    import numpy as _np
    import concourse.bacc as _bacc
    from concourse import mybir as _mybir
    from concourse.bass_utils import run_bass_kernel_spmd as _run

    t = {k: _np.asarray(v) for k, v in inputs.items()}
    lay = {k: v for k, v in t.items()}
    lay["x"] = t["x"].reshape(B * S, D)
    lay["ctxT"] = t["ctx_1024"].transpose(0, 2, 1)
    lay["mask_Bx1xSxS2_ff0"] = t["mask_Bx1xSxS2_ff0"].reshape(B * S, S2)
    del lay["ctx_1024"]
    for k in ("L0_attn_Wq", "L0_attn_Wk", "L0_attn_Wv", "L0_attn_Wo", "L0_ffn_gate_w", "L1_attn_Wq",
              "L1_attn_Wkv_down", "L1_attn_Wk_up", "L1_attn_Wv_up", "L1_attn_Wo"):
        lay[k] = t[k].T
    for k in ("wq", "wk", "wv"):
        lay["L0_xattn_" + k] = t["L0_xattn_" + k].reshape(D, D)
    lay["L0_xattn_wo"] = t["L0_xattn_wo"].reshape(D, D)

    nc = _bacc.Bacc("TRN2", target_bir_lowering=False, num_devices=1)
    arrays, io = {}, {}
    for k, v in lay.items():
        arrays[k] = _np.ascontiguousarray(v)
        io[k] = nc.dram_tensor(k, v.shape, _mybir.dt.from_np(v.dtype), kind="ExternalInput").ap()
    f32, i32 = _mybir.dt.float32, _mybir.dt.int32
    dr = {}
    for k, shape, dt in (("x_a", (B * S, D), f32), ("x_c", (B * S, D), f32), ("slots_in", (SLOTS, D), f32),
                         ("slots_out", (SLOTS, D), f32), ("slot_g", (NG, 128, TOPK * NT), i32),
                         ("wt", (NG, 128, TOPK * NT), f32)):
        dr[k] = nc.dram_tensor("t_" + k, shape, dt, kind="Internal").ap()
    out = nc.dram_tensor("out", (B * S, D), f32, kind="ExternalOutput").ap()
    program(nc, io, dr, out)
    r = _run(nc, [arrays], core_ids=[0])
    return r.results[0]["out"].reshape(B, S, D)
```

```python
import numpy as np
import concourse.bass as bass
from concourse import mybir
from collections import namedtuple
from contextlib import ExitStack

F32 = mybir.dt.float32
BF16 = mybir.dt.bfloat16
I32 = mybir.dt.int32
U32 = mybir.dt.uint32
I16 = mybir.dt.int16
U16 = mybir.dt.uint16
ALU = mybir.AluOpType
ACT = mybir.ActivationFunctionType
AX = mybir.AxisListType
RMAX = bass.bass_isa.ReduceOp.max

B, S, D = 16, 256, 256
S2 = 77
H, HD = 16, 16
T = 512
NT = T // 128
NB = T // S
NG = B * S // T
E, TOPK = 16, 2
CAP = int(1.25 * B * S * TOPK / E)
SLOTS = E * CAP
FF0 = 512
H1, HD1 = 8, 64
LR = 64
FF1 = 768
FC = FF1 // 128
BLK = 32
LN_EPS = 1e-5
DEN_EPS = 1e-5
QMAX = 32767.0
WMAX = 7.0


def signals(nc, ctx, names):
    return namedtuple("Signals", names)(*[ctx.enter_context(nc.semaphore(name)) for name in names.split()])


def clear(nc, q):
    numbers = sorted(s.num for s in q)
    while numbers:
        run = 1
        while run < len(numbers) and numbers[run] == numbers[0] + run:
            run += 1
        nc.gpsimd.sem_clear(range(numbers[0], numbers[0] + run))
        numbers = numbers[run:]
    nc.all_engine_barrier()


def bcast(ap, axis, n):
    shape = list(ap.shape)
    shape.insert(axis, n)
    return ap.unsqueeze(axis).broadcast_to(shape)


class Norm:

    def __init__(self, nc, ctx, tag):
        sb = lambda name, shape: ctx.enter_context(nc.sbuf_tensor(f"{tag}_{name}", shape, F32))
        self.stats = sb("stats", [128, NT, 6])
        self.mv = sb("mean_var", [128, NT, 2])
        self.ve = sb("var_eps", [128, NT])
        self.rstd = sb("rstd", [128, NT])
        self.power = sb("power", [128, NT])
        self.h = sb("h", [128, NT, D])

    def vector(self, v, q, src, n, tiles=range(NT), before=None):
        self.moments(v, q, src, n, tiles, before)
        self.scale(v, q, src, n, tiles)

    def moments(self, v, q, src, n, tiles=range(NT), before=None):
        before = NT * n if before is None else before
        for j in tiles:
            v.bn_stats(self.stats[:, j, :], src[:, j, :]).then_inc(q.ln_stats, 1)
        v.wait_ge(q.ln_stats, before + len(tiles))
        for j in tiles:
            v.bn_aggr(self.mv[:, j, :], self.stats[:, j, :]).then_inc(q.ln_moments, 1)
        v.wait_ge(q.ln_moments, before + len(tiles))
        own = slice(tiles[0], tiles[-1] + 1)
        v.tensor_scalar(self.ve[:, own], self.mv[:, own, 1], LN_EPS, None, ALU.add).then_inc(q.ln_var, 1)

    def scale(self, v, q, src, n, tiles=range(NT)):
        v.wait_ge(q.ln_rstd, n + 1)
        for j in tiles:
            v.tensor_scalar(self.h[:, j, :], src[:, j, :], self.mv[:, j, 0:1], self.rstd[:, j:j + 1],
                            ALU.subtract, ALU.mult).then_inc(q.ln_h, 1)

    def gpsimd(self, g, q, n, tiles=range(NT)):
        own = slice(tiles[0], tiles[-1] + 1)
        g.wait_ge(q.ln_var, n + 1)
        g.tensor_tensor(self.rstd[:, own], self.ve[:, own], self.power[:, own], ALU.pow).then_inc(q.ln_rstd, 1)

    def tensor(self, p, q, n, banks, ident, before=None):
        before = NT * n if before is None else before
        for j in range(NT):
            p.wait_ge(q.ln_h, before + j + 1)
            for c in range(2):
                t = p.transpose(banks[c][:, 128 * j:128 * j + 128], self.h[:, j, 128 * c:128 * c + 128], ident)
        t.then_inc(q.hT_psum, 1)

    def scalar(self, a, q, n, banks, hT):
        a.wait_ge(q.hT_psum, n + 1)
        for c in range(2):
            a.activation(hT[:, c, :], banks[c][:, :], ACT.Copy).then_inc(q.hT_ready, 1)


def fill_selector(g, q, out, conditions):
    n = q[1]
    g.memset(out, 1.0).then_inc(q[0], 1)
    n += 1
    for base, mult, pattern, op in conditions:
        g.wait_ge(q[0], n)
        g.affine_select(out=out, in_=out, pattern=pattern, base=base, channel_multiplier=mult,
                        compare_op=op, fill=0.0).then_inc(q[0], 1)
        n += 1
    q[1] = n
    return n


def layer0(nc, ctx, c, io, dr):
    st = ExitStack()
    with st:
        def sb(name, shape, dt=F32):
            return st.enter_context(nc.sbuf_tensor("a_" + name, shape, dt))
        P = c.banks
        ident = c.ident[:, :]
        wq, wk, wv, wo = (sb(n, [128, 2, D]) for n in ("wq", "wk", "wv", "wo"))
        xwq, xwk, xwv, xwo = (sb(n, [128, 2, D]) for n in ("xwq", "xwk", "xwv", "xwo"))
        wg = sb("wg", [128, 2, E])
        bo = sb("bo", [128, D])
        causal = sb("causal", [128, 384])
        headsel = sb("headsel", [128, 8])
        before = sb("before", [128, 128], BF16)
        ones = sb("ones", [128, 128], BF16)
        eid = sb("eid", [128, E])
        carry = sb("carry", [128, E])
        left = sb("left", [128, 1])
        zeros = sb("zeros", [128, 2048])

        norm0, norm, norm2 = Norm(nc, st, "a0"), Norm(nc, st, "a1"), Norm(nc, st, "a2")
        xin = sb("xin", [128, NT, D])
        x1 = sb("x1", [128, NT, D])
        x2 = sb("x2", [128, NT, D])
        hT0 = sb("hT0", [128, 2, T])
        hT = sb("hT", [128, 2, T])
        eq = sb("eq", [128, 2, T])
        ek = sb("ek", [128, 2, T])
        pq = sb("pq", [128, 2, T])
        pk = sb("pk", [128, 2, T])
        kbd = sb("kbd", [128, NB, 2, 8, S])
        vpad = sb("vpad", [128, NT, H, 32])
        A = sb("A", [128, 8, 384])
        oT = sb("oT", [128, 4, T])
        rden = sb("rden", [128, NT, H])
        den = sb("den", [128, NT, H])
        at = sb("at", [128, NT, D])
        aT = sb("aT", [128, 2, T])

        ctxT = sb("ctxT", [128, 2, NB, S2])
        amask = sb("amask", [128, NT, S2])
        xqT = sb("xqT", [128, 2, T])
        xk = sb("xk", [128, 2, NB, S2])
        xkbd = sb("xkbd", [128, NB, 2, 8, S2])
        xvpad = sb("xvpad", [S2, NB, H, 32])
        L = sb("L", [128, 3, H, S2])
        Lm = sb("Lm", [128, NT, H])
        L2 = sb("L2", [128, 3, H, S2])
        PT = kbd[0:S2, :, :, :, :].rearrange("k b u h t -> k b (u h) t")

        lg = sb("lg", [128, NT, E])
        top = sb("top", [128, NT, 8])
        topi = sb("topi", [128, NT, 8], U32)
        topf = sb("topf", [128, NT, TOPK])
        oh = sb("oh", [128, TOPK, NT, E])
        M = sb("M", [128, NT, E], BF16)
        rank = sb("rank", [128, NT, E])
        pick = sb("pick", [128, TOPK, NT, E])
        r = sb("r", [128, TOPK, NT])
        valid = sb("valid", [128, TOPK, NT])
        slot = sb("slot", [128, TOPK, NT])
        drop = sb("drop", [128, TOPK, NT])
        slot_s = sb("slot_s", [128, TOPK, NT], I32)
        slot_g = sb("slot_g", [128, TOPK, NT], I32)
        prob = sb("prob", [128, TOPK, NT])
        psum2 = sb("psum2", [128, NT])
        wt = sb("wt", [128, TOPK, NT])

        with ExitStack() as once:
            q = signals(nc, once, "a_w a_const a_dve")
            with nc.Block() as block:
                @block.sync
                def _(s):
                    n = 0
                    for dst, src in ((wq, io["L0_attn_Wq"]), (wk, io["L0_attn_Wk"]), (wv, io["L0_attn_Wv"]),
                                     (wo, io["L0_attn_Wo"]), (xwq, io["L0_xattn_wq"]), (xwk, io["L0_xattn_wk"]),
                                     (xwv, io["L0_xattn_wv"]), (xwo, io["L0_xattn_wo"]), (wg, io["L0_ffn_gate_w"])):
                        s.dma_start(dst[:, :, :], src.rearrange("(c p) n -> p c n", p=128)).then_inc(q.a_w, 16)
                        n += 16
                    s.dma_start(bo[:, :], io["L0_attn_bo"].unsqueeze(0).broadcast_to([128, D])).then_inc(q.a_w, 16)
                    n += 16
                    s.wait_ge(q.a_w, n)

                @block.vector
                def _(v):
                    v.memset(zeros[:, :], 0.0).then_inc(q.a_dve, 1)
                    v.memset(vpad[:, :, :, :], 0.0).then_inc(q.a_dve, 1)
                    v.memset(xvpad[:, :, :, :], 0.0).then_inc(q.a_dve, 1)
                    v.memset(carry[:, :], 0.0).then_inc(q.a_dve, 1)
                    v.memset(ones[:, :], 1.0).then_inc(q.a_dve, 1)
                    v.wait_ge(q.a_dve, 5)
                    v.memset(vpad[:, :, :, HD:HD + 1], 1.0).then_inc(q.a_dve, 1)
                    v.memset(xvpad[:, :, :, HD:HD + 1], 1.0).then_inc(q.a_dve, 1)

                @block.gpsimd
                def _(g):
                    k = [q.a_const, 0]
                    fill_selector(g, k, headsel[:, :], [(0, 1, [[-16, 8]], ALU.is_ge), (15, -1, [[16, 8]], ALU.is_ge)])
                    fill_selector(g, k, causal[:, 0:128], [(0, -1, [[1, 128]], ALU.is_ge)])
                    g.memset(causal[:, 128:256], 1.0)
                    fill_selector(g, k, causal[:, 256:384], [(0, -1, [[1, 128]], ALU.is_ge)])
                    fill_selector(g, k, before[:, :], [(0, -1, [[1, 128]], ALU.is_gt)])
                    g.iota(eid[:, :], [[1, E]], base=0, channel_multiplier=0, allow_small_or_imprecise_dtypes=True)
                    for m in (norm0, norm, norm2):
                        g.memset(m.power[:, :], -0.5)
            clear(nc, q)

        q = signals(nc, st, "x_in ctx_in next_in ln_stats ln_moments ln_var ln_rstd ln_h hT_psum hT_ready xh_psum xh_ready q_psum "
                            "v_psum eq_ready ek_ready eq_min ek_min pq_ready pk_ready kbd_ready kbd1_ready v_ready s_psum A_ready "
                            "o_psum oT_ready tok_psum den_ready rden_ready at_ready aT_psum aT_ready proj_psum xb_ready x1_ready "
                            "xk_psum xv_psum xq_psum xk_ready xkbd_ready xv_ready xq_ready l_psum L_ready Lm_ready L2_ready "
                            "exp_ready pt_psum PT_ready x2_ready gate_psum lg_ready top_ready topi_ready router "
                            "eneg rank_psum slots_ready stored x2_stored kept zeroed")
        scattered = c.scattered
        x_rows = io["x"].rearrange("(i j p) n -> i p j n", p=128, j=NT)
        y_rows = dr["x_a"].rearrange("(i j p) n -> i p j n", p=128, j=NT)
        ctx_cols = io["ctxT"].rearrange("(i b) (c p) k -> i c p b k", b=NB, p=128)
        mask_rows = io["mask_Bx1xSxS2_ff0"].rearrange("(i j p) k -> i p j k", p=128, j=NT)
        slot_rows = dr["slots_in"].rearrange("(a p r) n -> a p (r n)", p=128, r=8)

        def router_scalar(a):
            a.wait_ge(q.top_ready, NT)
            a.activation(prob[:, :, :], top[:, :, 0:TOPK].rearrange("p j k -> p k j"), ACT.Exp, scale=-1.0).then_inc(q.eneg, 1)

        def router_logits(p):
            for j in range(NT):
                for u in range(2):
                    t = p.matmul(P[6][:, E * j:E * j + E], hT[:, u, 128 * j:128 * j + 128], wg[:, u, :], start=(u == 0), stop=(u == 1))
            t.then_inc(q.gate_psum, 1)

        def router_choose(v):
            v.wait_ge(q.gate_psum, 1)
            v.tensor_copy(lg[:, :, :], P[6][:, 0:NT * E].rearrange("p (j e) -> p j e", e=E)).then_inc(q.lg_ready, 1)
            v.wait_ge(q.lg_ready, 1)
            for j in range(NT):
                v.max(top[:, j, :], lg[:, j, :]).then_inc(q.top_ready, 1)
            v.wait_ge(q.top_ready, NT)
            for j in range(NT):
                v.max_index(topi[:, j, :], top[:, j, :], lg[:, j, :]).then_inc(q.topi_ready, 1)
            v.wait_ge(q.topi_ready, NT)
            v.tensor_copy(topf[:, :, :], topi[:, :, 0:TOPK]).then_inc(q.router, 1)
            v.wait_ge(q.router, 1)
            for k in range(TOPK):
                v.tensor_tensor(oh[:, k, :, :], bcast(eid[:, :], 1, NT), bcast(topf[:, :, k], 2, E), ALU.is_equal).then_inc(q.router, 1)
            v.wait_ge(q.router, 3)
            v.tensor_tensor(M[:, :, :], oh[:, 0, :, :], oh[:, 1, :, :], ALU.add).then_inc(q.kept, 1)

        def router_rank(p):
            p.wait_ge(q.kept, 1)
            for j in range(NT + 1):
                if j < NT:
                    p.matmul(P[6][:, E * j:E * j + E], before[:, :], M[:, j, :], start=True, stop=(j == 0))
                for k in range(j):
                    t = p.matmul(P[6][:, E * j:E * j + E], ones[:, :], M[:, k, :], start=(j == NT and k == 0), stop=(k == j - 1))
            t.then_inc(q.rank_psum, 1)

        def router_steps(v, done):
            steps = [done]

            def step(ins):
                ins.then_inc(q.router, 1)
                steps[0] += 1
                v.wait_ge(q.router, steps[0])
            return step

        def router_weights(v):
            step = router_steps(v, 3)
            v.wait_ge(q.eneg, 1)
            step(v.tensor_scalar(prob[:, :, :], prob[:, :, :], 1.0, None, ALU.add))
            step(v.reciprocal(prob[:, :, :], prob[:, :, :]))
            step(v.tensor_tensor(psum2[:, :], prob[:, 0, :], prob[:, 1, :], ALU.add))
            step(v.tensor_scalar(psum2[:, :], psum2[:, :], 1e-6, None, ALU.add))
            step(v.reciprocal(psum2[:, :], psum2[:, :]))
            step(v.tensor_tensor(wt[:, :, :], prob[:, :, :], bcast(psum2[:, :], 1, TOPK), ALU.mult))

        def router_place(v):
            step = router_steps(v, 9)
            v.wait_ge(q.rank_psum, 1)
            step(v.tensor_tensor(rank[:, :, :], P[6][:, 0:NT * E].rearrange("p (j e) -> p j e", e=E), bcast(carry[:, :], 1, NT), ALU.add))
            step(v.tensor_tensor(carry[:, :], P[6][:, NT * E:NT * E + E], carry[:, :], ALU.add))
            for k in range(TOPK):
                step(v.tensor_tensor(pick[:, k, :, :], oh[:, k, :, :], rank[:, :, :], ALU.mult))
            step(v.tensor_reduce(r[:, :, :], pick[:, :, :, :], AX.X, ALU.add))
            step(v.tensor_scalar(valid[:, :, :], r[:, :, :], float(CAP), None, ALU.is_lt))
            step(v.scalar_tensor_tensor(slot[:, :, :], topf[:, :, :].rearrange("p j k -> p k j"), float(CAP), r[:, :, :], ALU.mult, ALU.add))
            step(v.tensor_scalar(drop[:, :, :], valid[:, :, :], -float(4 * SLOTS), float(4 * SLOTS), ALU.mult, ALU.add))
            step(v.tensor_tensor(slot[:, :, :], slot[:, :, :], drop[:, :, :], ALU.add))
            step(v.tensor_copy(slot_s[:, :, :], slot[:, :, :]))
            step(v.tensor_scalar(slot_g[:, :, :], slot[:, :, :], float(SLOTS - 1), None, ALU.min))
            v.tensor_tensor(wt[:, :, :], wt[:, :, :], valid[:, :, :], ALU.mult).then_inc(q.slots_ready, 1)

        def router_scatter(g):
            g.wait_ge(q.slots_ready, 1)
            for k in range(TOPK):
                for j in range(NT):
                    g.indirect_dma_start(out=dr["slots_in"], out_offset=bass.IndirectOffsetOnAxis(ap=slot_s[:, k, j:j + 1], axis=0),
                                         in_=norm2.h[:, j, :], in_offset=None,
                                         bounds_check=SLOTS - 1, oob_is_err=False).then_inc(scattered, 16)

        def router_store(s, i):
            s.wait_ge(q.slots_ready, 1)
            s.dma_start(dr["slot_g"][i], slot_g[:, :, :].rearrange("p k j -> p (k j)")).then_inc(q.stored, 16)
            s.dma_start(dr["wt"][i], wt[:, :, :].rearrange("p k j -> p (k j)")).then_inc(q.stored, 16)

        def keys(p, n, halves):
            p.wait_ge(q.hT_ready, 2 * n)
            for m in halves:
                for u in range(2):
                    p.matmul(P[m][:, :], wk[:, u, 128 * m:128 * m + 128], hT0[:, u, :], start=(u == 0), stop=(u == 1))

        with nc.Block() as block:
            @block.sync
            def _(s):
                s.dma_start(xin[:, :, :], x_rows[0]).then_inc(q.x_in, 16)

            @block.vector
            def _(v):
                v.wait_ge(q.x_in, 16)
                norm0.vector(v, q, xin, 0)

            @block.gpsimd
            def _(g):
                norm0.gpsimd(g, q, 0)

            @block.tensor
            def _(p):
                norm0.tensor(p, q, 0, P[6:8], ident)
                keys(p, 1, (0, 1))

            @block.scalar
            def _(a):
                norm0.scalar(a, q, 0, P[6:8], hT0)
        clear(nc, q)

        def group(i, first):
            N1 = 0 if first else 1
            with nc.Block() as block:
                @block.sync
                def _(s):
                    for u in range(2):
                        s.dma_start(ctxT[:, u, :, :], ctx_cols[i, u]).then_inc(q.ctx_in, 16)
                    s.dma_start(amask[:, :, :], mask_rows[i]).then_inc(q.ctx_in, 16)
                    if first:
                        for a in range(SLOTS // 1024):
                            s.dma_start(slot_rows[a], zeros[:, :]).then_inc(q.zeroed, 16)
                    else:
                        s.dma_start(y_rows[i - 1], x2[:, :, :]).then_inc(q.x2_stored, 16)
                        router_store(s, i - 1)
                    s.wait_ge(q.x1_ready, NB)
                    s.dma_start(xin[:, :, :], x_rows[(i + 1) % NG]).then_inc(q.next_in, 16)
                    if first:
                        s.wait_ge(q.zeroed, 16 * (SLOTS // 1024))
                    else:
                        s.wait_ge(q.x2_stored, 16)
                        s.wait_ge(q.stored, 32)
                    s.wait_ge(q.next_in, 16)

                @block.gpsimd
                def _(g):
                    for n, (b, u) in enumerate(((0, 1), (1, 0), (1, 1))):
                        if n == 0:
                            g.wait_ge(q.pk_ready, 2)
                        if n == 1 and not first:
                            norm2.gpsimd(g, q, 0)
                        g.tensor_tensor(kbd[:, b, u, :, :], bcast(pk[:, u, S * b:S * b + S], 1, 8), bcast(headsel[:, :], 2, S),
                                        ALU.mult).then_inc(q.kbd1_ready, 1)
                    for j in range(NT):
                        g.tensor_tensor(xin[:, j, :], xin[:, j, :], bo[:, :], ALU.add).then_inc(q.xb_ready, 1)
                    g.wait_ge(q.xk_ready, 1)
                    for b in range(NB):
                        for u in range(2):
                            g.tensor_tensor(xkbd[:, b, u, :, :], bcast(xk[:, u, b, :], 1, 8), bcast(headsel[:, :], 2, S2),
                                            ALU.mult).then_inc(q.xkbd_ready, 1)
                    if not first:
                        router_scatter(g)

                    def less_maximum(j):
                        g.wait_ge(q.Lm_ready, j + 1)
                        if j >= 3:
                            g.wait_ge(q.pt_psum, 4 * (j - 2))
                        g.tensor_tensor(L2[:, j % 3, :, :], L[:, j % 3, :, :],
                                        bcast(Lm[:, j, :], 2, S2), ALU.subtract).then_inc(q.L2_ready, 1)

                    norm.gpsimd(g, q, N1, range(0, 2))
                    less_maximum(0)
                    norm.gpsimd(g, q, N1 + 1, range(2, 4))
                    for j in range(1, NT):
                        less_maximum(j)
                    norm0.gpsimd(g, q, N1 + 2)
                    if not first:
                        g.wait_ge(scattered, 16 * TOPK * NT * i)
                        g.tensor_tensor(left[:, :], norm.power[:, 0:1], norm.power[:, 0:1], ALU.add)

                @block.tensor
                def _(p):
                    def to_tokens(n, b):
                        p.wait_ge(q.oT_ready, 8 * n + 4 * b + 4)
                        for j in (2 * b, 2 * b + 1):
                            for u in range(4):
                                t = p.transpose(P[6 + j % 2][:, 128 * u:128 * u + 128], oT[:, u, 128 * j:128 * j + 128], ident)
                            t.then_inc(q.tok_psum, 1)

                    def to_columns(n, b):
                        p.wait_ge(q.at_ready, NT * n + 2 * b + 2)
                        for j in (2 * b, 2 * b + 1):
                            for u in range(2):
                                t = p.transpose(P[6][:, S * u + 128 * (j % 2):S * u + 128 * (j % 2) + 128], at[:, j, 128 * u:128 * u + 128], ident)
                        t.then_inc(q.aT_psum, 1)

                    def project(n, b):
                        p.wait_ge(q.aT_ready, NB * n + b + 1)
                        w = wo if n == 0 else xwo
                        for j in (2 * b, 2 * b + 1):
                            for u in range(2):
                                t = p.matmul(P[7][:, D * (j % 2):D * (j % 2) + D], aT[:, u, 128 * j:128 * j + 128],
                                             w[:, u, :], start=(u == 0), stop=(u == 1))
                        t.then_inc(q.proj_psum, 1)

                    def turn_norm(b):
                        p.wait_ge(q.ln_h, NT * N1 + 2 * b + 2)
                        for j in (2 * b, 2 * b + 1):
                            for u in range(2):
                                t = p.transpose(P[6][:, S * u + 128 * (j % 2):S * u + 128 * (j % 2) + 128], norm.h[:, j, 128 * u:128 * u + 128], ident)
                        t.then_inc(q.xh_psum, 1)

                    def x_queries(b):
                        p.wait_ge(q.xh_ready, b + 1)
                        p.wait_ge(q.x1_ready, b + 1)
                        for m in range(2):
                            for u in range(2):
                                t = p.matmul(P[7][:, S * m:S * m + S], xwq[:, u, 128 * m:128 * m + 128], hT[:, u, S * b:S * b + S],
                                             start=(u == 0), stop=(u == 1))
                        t.then_inc(q.xq_psum, 1)

                    for m in range(2):
                        for u in range(2):
                            t = p.matmul(P[2 + m][:, :], wq[:, u, 128 * m:128 * m + 128], hT0[:, u, :], start=(u == 0), stop=(u == 1))
                        t.then_inc(q.q_psum, 1)
                    for j in range(NT):
                        for u in range(2):
                            t = p.matmul(P[6 + j // 2][:, D * (j % 2):D * (j % 2) + D], hT0[:, u, 128 * j:128 * j + 128], wv[:, u, :],
                                         start=(u == 0), stop=(u == 1))
                        t.then_inc(q.v_psum, 1)
                    p.wait_ge(q.ctx_in, 48)
                    for m in range(2):
                        for u in range(2):
                            t = p.matmul(P[4][:, 154 * m:154 * m + 154], xwk[:, u, 128 * m:128 * m + 128],
                                         ctxT[:, u, :, :].rearrange("p b k -> p (b k)"), start=(u == 0), stop=(u == 1))
                    t.then_inc(q.xk_psum, 1)
                    for b in range(NB):
                        for u in range(2):
                            t = p.matmul(P[5][0:S2, D * b:D * b + D], ctxT[:, u, b, :], xwv[:, u, :], start=(u == 0), stop=(u == 1))
                    t.then_inc(q.xv_psum, 1)
                    p.wait_ge(q.pk_ready, 2)
                    p.wait_ge(q.pq_ready, 2)

                    def lin_values(m):
                        b, u = m // 4, m % 4
                        if m >= 2:
                            p.wait_ge(q.oT_ready, m - 1)
                        for s in range(2):
                            for hh in range(4):
                                n = 4 * m + hh
                                p.wait_ge(q.A_ready, n + 1)
                                cols = slice(0, 256) if s == 0 else slice(256, 384)
                                t = p.matmul(P[4 + m % 2][32 * hh:32 * hh + 32, 128 * s:256], vpad[:, 2 * b + s, 4 * u + hh, :],
                                             A[:, n % 8, cols], start=(s == 0), stop=(s == 1), tile_position=(0, 32 * hh),
                                             skip_group_check=True)
                        t.then_inc(q.o_psum, 1)

                    for n in range(NB * H + 2):
                        if n < NB * H:
                            b, h = n // H, n % H
                            u = h // 8
                            if n == 0:
                                p.wait_ge(q.kbd_ready, 1)
                            elif h % 8 == 0:
                                p.wait_ge(q.kbd1_ready, 2 * b + u)
                            if n >= 4:
                                p.wait_ge(q.A_ready, n - 3)
                            p.matmul(P[n % 4][:, 0:256], kbd[:, b, u, h % 8, 0:128], pq[:, u, S * b:S * b + S], start=True, stop=True)
                            p.matmul(P[n % 4][:, 256:384], kbd[:, b, u, h % 8, 128:256], pq[:, u, S * b + 128:S * b + 256],
                                     start=True, stop=True).then_inc(q.s_psum, 1)
                        if n == 4:
                            p.wait_ge(q.v_ready, NT)
                            p.wait_ge(q.xk_ready, 1)
                            p.wait_ge(q.xv_ready, NB)
                            if not first:
                                norm2.tensor(p, q, 0, P[4:6], ident)
                                p.wait_ge(q.hT_ready, 2)
                        if n == 5 and not first:
                            router_logits(p)
                        if n == 11 and not first:
                            router_rank(p)
                        if n >= 5 and n % 4 == 1:
                            lin_values((n - 5) // 4)
                        if n == 19:
                            if not first:
                                p.wait_ge(q.slots_ready, 1)
                            to_tokens(0, 0)
                        if n == 23:
                            to_columns(0, 0)
                        if n == 25:
                            project(0, 0)
                        if n == 30:
                            turn_norm(0)
                        if n == 32:
                            x_queries(0)
                    p.wait_ge(q.A_ready, NB * H)

                    def x_scores(j):
                        for u in range(4):
                            n = 4 * j + u
                            if n >= 4:
                                p.wait_ge(q.L_ready, n - 3)
                            p.matmul(P[n % 4][:, 0:308], xqT[:, u // 2, 128 * j:128 * j + 128],
                                     xkbd[:, j // 2, u // 2, 4 * (u % 2):4 * (u % 2) + 4, :].rearrange("p h k -> p (h k)"),
                                     start=True, stop=True).then_inc(q.l_psum, 1)

                    def x_turn(j):
                        p.wait_ge(q.exp_ready, j + 1)
                        for u in range(4):
                            n = 4 * j + u
                            if n >= 2:
                                p.wait_ge(q.PT_ready, n - 1)
                            for hh in range(4):
                                t = p.transpose(P[4 + n % 2][0:S2, 128 * hh:128 * hh + 128], L2[:, j % 3, 4 * u + hh, :], ident)
                            t.then_inc(q.pt_psum, 1)

                    def x_values(b):
                        p.wait_ge(q.PT_ready, 8 * b + 8)
                        for u in range(4):
                            m = 4 * b + u
                            if m >= 2:
                                p.wait_ge(q.oT_ready, 8 + m - 1)
                            for hh in range(4):
                                t = p.matmul(P[6 + m % 2][32 * hh:32 * hh + 32, 0:256], xvpad[:, b, 4 * u + hh, :],
                                             PT[:, b, 4 * u + hh, :], start=True, stop=True, tile_position=(0, 32 * hh))
                            t.then_inc(q.o_psum, 1)

                    p.wait_ge(q.xq_ready, 1)
                    p.wait_ge(q.xkbd_ready, 4)
                    x_scores(0)
                    to_tokens(0, 1)
                    x_scores(1)
                    to_columns(0, 1)
                    project(0, 1)
                    x_turn(0)
                    turn_norm(1)
                    x_turn(1)
                    x_queries(1)
                    p.wait_ge(q.xq_ready, 2)
                    x_scores(2)
                    x_values(0)
                    x_scores(3)
                    to_tokens(1, 0)
                    x_turn(2)
                    to_columns(1, 0)
                    x_turn(3)
                    project(1, 0)
                    p.wait_ge(q.PT_ready, 16)
                    norm0.tensor(p, q, N1, P[4:6], ident, NT * (N1 + 1))
                    p.wait_ge(q.x2_ready, 1)
                    x_values(1)
                    p.wait_ge(q.L_ready, 16)
                    keys(p, N1 + 1, (0,))
                    to_tokens(1, 1)
                    keys(p, N1 + 1, (1,))
                    to_columns(1, 1)
                    project(1, 1)

                @block.scalar
                def _(a):
                    for m in range(2):
                        a.activation(ek[:, m, :], P[m][:, :], ACT.Exp).then_inc(q.ek_ready, 1)
                    for m in range(2):
                        a.wait_ge(q.q_psum, m + 1)
                        a.activation(eq[:, m, :], P[2 + m][:, :], ACT.Exp).then_inc(q.eq_ready, 1)
                    for j in range(NT):
                        a.wait_ge(q.v_psum, 2 * (j // 2) + 2)
                        a.activation(vpad[:, j, :, 0:HD], P[6 + j // 2][:, D * (j % 2):D * (j % 2) + D].rearrange("p (h d) -> p h d", d=HD),
                                     ACT.Copy).then_inc(q.v_ready, 1)
                    a.wait_ge(q.xk_psum, 1)
                    a.activation(xk[:, :, :, :].rearrange("p c b k -> p (c b k)"), P[4][:, 0:308], ACT.Copy).then_inc(q.xk_ready, 1)
                    a.wait_ge(q.xv_psum, 1)
                    for b in range(NB):
                        a.activation(xvpad[:, b, :, 0:HD], P[5][0:S2, D * b:D * b + D].rearrange("p (h d) -> p h d", d=HD),
                                     ACT.Copy).then_inc(q.xv_ready, 1)
                    if not first:
                        norm2.scalar(a, q, 0, P[4:6], hT)

                    def keep_columns(n, b):
                        a.wait_ge(q.aT_psum, NB * n + b + 1)
                        a.activation(aT[:, :, S * b:S * b + S], P[6][:, :].rearrange("p (c t) -> p c t", c=2), ACT.Copy).then_inc(q.aT_ready, 1)

                    def keep_norm(b):
                        a.wait_ge(q.xh_psum, b + 1)
                        a.activation(hT[:, :, S * b:S * b + S], P[6][:, :].rearrange("p (c t) -> p c t", c=2), ACT.Copy).then_inc(q.xh_ready, 1)

                    def keep_queries(b):
                        a.wait_ge(q.xq_psum, b + 1)
                        a.activation(xqT[:, :, S * b:S * b + S], P[7][:, :].rearrange("p (c t) -> p c t", c=2), ACT.Copy,
                                     scale=HD ** -0.5).then_inc(q.xq_ready, 1)

                    for m in range(8):
                        if m == 1 and not first:
                            router_scalar(a)
                        if m == 7:
                            keep_norm(0)
                            keep_queries(0)
                        a.wait_ge(q.o_psum, m + 1)
                        a.activation(oT[:, m % 4, S * (m // 4):S * (m // 4) + S], P[4 + m % 2][:, 0:256], ACT.Copy).then_inc(q.oT_ready, 1)
                        if m == 4:
                            keep_columns(0, 0)

                    def outputs(b):
                        for u in range(4):
                            m = 4 * b + u
                            a.wait_ge(q.o_psum, 8 + m + 1)
                            a.activation(oT[:, u, S * b:S * b + S], P[6 + m % 2][:, 0:256], ACT.Copy).then_inc(q.oT_ready, 1)

                    def exponents(j):
                        a.wait_ge(q.L2_ready, j + 1)
                        a.activation(L2[:, j % 3, :, :], L2[:, j % 3, :, :], ACT.Exp).then_inc(q.exp_ready, 1)

                    def by_key(j):
                        for u in range(4):
                            n = 4 * j + u
                            a.wait_ge(q.pt_psum, n + 1)
                            a.activation(PT[:, j // 2, 4 * u:4 * u + 4, 128 * (j % 2):128 * (j % 2) + 128],
                                         P[4 + n % 2][0:S2, :].rearrange("p (h t) -> p h t", h=4), ACT.Copy).then_inc(q.PT_ready, 1)

                    keep_columns(0, 1)
                    exponents(0)
                    by_key(0)
                    keep_norm(1)
                    exponents(1)
                    by_key(1)
                    keep_queries(1)
                    outputs(0)
                    exponents(2)
                    by_key(2)
                    keep_columns(1, 0)
                    exponents(3)
                    by_key(3)
                    norm0.scalar(a, q, N1, P[4:6], hT0)
                    outputs(1)
                    keep_columns(1, 1)

                @block.vector
                def _(v):
                    def divide(n, b, eps):
                        for j in (2 * b, 2 * b + 1):
                            v.wait_ge(q.tok_psum, NT * n + j + 1)
                            o = P[6 + j % 2][:, :].rearrange("p (h d) -> p h d", d=32)
                            v.tensor_scalar(den[:, j, :], o[:, :, HD], eps, None, ALU.add).then_inc(q.den_ready, 1)
                            v.wait_ge(q.den_ready, NT * n + j + 1)
                            v.reciprocal(rden[:, j, :], den[:, j, :]).then_inc(q.rden_ready, 1)
                            v.wait_ge(q.rden_ready, NT * n + j + 1)
                            v.tensor_tensor(at[:, j, :].rearrange("p (h d) -> p h d", d=HD), o[:, :, 0:HD],
                                            bcast(rden[:, j, :], 2, HD), ALU.mult).then_inc(q.at_ready, 1)

                    def add_stream(n, b, out, stream, done):
                        v.wait_ge(q.proj_psum, NB * n + b + 1)
                        v.tensor_tensor(out[:, 2 * b:2 * b + 2, :], P[7][:, :].rearrange("p (j n) -> p j n", j=2),
                                        stream[:, 2 * b:2 * b + 2, :], ALU.add).then_inc(done, 1)

                    def norm_moments(b):
                        v.wait_ge(q.x1_ready, b + 1)
                        norm.moments(v, q, x1, N1 + b, range(2 * b, 2 * b + 2), NT * N1 + 2 * b)

                    for e, e_ready, e_min, e_pos, pos_ready, bank in ((ek, q.ek_ready, q.ek_min, pk, q.pk_ready, 0),
                                                                      (eq, q.eq_ready, q.eq_min, pq, q.pq_ready, 2)):
                        for m in range(2):
                            v.wait_ge(e_ready, m + 1)
                            v.tensor_scalar(e[:, m, :], e[:, m, :], 1.0, None, ALU.min).then_inc(e_min, 1)
                            v.wait_ge(e_min, m + 1)
                            v.scalar_tensor_tensor(e_pos[:, m, :], P[bank + m][:, :], 0.0, e[:, m, :], ALU.max, ALU.add).then_inc(pos_ready, 1)
                    v.wait_ge(q.pk_ready, 1)
                    v.tensor_tensor(kbd[:, 0, 0, :, :], bcast(pk[:, 0, 0:S], 1, 8), bcast(headsel[:, :], 2, S), ALU.mult).then_inc(q.kbd_ready, 1)
                    if not first:
                        norm2.moments(v, q, x2, 0)
                    for n in range(NB * H):
                        if n == 3 and not first:
                            norm2.scale(v, q, x2, 0)
                        v.wait_ge(q.s_psum, n + 1)
                        if n >= 8:
                            v.wait_ge(q.o_psum, n // 4 - 1)
                        v.tensor_tensor(A[:, n % 8, :], P[n % 4][:, 0:384], causal[:, :], ALU.mult).then_inc(q.A_ready, 1)
                        if not first:
                            if n == 6:
                                router_choose(v)
                            if n == 9:
                                router_weights(v)
                            if n == 13:
                                router_place(v)
                        if n == 20:
                            divide(0, 0, DEN_EPS)
                        if n == 25:
                            v.wait_ge(q.xb_ready, NT)
                            add_stream(0, 0, x1, xin, q.x1_ready)
                        if n == 26:
                            norm_moments(0)
                        if n == 28:
                            norm.scale(v, q, x1, N1, range(0, 2))
                    def masked(j):
                        for u in range(4):
                            n = 4 * j + u
                            v.wait_ge(q.l_psum, n + 1)
                            if u == 0 and j >= 3:
                                v.wait_ge(q.L2_ready, j - 2)
                            v.tensor_tensor(L[:, j % 3, 4 * u:4 * u + 4, :], P[n % 4][:, 0:308].rearrange("p (h k) -> p h k", h=4),
                                            bcast(amask[:, j, :], 1, 4), ALU.add).then_inc(q.L_ready, 1)
                        v.wait_ge(q.L_ready, 4 * j + 4)
                        v.tensor_reduce(Lm[:, j, :], L[:, j % 3, :, :], AX.X, ALU.max).then_inc(q.Lm_ready, 1)

                    masked(0)
                    divide(0, 1, DEN_EPS)
                    masked(1)
                    add_stream(0, 1, x1, xin, q.x1_ready)
                    norm_moments(1)
                    norm.scale(v, q, x1, N1 + 1, range(2, 4))
                    masked(2)
                    masked(3)
                    divide(1, 0, 0.0)
                    v.wait_ge(q.next_in, 16)
                    norm0.vector(v, q, xin, N1 + 2, range(NT), NT * (N1 + 1))
                    if not first:
                        v.wait_ge(q.x2_stored, 16)
                    add_stream(1, 0, x2, x1, q.x2_ready)
                    divide(1, 1, 0.0)
                    add_stream(1, 1, x2, x1, q.x2_ready)
            clear(nc, q)

        group(0, True)
        with nc.Fori(1, NG) as i:
            group(i, False)

        with nc.Block() as block:
            @block.vector
            def _(v):
                norm2.vector(v, q, x2, 0)
                router_choose(v)
                router_weights(v)
                router_place(v)

            @block.tensor
            def _(p):
                norm2.tensor(p, q, 0, P[0:2], ident)
                p.wait_ge(q.hT_ready, 2)
                router_logits(p)
                router_rank(p)

            @block.scalar
            def _(a):
                norm2.scalar(a, q, 0, P[0:2], hT)
                router_scalar(a)

            @block.gpsimd
            def _(g):
                norm2.gpsimd(g, q, 0)
                router_scatter(g)
                g.wait_ge(scattered, 16 * TOPK * NT * NG)

            @block.sync
            def _(s):
                s.dma_start(y_rows[NG - 1], x2[:, :, :]).then_inc(q.x2_stored, 16)
                router_store(s, NG - 1)
                s.wait_ge(q.x2_stored, 16)
                s.wait_ge(q.stored, 32)
        clear(nc, q)


def experts(nc, ctx, c, io, dr):
    st = ExitStack()
    with st:
        def sb(name, shape, dt=F32):
            return st.enter_context(nc.sbuf_tensor("b_" + name, shape, dt))
        P = c.banks
        ident = c.ident[:, :]
        RT = CAP // 128
        HC = CAP // 2
        w1 = [sb(f"w1_{k}", [128, 2, FF0]) for k in range(2)]
        w2 = [sb(f"w2_{k}", [128, 4, D]) for k in range(2)]
        X = [sb(f"X_{k}", [128, RT, D]) for k in range(2)]
        XT = [sb(f"XT_{k}", [128, 2, CAP]) for k in range(2)]
        G = sb("G", [128, 4, CAP])
        Y = [sb(f"Y_{k}", [128, RT, D]) for k in range(2)]
        NE = 4
        W = [sb(f"w_rows_{k}", [128, FF1 * D // 128 // BLK, BLK]) for k in range(3)]
        Wi = sb("w_int", [128, FF1 * D // 128 // BLK, BLK], I16)
        wa = sb("w_amax", [128, FF1 * D // 128 // BLK])
        wi = sb("w_inv", [128, FF1 * D // 128 // BLK])
        WT = [w[:, :, :].rearrange("p c n -> p (c n)") for w in (c.wuT, c.wgT, c.wdT)]
        w1_d = io["L0_ffn_w1"].rearrange("e (c p) f -> e p c f", p=128)
        w2_d = io["L0_ffn_w2"].rearrange("e (c p) d -> e p c d", p=128)
        in_d = dr["slots_in"].rearrange("(e j p) d -> e p j d", p=128, j=RT)
        out_d = dr["slots_out"].rearrange("(e j p) d -> e p j d", p=128, j=RT)

        def load(s, e, k, done):
            s.dma_start(w1[k][:, :, :], w1_d[e]).then_inc(done, 16)
            s.dma_start(w2[k][:, :, :], w2_d[e]).then_inc(done, 16)
            s.dma_start(X[k][:, :, :], in_d[e]).then_inc(done, 16)

        with ExitStack() as once:
            q = signals(nc, once, "b_first")
            with nc.Block() as block:
                @block.sync
                def _(s):
                    load(s, 0, 0, q.b_first)
                    s.wait_ge(q.b_first, 48)
            clear(nc, q)

        q = signals(nc, st, "b_in1 b_in2 b_in3 b_in4 xT_psum xT_ready g_psum g_ready y_psum y_ready b_out0 b_out1 b_out2 b_out3 "
                            "w_in w_steps wt_psum wt_ready")
        arrived = (None, q.b_in1, q.b_in2, q.b_in3, q.b_in4)
        left = (q.b_out1, q.b_out2, q.b_out3)

        def turn(e0, first):
            with nc.Block() as block:
                @block.sync
                def _(s):
                    load(s, e0 + 1, 1, arrived[1])
                    if first:
                        for k, (name, r) in enumerate((("L1_ffn_w_up", FC), ("L1_ffn_w_gate", FC), ("L1_ffn_w_down", D // 128))):
                            s.dma_start(W[k][:, :, :].rearrange("p a b -> p (a b)").rearrange("p (r n) -> p r n", r=r),
                                        io[name].rearrange("(r p) n -> p r n", p=128)).then_inc(q.w_in, 16)
                    if not first:
                        s.dma_start(out_d[e0 - 1], Y[1][:, :, :]).then_inc(q.b_out0, 16)
                    for k in range(NE):
                        s.wait_ge(q.y_ready, RT * (k + 1))
                        if k + 2 <= NE:
                            load(s, (e0 + k + 2) % E, k % 2, arrived[k + 2])
                        if k < NE - 1:
                            s.dma_start(out_d[e0 + k], Y[k % 2][:, :, :]).then_inc(left[k], 16)
                    for k in range(1, NE + 1):
                        s.wait_ge(arrived[k], 48)
                    for k in range(NE - 1):
                        s.wait_ge(left[k], 16)
                    if not first:
                        s.wait_ge(q.b_out0, 16)

                @block.tensor
                def _(p):
                    def by_width(k):
                        if k:
                            p.wait_ge(arrived[k], 48)
                        if first and k >= 2:
                            p.wait_ge(q.wt_ready, 3 * (k - 1))
                        for j in range(RT):
                            if j >= 2 or k:
                                p.wait_ge(q.xT_ready, RT * k + j - 1)
                            for u in range(2):
                                t = p.transpose(P[j % 2][:, 128 * u:128 * u + 128], X[k % 2][:, j, 128 * u:128 * u + 128], ident)
                            t.then_inc(q.xT_psum, 1)

                    def weight_turned(k):
                        w = W[k][:, :, :].rearrange("p a b -> p (a b)")
                        nr = FC if k < 2 else D // 128
                        ncol = 2 * FC // nr
                        p.wait_ge(q.w_steps, 6 * (k + 1))
                        p.wait_ge(q.xT_ready, RT * (k + 2))
                        for n in range(2 * FC):
                            col, r = n // nr, n % nr
                            if n == 8:
                                p.wait_ge(q.wt_ready, 3 * k + 1)
                            t = p.transpose(P[(n // 4) % 2][:, 128 * (n % 4):128 * (n % 4) + 128],
                                            w[:, 128 * (ncol * r + col):128 * (ncol * r + col) + 128], ident)
                            if n % 4 == 3:
                                t.then_inc(q.wt_psum, 1)

                    by_width(0)
                    for k in range(NE):
                        p.wait_ge(q.xT_ready, RT * (k + 1))
                        for n in range(8):
                            f, m = n // 2, n % 2
                            if n >= 2 or k:
                                p.wait_ge(q.g_ready, 8 * k + n - 1)
                            for u in range(2):
                                t = p.matmul(P[2 + n % 2][:, 0:HC], w1[k % 2][:, u, 128 * f:128 * f + 128], XT[k % 2][:, u, HC * m:HC * m + HC],
                                             start=(u == 0), stop=(u == 1))
                            t.then_inc(q.g_psum, 1)
                        if k + 1 < NE:
                            by_width(k + 1)
                        p.wait_ge(q.g_ready, 8 * (k + 1))
                        for j in range(RT):
                            n = RT * k + j
                            if n >= 4:
                                p.wait_ge(q.y_ready, n - 3)
                            for f in range(4):
                                t = p.matmul(P[4 + n % 4][:, 0:D], G[:, f, 128 * j:128 * j + 128], w2[k % 2][:, f, :], start=(f == 0), stop=(f == 3))
                            t.then_inc(q.y_psum, 1)
                        if first and k < 3:
                            weight_turned(k)

                @block.scalar
                def _(a):
                    for k in range(NE):
                        for n in range(8):
                            f, m = n // 2, n % 2
                            a.wait_ge(q.g_psum, 8 * k + n + 1)
                            if k and n == 0:
                                a.wait_ge(q.y_psum, RT * k)
                            a.activation(G[:, f, HC * m:HC * m + HC], P[2 + n % 2][:, 0:HC], ACT.Gelu).then_inc(q.g_ready, 1)
                        if first and k < 3:
                            for m in range(3):
                                a.wait_ge(q.wt_psum, 3 * k + m + 1)
                                a.activation(WT[k][:, 512 * m:512 * m + 512], P[m % 2][:, :], ACT.Copy).then_inc(q.wt_ready, 1)

                @block.vector
                def _(v):
                    def keep_width(k):
                        for j in range(RT):
                            v.wait_ge(q.xT_psum, RT * k + j + 1)
                            if k >= 2 and j == 0:
                                v.wait_ge(q.g_psum, 8 * (k - 1))
                            v.tensor_copy(XT[k % 2][:, :, 128 * j:128 * j + 128],
                                          P[j % 2][:, 0:256].rearrange("p (c t) -> p c t", c=2)).then_inc(q.xT_ready, 1)

                    def quantise_weight(k):
                        n = [6 * k]

                        def step(ins):
                            ins.then_inc(q.w_steps, 1)
                            n[0] += 1
                            v.wait_ge(q.w_steps, n[0])

                        v.wait_ge(q.w_in, 48)
                        step(v.tensor_reduce(wa[:, :], W[k][:, :, :], AX.X, ALU.max, apply_absolute_value=True))
                        step(v.tensor_scalar(wa[:, :], wa[:, :], 1.0 / WMAX, 1e-12, ALU.mult, ALU.max))
                        step(v.reciprocal(wi[:, :], wa[:, :]))
                        step(v.tensor_tensor(Wi[:, :, :], W[k][:, :, :], bcast(wi[:, :], 2, BLK), ALU.mult))
                        step(v.tensor_scalar(Wi[:, :, :], Wi[:, :, :], WMAX, -WMAX - 1.0, ALU.min, ALU.max))
                        step(v.tensor_tensor(W[k][:, :, :], Wi[:, :, :], bcast(wa[:, :], 2, BLK), ALU.mult))

                    keep_width(0)
                    for k in range(NE):
                        if k + 1 < NE:
                            keep_width(k + 1)
                        if first and k < 3:
                            quantise_weight(k)
                        for j in range(RT):
                            n = RT * k + j
                            v.wait_ge(q.y_psum, n + 1)
                            if j == 0 and k >= 2:
                                v.wait_ge(left[k - 2], 16)
                            if j == 0 and k == 1 and not first:
                                v.wait_ge(q.b_out0, 16)
                            v.tensor_copy(Y[k % 2][:, j, :], P[4 + n % 4][:, 0:D]).then_inc(q.y_ready, 1)
            clear(nc, q)

        turn(0, True)
        with nc.Fori(1, E // NE) as i:
            turn(NE * i, False)
        with nc.Block() as block:
            @block.sync
            def _(s):
                s.dma_start(out_d[E - 1], Y[1][:, :, :]).then_inc(q.b_out0, 16)
                s.wait_ge(q.b_out0, 16)
        clear(nc, q)


def layer1(nc, ctx, c, io, dr):
    st = ExitStack()
    with st:
        def sb(name, shape, dt=F32):
            return st.enter_context(nc.sbuf_tensor("c_" + name, shape, dt))
        P = c.banks
        ident = c.ident[:, :]
        HW = H1 * HD1
        NP = H1 // 2
        wq = sb("wq", [128, 2, HW])
        wdn = sb("wdn", [128, 2, LR])
        wku = sb("wku", [128, HW])
        wvu = sb("wvu", [128, HW])
        wo = sb("wo", [128, NP, D])
        xwq, xwk, xwv, xwo = (sb(n, [128, 2, D]) for n in ("xwq", "xwk", "xwv", "xwo"))
        bq, bqs, bk = (sb(n, [128, 2]) for n in ("bq", "bqs", "bk"))
        bv = sb("bv", [128, D])
        bo = sb("bo", [128, D])
        imask = sb("imask", [128, NB, S2], I32)
        keep = sb("keep", [128, NB, S2])
        pen = sb("pen", [128, NB, S2])

        norm0, norm, norm2 = Norm(nc, st, "c0"), Norm(nc, st, "c1"), Norm(nc, st, "c2")
        slot = sb("slot", [128, TOPK * NT], I32)
        wt = sb("wt", [128, TOPK * NT])
        rows = sb("rows", [128, TOPK, NT, D])
        arrived = sb("arrived", [128, 1])
        xin = sb("xin", [128, NT, D])
        x3 = sb("x3", [128, NT, D])
        x4 = sb("x4", [128, NT, D])
        x5 = sb("x5", [128, NT, D])
        hT0 = sb("hT0", [128, 2, T])
        hT = sb("hT", [128, 2, T])
        qT = sb("qT", [128, NP, T])
        latT = sb("latT", [128, T])
        kz = sb("kz", [128, H1, T])
        vs = sb("vs", [128, NT, HW])
        nmax = sb("nmax", [128, NB * H1, 2])
        sums = sb("sums", [128, NB * H1, 2])
        rsum = sb("rsum", [128, NB * H1, 2])
        pr = sb("pr", [128, 4, 2, S])
        PT = sb("PT", [128, 4, 2, S])
        aT = sb("aT", [128, NP, T])
        ctxT = sb("ctxT", [128, 2, NB, S2])
        xqT = sb("xqT", [128, 2, T])
        xkT = sb("xkT", [128, 2, NB, S2])
        xv = sb("xv", [S2, NB, D])
        L = sb("L", [128, NT, S2])
        xm = sb("xm", [128, NT])
        xs = sb("xs", [128, NT])
        xr = sb("xr", [128, NT])
        xPT = sb("xPT", [S2, T])
        xaT = sb("xaT", [128, 2, T])
        amax = sb("amax", [128, 1])

        weights = ((wq[:, :, :], io["L1_attn_Wq"].rearrange("(c p) n -> p c n", p=128)),
                   (wdn[:, :, :], io["L1_attn_Wkv_down"].rearrange("(c p) n -> p c n", p=128)),
                   (wo[:, :, :], io["L1_attn_Wo"].rearrange("(c p) n -> p c n", p=128)),
                   (xwq[:, :, :], io["L1_xattn_Wq"].rearrange("(c p) n -> p c n", p=128)),
                   (xwk[:, :, :], io["L1_xattn_Wk"].rearrange("(c p) n -> p c n", p=128)),
                   (xwv[:, :, :], io["L1_xattn_Wv"].rearrange("(c p) n -> p c n", p=128)),
                   (xwo[:, :, :], io["L1_xattn_Wo"].rearrange("(c p) n -> p c n", p=128)),
                   (wku[0:LR, :], io["L1_attn_Wk_up"]),
                   (wvu[0:LR, :], io["L1_attn_Wv_up"]),
                   (bv[:, :], io["L1_xattn_bv"].unsqueeze(0).broadcast_to([128, D])),
                   (bo[:, :], io["L1_xattn_bo"].unsqueeze(0).broadcast_to([128, D])),
                   (imask[:, :, :], io["mask_SxS2_ik0"].rearrange("(j p) k -> p j k", p=128)))
        NLOAD = len(weights) + 4

        def load_weights(s):
            for dst, src in weights:
                s.dma_start(dst, src).then_inc(loads.c_w, 16)
            for dst, src in ((bq, io["L1_xattn_bq"]), (bk, io["L1_xattn_bk"])):
                for u in range(2):
                    s.dma_start(dst[:, u:u + 1], src[128 * u:128 * u + 128].unsqueeze(1)).then_inc(loads.c_w, 16)

        def constants(v):
            v.memset(wku[LR:128, :], 0.0)
            v.memset(wvu[LR:128, :], 0.0)
            v.memset(latT[LR:128, :], 0.0)
            v.memset(kz[:, :, :], 0.0)
            v.memset(c.amax[:, :], 0.0)

        def masks(v):
            v.wait_ge(loads.c_w, 16 * NLOAD)
            v.tensor_scalar(bqs[:, :], bq[:, :], HD ** -0.5, None, ALU.mult)
            v.tensor_scalar(keep[:, :, :], imask[:, :, :], 0.0, None, ALU.not_equal).then_inc(loads.c_dve, 1)
            v.wait_ge(loads.c_dve, 4)
            v.tensor_scalar(pen[:, :, :], keep[:, :, :], 1.0, 1e9, ALU.subtract, ALU.mult)

        q = signals(nc, st, "r_in x_in ctx_in rows_in mixed ln_stats ln_moments ln_var ln_rstd ln_h hT_psum hT_ready q_psum qT_ready "
                         "lat_ready k_psum kz_ready v_psum v_ready s_psum nmax_ready exp_ready rsum_ready pr_ready pt_psum PT_ready "
                         "a_psum aT_ready proj_psum x4_ready xb_ready xk_psum xv_psum xk_ready xv_ready xq_psum xq_ready l_psum "
                         "L_kept L_ready xm_ready xe_ready xr_ready xp_ready xpt_psum xPT_ready xa_psum xaT_ready xproj_psum "
                         "x5_ready amax_part amax_ready stored")
        gathered = c.gathered
        x5_rows = dr["x_c"].rearrange("(i j p) n -> i p j n", p=128, j=NT)
        NH = NB * H1
        SB = (0, 1, 6, 7)
        QB = (4, 5, 2, 3)

        def fetch(s, i):
            s.dma_start(slot[:, :], dr["slot_g"][i]).then_inc(q.r_in, 16)
            s.dma_start(wt[:, :], dr["wt"][i]).then_inc(q.x_in, 16)
            s.dma_start(xin[:, :, :], dr["x_a"].rearrange("(i j p) n -> i p j n", p=128, j=NT)[i]).then_inc(q.x_in, 16)

        def gather(g):
            g.wait_ge(q.r_in, 16)
            for k in range(TOPK):
                for j in range(NT):
                    g.indirect_dma_start(out=rows[:, k, j, :], out_offset=None, in_=dr["slots_out"],
                                         in_offset=bass.IndirectOffsetOnAxis(ap=slot[:, NT * k + j:NT * k + j + 1], axis=0),
                                         bounds_check=SLOTS - 1, oob_is_err=False).then_inc(gathered, 16)

        def gathers_done(g, n):
            g.wait_ge(gathered, 16 * TOPK * NT * n)
            g.tensor_tensor(arrived[:, :], norm.power[:, 0:1], norm.power[:, 0:1], ALU.add).then_inc(q.rows_in, 1)

        def mix(v):
            v.wait_ge(q.x_in, 32)
            v.wait_ge(q.rows_in, 1)
            for j in range(NT):
                v.scalar_tensor_tensor(x3[:, j, :], rows[:, 0, j, :], wt[:, j:j + 1], xin[:, j, :], ALU.mult, ALU.add).then_inc(q.mixed, 1)
            v.wait_ge(q.mixed, NT)
            for j in range(NT):
                v.scalar_tensor_tensor(x3[:, j, :], rows[:, 1, j, :], wt[:, NT + j:NT + j + 1], x3[:, j, :], ALU.mult, ALU.add).then_inc(q.mixed, 1)
            v.wait_ge(q.mixed, 2 * NT)

        def last_norm(v):
            norm2.vector(v, q, x5, 0)
            v.wait_ge(q.ln_h, NT)
            v.tensor_reduce(amax[:, :], norm2.h[:, :, :].rearrange("p j n -> p (j n)"), AX.X, ALU.max, apply_absolute_value=True).then_inc(q.amax_part, 1)
            v.wait_ge(q.amax_part, 1)
            v.tensor_tensor(c.amax[:, :], c.amax[:, :], amax[:, :], ALU.max).then_inc(q.amax_ready, 1)

        def keep_input(a, i):
            a.wait_ge(q.hT_psum, 1)
            for u in range(2):
                a.activation(c.hT_all[:, u, bass.ts(i, T)], P[u][:, :], ACT.Copy).then_inc(q.hT_ready, 1)

        def ahead(p):
            for u in range(2):
                p.matmul(P[6][0:LR, :], wdn[:, u, :], hT0[:, u, :], start=(u == 0), stop=(u == 1))
            for m in range(2):
                for u in range(2):
                    p.matmul(P[QB[m]][:, :], wq[:, u, 128 * m:128 * m + 128], hT0[:, u, :], start=(u == 0), stop=(u == 1))

        loads = signals(nc, st, "c_w c_dve")
        with nc.Block() as block:
            @block.sync
            def _(s):
                fetch(s, 0)
                load_weights(s)
                s.wait_ge(loads.c_w, 16 * NLOAD)

            @block.gpsimd
            def _(g):
                for m in (norm0, norm, norm2):
                    g.memset(m.power[:, :], -0.5).then_inc(loads.c_dve, 1)
                gather(g)
                g.wait_ge(loads.c_dve, 3)
                gathers_done(g, 1)
                norm0.gpsimd(g, q, 0)

            @block.vector
            def _(v):
                constants(v)
                mix(v)
                norm0.vector(v, q, x3, 0)
                masks(v)

            @block.tensor
            def _(p):
                norm0.tensor(p, q, 0, P[4:6], ident)
                p.wait_ge(loads.c_w, 16 * NLOAD)
                p.wait_ge(q.hT_ready, 2)
                ahead(p)

            @block.scalar
            def _(a):
                norm0.scalar(a, q, 0, P[4:6], hT0)
        clear(nc, q)
        clear(nc, loads)

        def group(i, first):
            N1 = 0 if first else 1
            with nc.Block() as block:
                @block.sync
                def _(s):
                    fetch(s, (i + 1) % NG)
                    if not first:
                        s.dma_start(x5_rows[i - 1], x5[:, :, :]).then_inc(q.stored, 16)
                    for u in range(2):
                        s.dma_start(ctxT[:, u, :, :], io["ctxT"].rearrange("(i b) (c p) k -> i c p b k", b=NB, p=128)[i, u]).then_inc(q.ctx_in, 16)
                    s.wait_ge(q.x_in, 32)
                    if not first:
                        s.wait_ge(q.stored, 16)

                @block.gpsimd
                def _(g):
                    if not first:
                        norm2.gpsimd(g, q, 0)
                    gather(g)
                    for n in range(NH):
                        g.wait_ge(q.rsum_ready, n + 1)
                        for u in range(2):
                            g.tensor_scalar(pr[:, n % 4, u, :], pr[:, n % 4, u, :], rsum[:, n, u:u + 1], 1.0,
                                            ALU.mult, ALU.mult).then_inc(q.pr_ready, 1)
                    norm.gpsimd(g, q, N1, range(0, 2))
                    norm.gpsimd(g, q, N1 + 1, range(2, 4))
                    gathers_done(g, i + 2)
                    norm0.gpsimd(g, q, N1 + 2)
                    g.wait_ge(q.ln_h, NT * (N1 + 1))
                    for j in range(NT):
                        g.tensor_tensor(x4[:, j, :], x4[:, j, :], bo[:, :], ALU.add).then_inc(q.xb_ready, 1)

                @block.tensor
                def _(p):
                    for m in range(2, NP):
                        for u in range(2):
                            t = p.matmul(P[QB[m]][:, :], wq[:, u, 128 * m:128 * m + 128], hT0[:, u, :], start=(u == 0), stop=(u == 1))
                        t.then_inc(q.q_psum, 1)
                    if not first:
                        norm2.tensor(p, q, 0, P[0:2], ident)
                        p.wait_ge(q.hT_ready, 2)
                    p.wait_ge(q.lat_ready, 1)
                    for m in range(NP):
                        p.matmul(P[(7, 0, 1, 6)[m]][:, :], wku[:, 128 * m:128 * m + 128], latT[:, :], start=True, stop=True).then_inc(q.k_psum, 1)
                    for j in range(NT):
                        p.wait_ge(q.qT_ready, j + 1)
                        p.matmul(P[QB[j]][:, :], latT[:, 128 * j:128 * j + 128], wvu[:, :], start=True, stop=True).then_inc(q.v_psum, 1)
                    p.wait_ge(q.kz_ready, H1)

                    def scores(n):
                        b, h = n // H1, n % H1
                        if n >= 4:
                            p.wait_ge(q.exp_ready, 2 * (n - 3))
                        for u in range(2):
                            t = p.matmul(P[SB[n % 4]][:, S * u:S * u + S], qT[:, h // 2, S * b + 128 * u:S * b + 128 * u + 128],
                                         kz[:, h, S * b:S * b + S], start=True, stop=True)
                        t.then_inc(q.s_psum, 1)

                    def turn(n):
                        p.wait_ge(q.pr_ready, 2 * n + 2)
                        if n == 0:
                            p.wait_ge(q.v_ready, NT)
                        if n >= 2:
                            p.wait_ge(q.PT_ready, n - 1)
                        for k in range(2):
                            for u in range(2):
                                t = p.transpose(P[2 + n % 2][:, S * k + 128 * u:S * k + 128 * u + 128],
                                                pr[:, n % 4, u, 128 * k:128 * k + 128], ident)
                        t.then_inc(q.pt_psum, 1)

                    def values(m):
                        b, g = m // NP, m % NP
                        p.wait_ge(q.PT_ready, 2 * m + 2)
                        if m == 0:
                            p.wait_ge(q.v_ready, NT)
                        if m >= 2:
                            p.wait_ge(q.aT_ready, m - 1)
                        for k in range(2):
                            for e in range(2):
                                h = 2 * g + e
                                t = p.matmul(P[4 + m % 2][HD1 * e:HD1 * e + HD1, 0:S], vs[:, 2 * b + k, HD1 * h:HD1 * h + HD1],
                                             PT[:, (2 * m + e) % 4, k, :], start=(k == 0), stop=(k == 1),
                                             tile_position=(0, HD1 * e), skip_group_check=True)
                        t.then_inc(q.a_psum, 1)

                    def project(b):
                        p.wait_ge(q.aT_ready, NP * (b + 1))
                        for j in (2 * b, 2 * b + 1):
                            for m in range(NP):
                                t = p.matmul(P[6 + b][:, D * (j % 2):D * (j % 2) + D], aT[:, m, 128 * j:128 * j + 128], wo[:, m, :],
                                             start=(m == 0), stop=(m == NP - 1))
                        t.then_inc(q.proj_psum, 1)

                    for n in range(NH + 4):
                        if n < NH:
                            scores(n)
                        if 0 <= n - 3 < NH:
                            turn(n - 3)
                        if n == NH + 2:
                            p.wait_ge(q.exp_ready, 2 * (NH - 1))
                            project(0)
                        if n >= 5 and n % 2:
                            values((n - 5) // 2)
                    project(1)

                    p.wait_ge(q.ctx_in, 32)
                    p.wait_ge(q.PT_ready, NH)
                    for m in range(2):
                        for u in range(2):
                            t = p.matmul(P[2][:, 154 * m:154 * m + 154], xwk[:, u, 128 * m:128 * m + 128],
                                         ctxT[:, u, :, :].rearrange("p b k -> p (b k)"), start=(u == 0), stop=(u == 1))
                    t.then_inc(q.xk_psum, 1)
                    for b in range(NB):
                        for u in range(2):
                            t = p.matmul(P[3][0:S2, D * b:D * b + D], ctxT[:, u, b, :], xwv[:, u, :], start=(u == 0), stop=(u == 1))
                    t.then_inc(q.xv_psum, 1)
                    norm.tensor(p, q, N1, P[0:2], ident, NT * N1)
                    p.wait_ge(q.hT_ready, 2 * N1 + 2)
                    for m in range(2):
                        for u in range(2):
                            t = p.matmul(P[4 + m][:, :], xwq[:, u, 128 * m:128 * m + 128], hT[:, u, :], start=(u == 0), stop=(u == 1))
                        t.then_inc(q.xq_psum, 1)
                    p.wait_ge(q.xq_ready, 2)
                    p.wait_ge(q.xk_ready, 2)
                    for j in range(NT):
                        for u in range(2):
                            t = p.matmul(P[6][:, S2 * j:S2 * j + S2], xqT[:, u, 128 * j:128 * j + 128], xkT[:, u, j // 2, :],
                                         start=(u == 0), stop=(u == 1))
                    t.then_inc(q.l_psum, 1)
                    norm0.tensor(p, q, N1 + 1, P[4:6], ident, NT * (N1 + 1))
                    p.wait_ge(q.hT_ready, 2 * (N1 + 2))
                    p.wait_ge(q.L_kept, 1)
                    ahead(p)
                    for j in range(NT):
                        p.wait_ge(q.xp_ready, j + 1)
                        t = p.transpose(P[7][0:S2, 128 * j:128 * j + 128], L[:, j, :], ident)
                    t.then_inc(q.xpt_psum, 1)
                    p.wait_ge(q.xPT_ready, 1)
                    p.wait_ge(q.xv_ready, NB)
                    for u in range(2):
                        for b in range(NB):
                            t = p.matmul(P[u][:, S * b:S * b + S], xv[:, b, 128 * u:128 * u + 128], xPT[:, S * b:S * b + S], start=True, stop=True)
                        t.then_inc(q.xa_psum, 1)
                    p.wait_ge(q.xaT_ready, 2)
                    for j in range(NT):
                        for u in range(2):
                            t = p.matmul(P[2 + j // 2][:, D * (j % 2):D * (j % 2) + D], xaT[:, u, 128 * j:128 * j + 128], xwo[:, u, :],
                                         start=(u == 0), stop=(u == 1))
                        t.then_inc(q.xproj_psum, 1)

                @block.scalar
                def _(a):
                    a.activation(latT[0:LR, :], P[6][0:LR, :], ACT.Copy).then_inc(q.lat_ready, 1)
                    for m in range(NP):
                        if m >= 2:
                            a.wait_ge(q.q_psum, m - 1)
                        a.activation(qT[:, m, :], P[QB[m]][:, :], ACT.Copy, scale=HD1 ** -0.5).then_inc(q.qT_ready, 1)
                    if not first:
                        keep_input(a, i - 1)
                    for j in range(NT):
                        a.wait_ge(q.v_psum, j + 1)
                        a.activation(vs[:, j, :], P[QB[j]][:, :], ACT.Copy).then_inc(q.v_ready, 1)

                    def heads(m):
                        a.wait_ge(q.a_psum, m + 1)
                        a.activation(aT[:, m % NP, S * (m // NP):S * (m // NP) + S], P[4 + m % 2][:, 0:S], ACT.Copy).then_inc(q.aT_ready, 1)

                    for n in range(NH):
                        a.wait_ge(q.nmax_ready, n + 1)
                        if n >= 4:
                            a.wait_ge(q.pt_psum, n - 3)
                        for u in range(2):
                            a.activation(pr[:, n % 4, u, :], P[SB[n % 4]][:, S * u:S * u + S], ACT.Exp, bias=nmax[:, n, u:u + 1],
                                         accum_out=sums[:, n, u:u + 1]).then_inc(q.exp_ready, 1)
                        if n >= 7 and n % 2:
                            heads((n - 7) // 2)
                    heads(NH // 2 - 3)
                    heads(NH // 2 - 2)
                    heads(NH // 2 - 1)
                    a.wait_ge(q.xk_psum, 1)
                    for m in range(2):
                        a.activation(xkT[:, m, :, :].rearrange("p b k -> p (b k)"), P[2][:, 154 * m:154 * m + 154], ACT.Identity,
                                     bias=bk[:, m:m + 1]).then_inc(q.xk_ready, 1)
                    norm.scalar(a, q, N1, P[0:2], hT)
                    for m in range(2):
                        a.wait_ge(q.xq_psum, m + 1)
                        a.activation(xqT[:, m, :], P[4 + m][:, :], ACT.Identity, bias=bqs[:, m:m + 1], scale=HD ** -0.5).then_inc(q.xq_ready, 1)
                    norm0.scalar(a, q, N1 + 1, P[4:6], hT0)
                    a.wait_ge(q.xm_ready, 1)
                    for j in range(NT):
                        a.activation(L[:, j, :], L[:, j, :], ACT.Exp, bias=xm[:, j:j + 1], accum_out=xs[:, j:j + 1]).then_inc(q.xe_ready, 1)
                    a.wait_ge(q.xpt_psum, 1)
                    a.activation(xPT[:, :], P[7][0:S2, :], ACT.Copy).then_inc(q.xPT_ready, 1)
                    for u in range(2):
                        a.wait_ge(q.xa_psum, u + 1)
                        a.activation(xaT[:, u, :], P[u][:, :], ACT.Copy).then_inc(q.xaT_ready, 1)
                @block.vector
                def _(v):
                    if not first:
                        last_norm(v)
                    for m in range(NP):
                        v.wait_ge(q.k_psum, m + 1)
                        for e in range(2):
                            rows_ = slice(HD1 * e, HD1 * e + HD1)
                            v.tensor_copy(kz[rows_, 2 * m + e, :], P[(7, 0, 1, 6)[m]][rows_, :]).then_inc(q.kz_ready, 1)

                    def maxima(n):
                        v.wait_ge(q.s_psum, n + 1)
                        v.tensor_reduce(nmax[:, n, :], P[SB[n % 4]][:, :].rearrange("p (u k) -> p u k", u=2), AX.X, ALU.max,
                                        negate=True).then_inc(q.nmax_ready, 1)

                    def invert(n):
                        v.wait_ge(q.exp_ready, 2 * n + 2)
                        v.reciprocal(rsum[:, n, :], sums[:, n, :]).then_inc(q.rsum_ready, 1)

                    def by_key(n):
                        v.wait_ge(q.pt_psum, n + 1)
                        if n >= 4:
                            v.wait_ge(q.a_psum, n // 2 - 1)
                        v.tensor_copy(PT[:, n % 4, :, :].rearrange("p k t -> p (k t)"), P[2 + n % 2][:, :]).then_inc(q.PT_ready, 1)

                    for n in range(NH + 3):
                        if n < NH:
                            maxima(n)
                        if 0 <= n - 1 < NH:
                            invert(n - 1)
                        if n >= 3:
                            by_key(n - 3)
                    for b in range(NB):
                        own = slice(2 * b, 2 * b + 2)
                        v.wait_ge(q.proj_psum, b + 1)
                        v.tensor_tensor(x4[:, own, :], P[6 + b][:, :].rearrange("p (j n) -> p j n", j=2), x3[:, own, :], ALU.add).then_inc(q.x4_ready, 1)
                        v.wait_ge(q.x4_ready, b + 1)
                        norm.moments(v, q, x4, N1 + b, range(2 * b, 2 * b + 2), NT * N1 + 2 * b)
                        norm.scale(v, q, x4, N1 + b, range(2 * b, 2 * b + 2))
                    v.wait_ge(q.xv_psum, 1)
                    for b in range(NB):
                        v.tensor_tensor(xv[:, b, :], P[3][0:S2, D * b:D * b + D], bv[0:S2, :], ALU.add).then_inc(q.xv_ready, 1)
                    mix(v)
                    norm0.vector(v, q, x3, N1 + 2, range(NT), NT * (N1 + 1))
                    v.wait_ge(q.l_psum, 1)
                    l = P[6][:, 0:NT * S2].rearrange("p (b r k) -> p b r k", b=NB, r=NB)
                    l3 = L[:, :, :].rearrange("p (b r) k -> p b r k", b=NB)
                    v.tensor_tensor(l3, l, bcast(keep[:, :, :], 1, NB), ALU.mult).then_inc(q.L_kept, 1)
                    v.wait_ge(q.L_kept, 1)
                    v.tensor_tensor(l3, l3, bcast(pen[:, :, :], 1, NB), ALU.add).then_inc(q.L_ready, 1)
                    v.wait_ge(q.L_ready, 1)
                    v.tensor_reduce(xm[:, :], L[:, :, :], AX.X, ALU.max, negate=True).then_inc(q.xm_ready, 1)
                    v.wait_ge(q.xe_ready, NT)
                    v.reciprocal(xr[:, :], xs[:, :]).then_inc(q.xr_ready, 1)
                    v.wait_ge(q.xr_ready, 1)
                    for j in range(NT):
                        v.tensor_scalar(L[:, j, :], L[:, j, :], xr[:, j:j + 1], None, ALU.mult).then_inc(q.xp_ready, 1)
                    v.wait_ge(q.xb_ready, NT)
                    if not first:
                        v.wait_ge(q.stored, 16)
                    for j in range(NT):
                        v.wait_ge(q.xproj_psum, 2 * (j // 2) + 2)
                        v.tensor_tensor(x5[:, j, :], P[2 + j // 2][:, D * (j % 2):D * (j % 2) + D], x4[:, j, :], ALU.add).then_inc(q.x5_ready, 1)
            clear(nc, q)

        group(0, True)
        with nc.Fori(1, NG) as i:
            group(i, False)

        with nc.Block() as block:
            @block.sync
            def _(s):
                s.dma_start(x5_rows[NG - 1], x5[:, :, :]).then_inc(q.stored, 16)
                s.wait_ge(q.stored, 16)

            @block.vector
            def _(v):
                last_norm(v)

            @block.gpsimd
            def _(g):
                norm2.gpsimd(g, q, 0)

            @block.tensor
            def _(p):
                norm2.tensor(p, q, 0, P[0:2], ident)

            @block.scalar
            def _(a):
                keep_input(a, NG - 1)
        clear(nc, q)


def feed_forward(nc, ctx, c, io, dr, out):
    st = ExitStack()
    with st:
        def sb(name, shape, dt=F32):
            return st.enter_context(nc.sbuf_tensor("d_" + name, shape, dt))
        P = c.banks
        ident = c.ident[:, :]
        NTOK = B * S
        wuT, wgT, wdT = c.wuT, c.wgT, c.wdT
        raw = sb("raw", [128, FC, NTOK])
        mx = sb("mx", [128, 1])
        gmx = sb("gmx", [128, 1])
        cur = sb("cur", [128, 4 * FC])
        cur1 = sb("cur1", [128, 1])
        scale = {k: sb("scale_" + k, [128, 1]) for k in "xugao"}
        inv = {k: sb("inv_" + k, [128, 1]) for k in "xugao"}
        unit = {k: sb("unit_" + k, [128, 1]) for k in "ao"}


        def make_scale(k, src, unit=None, factors=None):
            with ExitStack() as once:
                q = signals(nc, once, "all_max scale_steps")
                with nc.Block() as block:
                    @block.gpsimd
                    def _(g):
                        g.partition_all_reduce(gmx[:, :], src[:, :], 128, RMAX).then_inc(q.all_max, 1)

                    @block.vector
                    def _(v):
                        n = [0]

                        def step(ins):
                            ins.then_inc(q.scale_steps, 1)
                            n[0] += 1
                            v.wait_ge(q.scale_steps, n[0])

                        if unit is not None:
                            step(v.tensor_scalar(unit[:, :], factors[0], factors[1], None, ALU.mult))
                        v.wait_ge(q.all_max, 1)
                        if unit is not None:
                            step(v.tensor_scalar(gmx[:, :], gmx[:, :], unit[:, :], None, ALU.mult))
                        step(v.tensor_scalar(scale[k][:, :], gmx[:, :], 1.0 / QMAX, 1e-12, ALU.mult, ALU.max))
                        step(v.reciprocal(inv[k][:, :], scale[k][:, :]))
                        if unit is not None:
                            step(v.tensor_scalar(inv[k][:, :], inv[k][:, :], unit[:, :], None, ALU.mult))
                        v.memset(mx[:, :], 0.0)
                clear(nc, q)

        def quantise_input():
            with ExitStack() as once:
                q = signals(nc, once, "xi_ready xq_ready")
                xi = raw[:, 0:1, :].bitcast(I16)
                with nc.Block() as block:
                    @block.scalar
                    def _(a):
                        part = xi[:, 0, 0:NTOK]
                        a.activation(part, c.hT_all[:, 0, :], ACT.Copy, scale=inv["x"][:, :]).then_inc(q.xi_ready, 1)
                        a.wait_ge(q.xi_ready, 1)
                        a.activation(c.hT_all[:, 0, :], part, ACT.Copy, scale=scale["x"][:, :])

                    @block.vector
                    def _(v):
                        part = xi[:, 0, NTOK:2 * NTOK]
                        v.tensor_scalar(part, c.hT_all[:, 1, :], inv["x"][:, :], None, ALU.mult).then_inc(q.xq_ready, 1)
                        v.wait_ge(q.xq_ready, 1)
                        v.tensor_scalar(c.hT_all[:, 1, :], part, scale["x"][:, :], None, ALU.mult)
                clear(nc, q)

        def project(tag, wT, up):
            with ExitStack() as once:
                q = signals(nc, once, f"up_ready_{tag} r_psum_{tag} raw_ready_{tag} cur_ready_{tag} cur1_ready_{tag} mx_ready_{tag}")
                up_ready, r_psum, raw_ready, cur_ready, cur1_ready, mx_ready = q
                K = 4
                N = K * FC
                with nc.Fori(0, NG // K) as i:
                    with nc.Block() as block:
                        @block.vector
                        def _(v):
                            def keep_up(k):
                                at = bass.ts(K * i + k, T)
                                v.tensor_scalar(up[:, :, at], raw[:, :, at], inv["u"][:, :], None, ALU.mult).then_inc(up_ready, 1)

                            if up is not None:
                                keep_up(0)
                            for n in range(N):
                                if up is not None and n % FC == 1 and n // FC + 1 < K:
                                    keep_up(n // FC + 1)
                                v.wait_ge(raw_ready, n + 1)
                                v.tensor_reduce(cur[:, n:n + 1], P[n % 8][:, :], AX.X, ALU.max, apply_absolute_value=True).then_inc(cur_ready, 1)
                            v.wait_ge(cur_ready, N)
                            v.tensor_reduce(cur1[:, :], cur[:, :], AX.X, ALU.max).then_inc(cur1_ready, 1)
                            v.wait_ge(cur1_ready, 1)
                            v.tensor_tensor(mx[:, :], mx[:, :], cur1[:, :], ALU.max).then_inc(mx_ready, 1)

                        @block.tensor
                        def _(p):
                            for n in range(N):
                                k, f = n // FC, n % FC
                                if n >= 8:
                                    p.wait_ge(cur_ready, n - 7)
                                for u in range(2):
                                    t = p.matmul(P[n % 8][:, :], wT[:, u, 128 * f:128 * f + 128], c.hT_all[:, u, bass.ts(K * i + k, T)],
                                                 start=(u == 0), stop=(u == 1))
                                t.then_inc(r_psum, 1)

                        @block.scalar
                        def _(a):
                            for n in range(N):
                                k, f = n // FC, n % FC
                                if up is not None and f == 0:
                                    a.wait_ge(up_ready, k + 1)
                                a.wait_ge(r_psum, n + 1)
                                a.activation(raw[:, f, bass.ts(K * i + k, T)], P[n % 8][:, :], ACT.Copy).then_inc(raw_ready, 1)
                    clear(nc, q)

        TP = T // 2
        NPC = 8

        def carve(tiles, width):
            room = c.hT_all[:, :, :].rearrange("p c t -> p (c t)")
            at, out = 0, {}
            for k, dt in tiles:
                words = FC * width // (1 if dt == F32 else 2)
                part = room[:, at:at + words]
                out[k] = (part if dt == F32 else part.bitcast(dt)).rearrange("p (f t) -> p f t", f=FC)
                at += words
            assert at <= 2 * B * S
            return out

        def magnitude(v, n, r, part, total, done):
            v.tensor_reduce(cur[:, n:n + 1], r, AX.XY, ALU.max, apply_absolute_value=True).then_inc(part, 1)
            if n == NPC - 1:
                v.wait_ge(part, NPC)
                v.tensor_reduce(cur1[:, :], cur[:, 0:NPC], AX.X, ALU.max).then_inc(total, 1)
                v.wait_ge(total, 1)
                v.tensor_tensor(mx[:, :], mx[:, :], cur1[:, :], ALU.max).then_inc(done, 1)

        make_scale("x", c.amax)
        quantise_input()
        project("up", wuT, None)
        make_scale("u", mx)
        up = sb("up", [128, FC, NTOK], I16)
        project("gate", wgT, up)
        make_scale("g", mx)

        with ExitStack() as once:
            q = signals(nc, once, "gi_ready sig_ready sq_ready act_ready g_part g_total g_done")
            tl = carve([(n + str(k), dt) for k in range(2) for n, dt in (("sig", F32), ("gi", I16), ("sq", U16))], TP)
            with nc.Fori(0, NTOK // (TP * NPC)) as i:
                with nc.Block() as block:
                    @block.vector
                    def _(v):
                        def whole(n):
                            v.wait_ge(q.act_ready, n + 1)
                            magnitude(v, n, raw[:, :, bass.ts(NPC * i + n, TP)], q.g_part, q.g_total, q.g_done)

                        for n in range(NPC):
                            k, r = n % 2, raw[:, :, bass.ts(NPC * i + n, TP)]
                            v.wait_ge(q.sig_ready, n + 1)
                            v.tensor_scalar(tl[f"sq{k}"], tl[f"sig{k}"], 65536.0, None, ALU.mult).then_inc(q.sq_ready, 1)
                            v.wait_ge(q.sq_ready, n + 1)
                            v.tensor_tensor(r, tl[f"sq{k}"][:, :, :], tl[f"gi{k}"][:, :, :], ALU.mult).then_inc(q.act_ready, 1)
                            if n:
                                whole(n - 1)
                        whole(NPC - 1)

                    @block.scalar
                    def _(a):
                        for n in range(NPC):
                            k, r = n % 2, raw[:, :, bass.ts(NPC * i + n, TP)]
                            if n >= 2:
                                a.wait_ge(q.act_ready, n - 1)
                            a.activation(tl[f"gi{k}"], r, ACT.Copy, scale=inv["g"][:, :]).then_inc(q.gi_ready, 1)
                            a.wait_ge(q.gi_ready, n + 1)
                            a.activation(tl[f"sig{k}"], tl[f"gi{k}"], ACT.Sigmoid, scale=scale["g"][:, :]).then_inc(q.sig_ready, 1)
                clear(nc, q)
        make_scale("a", mx, unit["a"], (scale["g"][:, :], 1.0 / 65536.0))

        with ExitStack() as once:
            q = signals(nc, once, "ai_ready prod_ready p_part p_total p_done")
            tl = carve([(f"ai{k}", I16) for k in range(3)], TP)
            with nc.Fori(0, NTOK // (TP * NPC)) as i:
                with nc.Block() as block:
                    @block.vector
                    def _(v):
                        def whole(n):
                            v.wait_ge(q.prod_ready, n + 1)
                            magnitude(v, n, raw[:, :, bass.ts(NPC * i + n, TP)], q.p_part, q.p_total, q.p_done)

                        for n in range(NPC):
                            v.wait_ge(q.ai_ready, n + 1)
                            v.tensor_tensor(raw[:, :, bass.ts(NPC * i + n, TP)], tl[f"ai{n % 3}"][:, :, :],
                                            up[:, :, bass.ts(NPC * i + n, TP)], ALU.mult).then_inc(q.prod_ready, 1)
                            if n:
                                whole(n - 1)
                        whole(NPC - 1)

                    @block.scalar
                    def _(a):
                        for n in range(NPC):
                            if n >= 3:
                                a.wait_ge(q.prod_ready, n - 2)
                            a.activation(tl[f"ai{n % 3}"], raw[:, :, bass.ts(NPC * i + n, TP)], ACT.Copy, scale=inv["a"][:, :]).then_inc(q.ai_ready, 1)
                clear(nc, q)
        make_scale("o", mx, unit["o"], (scale["a"][:, :], scale["u"][:, :]))

        with ExitStack() as once:
            K = 4
            q = signals(nc, once, "xf_in0 xf_in1 xf_in2 xf_in3 oi_ready of_ready y_psum y_ready y_out")
            arrived = (q.xf_in0, q.xf_in1, q.xf_in2, q.xf_in3)
            tl = carve((("of0", F32), ("of1", F32), ("oi", I16)), T)
            room = up[:, :, :].rearrange("p f t -> p (f t)").bitcast(F32)
            xin = [room[:, NT * D * k:NT * D * k + NT * D].rearrange("p (j n) -> p j n", j=NT) for k in range(K)]
            with nc.Fori(0, NG // K) as i:
                with nc.Block() as block:
                    @block.sync
                    def _(s):
                        for k in range(K):
                            s.dma_start(xin[k], dr["x_c"].rearrange("(i j p) n -> i p j n", p=128, j=NT)[K * i + k]).then_inc(arrived[k], 16)
                        for k in range(K):
                            s.wait_ge(q.y_ready, NT * (k + 1))
                            s.dma_start(out.rearrange("(i j p) n -> i p j n", p=128, j=NT)[K * i + k], xin[k]).then_inc(q.y_out, 16)
                        s.wait_ge(q.y_out, 16 * K)

                    @block.scalar
                    def _(a):
                        for k in range(K):
                            if k:
                                a.wait_ge(q.of_ready, k)
                            a.activation(tl["oi"], raw[:, :, bass.ts(K * i + k, T)], ACT.Copy, scale=inv["o"][:, :]).then_inc(q.oi_ready, 1)

                    @block.vector
                    def _(v):
                        def scale_back(k):
                            v.wait_ge(q.oi_ready, k + 1)
                            if k >= 2:
                                v.wait_ge(q.y_psum, NT * (k - 1))
                            v.tensor_scalar(tl[f"of{k % 2}"], tl["oi"], scale["o"][:, :], None, ALU.mult).then_inc(q.of_ready, 1)

                        scale_back(0)
                        scale_back(1)
                        for k in range(K):
                            v.wait_ge(arrived[k], 16)
                            for j in range(NT):
                                n = NT * k + j
                                v.wait_ge(q.y_psum, n + 1)
                                v.tensor_tensor(xin[k][:, j, :], P[n % 8][:, 0:D], xin[k][:, j, :], ALU.add).then_inc(q.y_ready, 1)
                            if k + 2 < K:
                                scale_back(k + 2)

                    @block.tensor
                    def _(p):
                        for k in range(K):
                            p.wait_ge(q.of_ready, k + 1)
                            for j in range(NT):
                                n = NT * k + j
                                if n >= 8:
                                    p.wait_ge(q.y_ready, n - 7)
                                for f in range(FC):
                                    t = p.matmul(P[n % 8][:, 0:D], tl[f"of{k % 2}"][:, f, 128 * j:128 * j + 128], wdT[:, f, :],
                                                 start=(f == 0), stop=(f == FC - 1))
                                t.then_inc(q.y_psum, 1)
                clear(nc, q)


class Common:
    pass


def program(nc, io, dr, out):
    ctx = ExitStack()
    with ctx:
        c = Common()
        c.banks = [ctx.enter_context(nc.psum_tensor(f"bank{k}", [128, 512], F32)) for k in range(8)]
        c.scattered = ctx.enter_context(nc.semaphore("scattered"))
        c.gathered = ctx.enter_context(nc.semaphore("gathered"))
        c.ident = ctx.enter_context(nc.sbuf_tensor("ident", [128, 128], F32))
        with ExitStack() as once:
            q = signals(nc, once, "ident_made")
            with nc.Block() as block:
                @block.gpsimd
                def _(g):
                    g.memset(c.ident[:, :], 0.0).then_inc(q.ident_made, 1)
                    g.wait_ge(q.ident_made, 1)
                    g.affine_select(out=c.ident[:, :], in_=c.ident[:, :], pattern=[[-1, 128]], base=0, channel_multiplier=1,
                                    compare_op=ALU.not_equal, fill=1.0).then_inc(q.ident_made, 1)
            clear(nc, q)
        layer0(nc, ctx, c, io, dr)
        c.wuT = ctx.enter_context(nc.sbuf_tensor("wuT", [128, 2, FF1], F32))
        c.wgT = ctx.enter_context(nc.sbuf_tensor("wgT", [128, 2, FF1], F32))
        c.wdT = ctx.enter_context(nc.sbuf_tensor("wdT", [128, FC, D], F32))
        experts(nc, ctx, c, io, dr)
        c.hT_all = ctx.enter_context(nc.sbuf_tensor("hT_all", [128, 2, B * S], F32))
        c.amax = ctx.enter_context(nc.sbuf_tensor("amax_all", [128, 1], F32))
        layer1(nc, ctx, c, io, dr)
        feed_forward(nc, ctx, c, io, dr, out)


def kernel(**inputs):
    import numpy as _np
    import concourse.bacc as _bacc
    from concourse import mybir as _mybir
    from concourse.bass_utils import run_bass_kernel_spmd as _run

    t = {k: _np.asarray(v) for k, v in inputs.items()}
    lay = {k: v for k, v in t.items()}
    lay["x"] = t["x"].reshape(B * S, D)
    lay["ctxT"] = t["ctx_1024"].transpose(0, 2, 1)
    lay["mask_Bx1xSxS2_ff0"] = t["mask_Bx1xSxS2_ff0"].reshape(B * S, S2)
    del lay["ctx_1024"]
    for k in ("L0_attn_Wq", "L0_attn_Wk", "L0_attn_Wv", "L0_attn_Wo", "L0_ffn_gate_w", "L1_attn_Wq",
              "L1_attn_Wkv_down", "L1_attn_Wk_up", "L1_attn_Wv_up", "L1_attn_Wo"):
        lay[k] = t[k].T
    for k in ("wq", "wk", "wv"):
        lay["L0_xattn_" + k] = t["L0_xattn_" + k].reshape(D, D)
    lay["L0_xattn_wo"] = t["L0_xattn_wo"].reshape(D, D)

    nc = _bacc.Bacc("TRN2", target_bir_lowering=False, num_devices=1)
    arrays, io = {}, {}
    for k, v in lay.items():
        arrays[k] = _np.ascontiguousarray(v)
        io[k] = nc.dram_tensor(k, v.shape, _mybir.dt.from_np(v.dtype), kind="ExternalInput").ap()
    f32, i32 = _mybir.dt.float32, _mybir.dt.int32
    dr = {}
    for k, shape, dt in (("x_a", (B * S, D), f32), ("x_c", (B * S, D), f32), ("slots_in", (SLOTS, D), f32),
                         ("slots_out", (SLOTS, D), f32), ("slot_g", (NG, 128, TOPK * NT), i32),
                         ("wt", (NG, 128, TOPK * NT), f32)):
        dr[k] = nc.dram_tensor("t_" + k, shape, dt, kind="Internal").ap()
    out = nc.dram_tensor("out", (B * S, D), f32, kind="ExternalOutput").ap()
    program(nc, io, dr, out)
    r = _run(nc, [arrays], core_ids=[0])
    return r.results[0]["out"].reshape(B, S, D)
```

```python
import numpy as np
import concourse.bass as bass
from concourse import mybir
from collections import namedtuple
from contextlib import ExitStack

F32 = mybir.dt.float32
BF16 = mybir.dt.bfloat16
I32 = mybir.dt.int32
U32 = mybir.dt.uint32
I16 = mybir.dt.int16
U16 = mybir.dt.uint16
ALU = mybir.AluOpType
ACT = mybir.ActivationFunctionType
AX = mybir.AxisListType
RMAX = bass.bass_isa.ReduceOp.max

B, S, D = 16, 256, 256
S2 = 77
H, HD = 16, 16
T = 512
NT = T // 128
NB = T // S
NG = B * S // T
E, TOPK = 16, 2
CAP = int(1.25 * B * S * TOPK / E)
SLOTS = E * CAP
FF0 = 512
H1, HD1 = 8, 64
LR = 64
FF1 = 768
FC = FF1 // 128
BLK = 32
LN_EPS = 1e-5
DEN_EPS = 1e-5
QMAX = 32767.0
WMAX = 7.0


def signals(nc, ctx, names):
    return namedtuple("Signals", names)(*[ctx.enter_context(nc.semaphore(name)) for name in names.split()])


def clear(nc, q):
    numbers = sorted(s.num for s in q)
    while numbers:
        run = 1
        while run < len(numbers) and numbers[run] == numbers[0] + run:
            run += 1
        nc.gpsimd.sem_clear(range(numbers[0], numbers[0] + run))
        numbers = numbers[run:]
    nc.all_engine_barrier()


def bcast(ap, axis, n):
    shape = list(ap.shape)
    shape.insert(axis, n)
    return ap.unsqueeze(axis).broadcast_to(shape)


class Norm:

    def __init__(self, nc, ctx, tag):
        sb = lambda name, shape: ctx.enter_context(nc.sbuf_tensor(f"{tag}_{name}", shape, F32))
        self.stats = sb("stats", [128, NT, 6])
        self.mv = sb("mean_var", [128, NT, 2])
        self.ve = sb("var_eps", [128, NT])
        self.rstd = sb("rstd", [128, NT])
        self.power = sb("power", [128, NT])
        self.h = sb("h", [128, NT, D])

    def vector(self, v, q, src, n, tiles=range(NT), before=None):
        self.moments(v, q, src, n, tiles, before)
        self.scale(v, q, src, n, tiles)

    def moments(self, v, q, src, n, tiles=range(NT), before=None):
        before = NT * n if before is None else before
        for j in tiles:
            v.bn_stats(self.stats[:, j, :], src[:, j, :]).then_inc(q.ln_stats, 1)
        v.wait_ge(q.ln_stats, before + len(tiles))
        for j in tiles:
            v.bn_aggr(self.mv[:, j, :], self.stats[:, j, :]).then_inc(q.ln_moments, 1)
        v.wait_ge(q.ln_moments, before + len(tiles))
        own = slice(tiles[0], tiles[-1] + 1)
        v.tensor_scalar(self.ve[:, own], self.mv[:, own, 1], LN_EPS, None, ALU.add).then_inc(q.ln_var, 1)

    def scale(self, v, q, src, n, tiles=range(NT)):
        v.wait_ge(q.ln_rstd, n + 1)
        for j in tiles:
            v.tensor_scalar(self.h[:, j, :], src[:, j, :], self.mv[:, j, 0:1], self.rstd[:, j:j + 1],
                            ALU.subtract, ALU.mult).then_inc(q.ln_h, 1)

    def gpsimd(self, g, q, n, tiles=range(NT)):
        own = slice(tiles[0], tiles[-1] + 1)
        g.wait_ge(q.ln_var, n + 1)
        g.tensor_tensor(self.rstd[:, own], self.ve[:, own], self.power[:, own], ALU.pow).then_inc(q.ln_rstd, 1)

    def tensor(self, p, q, n, banks, ident, before=None):
        before = NT * n if before is None else before
        for j in range(NT):
            p.wait_ge(q.ln_h, before + j + 1)
            for c in range(2):
                t = p.transpose(banks[c][:, 128 * j:128 * j + 128], self.h[:, j, 128 * c:128 * c + 128], ident)
        t.then_inc(q.hT_psum, 1)

    def scalar(self, a, q, n, banks, hT):
        a.wait_ge(q.hT_psum, n + 1)
        for c in range(2):
            a.activation(hT[:, c, :], banks[c][:, :], ACT.Copy).then_inc(q.hT_ready, 1)


def fill_selector(g, q, out, conditions):
    n = q[1]
    g.memset(out, 1.0).then_inc(q[0], 1)
    n += 1
    for base, mult, pattern, op in conditions:
        g.wait_ge(q[0], n)
        g.affine_select(out=out, in_=out, pattern=pattern, base=base, channel_multiplier=mult,
                        compare_op=op, fill=0.0).then_inc(q[0], 1)
        n += 1
    q[1] = n
    return n


def layer0(nc, ctx, c, io, dr):
    st = ExitStack()
    with st:
        def sb(name, shape, dt=F32):
            return st.enter_context(nc.sbuf_tensor("a_" + name, shape, dt))
        P = c.banks
        ident = c.ident[:, :]
        wq, wk, wv, wo = (sb(n, [128, 2, D]) for n in ("wq", "wk", "wv", "wo"))
        xwq, xwk, xwv, xwo = (sb(n, [128, 2, D]) for n in ("xwq", "xwk", "xwv", "xwo"))
        wg = sb("wg", [128, 2, E])
        bo = sb("bo", [128, D])
        causal = sb("causal", [128, 384])
        headsel = sb("headsel", [128, 8])
        before = sb("before", [128, 128], BF16)
        ones = sb("ones", [128, 128], BF16)
        eid = sb("eid", [128, E])
        carry = sb("carry", [128, E])
        left = sb("left", [128, 1])
        zeros = sb("zeros", [128, 2048])

        norm0, norm, norm2 = Norm(nc, st, "a0"), Norm(nc, st, "a1"), Norm(nc, st, "a2")
        xin = sb("xin", [128, NT, D])
        x1 = sb("x1", [128, NT, D])
        x2 = sb("x2", [128, NT, D])
        hT0 = sb("hT0", [128, 2, T])
        hT = sb("hT", [128, 2, T])
        eq = sb("eq", [128, 2, T])
        ek = sb("ek", [128, 2, T])
        pq = sb("pq", [128, 2, T])
        pk = sb("pk", [128, 2, T])
        kbd = sb("kbd", [128, NB, 2, 8, S])
        vpad = sb("vpad", [128, NT, H, 32])
        A = sb("A", [128, 8, 384])
        oT = sb("oT", [128, 4, T])
        rden = sb("rden", [128, NT, H])
        den = sb("den", [128, NT, H])
        at = sb("at", [128, NT, D])
        aT = sb("aT", [128, 2, T])

        ctxT = sb("ctxT", [128, 2, NB, S2])
        amask = sb("amask", [128, NT, S2])
        xqT = sb("xqT", [128, 2, T])
        xk = sb("xk", [128, 2, NB, S2])
        xkbd = sb("xkbd", [128, NB, 2, 8, S2])
        xvpad = sb("xvpad", [S2, NB, H, 32])
        L = sb("L", [128, 3, H, S2])
        Lm = sb("Lm", [128, NT, H])
        L2 = sb("L2", [128, 3, H, S2])
        PT = kbd[0:S2, :, :, :, :].rearrange("k b u h t -> k b (u h) t")

        lgT = sb("lgT", [E, T])
        lg = sb("lg", [128, NT, E])
        top = sb("top", [128, NT, 8])
        topi = sb("topi", [128, NT, 8], U32)
        topf = sb("topf", [128, NT, TOPK])
        oh = sb("oh", [128, TOPK, NT, E])
        M = sb("M", [128, NT + 1, E], BF16)
        rank = sb("rank", [128, NT, E])
        pick = sb("pick", [128, TOPK, NT, E])
        r = sb("r", [128, TOPK, NT])
        valid = sb("valid", [128, TOPK, NT])
        slot = sb("slot", [128, TOPK, NT])
        drop = sb("drop", [128, TOPK, NT])
        slot_s = sb("slot_s", [128, TOPK, NT], I32)
        slot_g = sb("slot_g", [128, TOPK, NT], I32)
        prob = sb("prob", [128, TOPK, NT])
        psum2 = sb("psum2", [128, NT])
        wt = sb("wt", [128, TOPK, NT])

        loads = signals(nc, st, "a_w a_const a_dve")
        weights = ((wk, io["L0_attn_Wk"]), (wq, io["L0_attn_Wq"]), (wv, io["L0_attn_Wv"]),
                   (wo, io["L0_attn_Wo"]), (xwq, io["L0_xattn_wq"]), (xwk, io["L0_xattn_wk"]),
                   (xwv, io["L0_xattn_wv"]), (xwo, io["L0_xattn_wo"]), (wg, io["L0_ffn_gate_w"]))
        NLOAD = len(weights) + 1

        def load_weights(s):
            for dst, src in weights:
                s.dma_start(dst[:, :, :], src.rearrange("(c p) n -> p c n", p=128)).then_inc(loads.a_w, 16)
            s.dma_start(bo[:, :], io["L0_attn_bo"].unsqueeze(0).broadcast_to([128, D])).then_inc(loads.a_w, 16)

        def constants(v):
            v.memset(zeros[:, :], 0.0).then_inc(loads.a_dve, 1)
            v.memset(vpad[:, :, :, :], 0.0).then_inc(loads.a_dve, 1)
            v.memset(xvpad[:, :, :, :], 0.0).then_inc(loads.a_dve, 1)
            v.memset(carry[:, :], 0.0).then_inc(loads.a_dve, 1)
            v.memset(ones[:, :], 1.0).then_inc(loads.a_dve, 1)
            v.memset(M[:, NT, :], 0.0).then_inc(loads.a_dve, 1)
            v.wait_ge(loads.a_dve, 6)
            v.memset(vpad[:, :, :, HD:HD + 1], 1.0).then_inc(loads.a_dve, 1)
            v.memset(xvpad[:, :, :, HD:HD + 1], 1.0).then_inc(loads.a_dve, 1)

        def selectors(g):
            k = [loads.a_const, 3]
            fill_selector(g, k, headsel[:, :], [(0, 1, [[-16, 8]], ALU.is_ge), (15, -1, [[16, 8]], ALU.is_ge)])
            fill_selector(g, k, causal[:, 0:128], [(0, -1, [[1, 128]], ALU.is_ge)])
            g.memset(causal[:, 128:256], 1.0)
            fill_selector(g, k, causal[:, 256:384], [(0, -1, [[1, 128]], ALU.is_ge)])
            fill_selector(g, k, before[:, :], [(0, -1, [[1, 128]], ALU.is_gt)])
            g.iota(eid[:, :], [[1, E]], base=0, channel_multiplier=0, allow_small_or_imprecise_dtypes=True)

        q = signals(nc, st, "x_in ctx_in next_in ln_stats ln_moments ln_var ln_rstd ln_h hT_psum hT_ready xh_psum xh_ready q_psum "
                            "v_psum eq_ready ek_ready eq_min ek_min pq_ready pk_ready kbd_ready kbd1_ready v_ready s_psum A_ready "
                            "o_psum oT_ready tok_psum den_ready rden_ready at_ready aT_psum aT_ready proj_psum xb_ready x1_ready "
                            "xk_psum xv_psum xq_psum xk_ready xkbd_ready xv_ready xq_ready l_psum L_ready Lm_ready L2_ready "
                            "exp_ready pt_psum PT_ready x2_ready gate_psum lg_ready top_ready topi_ready router "
                            "lgT_psum lgT_ready eneg rank_psum slots_ready stored x2_stored kept zeroed")
        scattered = c.scattered
        x_rows = io["x"].rearrange("(i j p) n -> i p j n", p=128, j=NT)
        y_rows = dr["x_a"].rearrange("(i j p) n -> i p j n", p=128, j=NT)
        ctx_cols = io["ctxT"].rearrange("(i b) (c p) k -> i c p b k", b=NB, p=128)
        mask_rows = io["mask_Bx1xSxS2_ff0"].rearrange("(i j p) k -> i p j k", p=128, j=NT)
        slot_rows = dr["slots_in"].rearrange("(a p r) n -> a p (r n)", p=128, r=8)

        def router_scalar(a):
            a.wait_ge(q.top_ready, NT)
            a.activation(prob[:, :, :], top[:, :, 0:TOPK].rearrange("p j k -> p k j"), ACT.Exp, scale=-1.0).then_inc(q.eneg, 1)

        def router_logits(p):
            for u in range(2):
                t = p.matmul(P[7][0:E, :], wg[:, u, :], hT[:, u, :], start=(u == 0), stop=(u == 1))
            t.then_inc(q.lgT_psum, 1)

        def router_keep(a):
            a.wait_ge(q.lgT_psum, 1)
            a.activation(lgT[:, :], P[7][0:E, :], ACT.Copy).then_inc(q.lgT_ready, 1)

        def router_turn(p):
            p.wait_ge(q.lgT_ready, 1)
            for j in range(NT):
                t = p.transpose(P[6][:, E * j:E * j + E], lgT[:, 128 * j:128 * j + 128], c.ident[0:E, 0:E])
            t.then_inc(q.gate_psum, 1)

        def router_largest(v):
            v.wait_ge(q.gate_psum, 1)
            v.tensor_copy(lg[:, :, :], P[6][:, 0:NT * E].rearrange("p (j e) -> p j e", e=E)).then_inc(q.lg_ready, 1)
            v.wait_ge(q.lg_ready, 1)
            for j in range(NT):
                v.max(top[:, j, :], lg[:, j, :]).then_inc(q.top_ready, 1)

        def router_choose(v):
            v.wait_ge(q.top_ready, NT)
            for j in range(NT):
                v.max_index(topi[:, j, :], top[:, j, :], lg[:, j, :]).then_inc(q.topi_ready, 1)
            v.wait_ge(q.topi_ready, NT)
            v.tensor_copy(topf[:, :, :], topi[:, :, 0:TOPK]).then_inc(q.router, 1)
            v.wait_ge(q.router, 1)
            for k in range(TOPK):
                v.tensor_tensor(oh[:, k, :, :], bcast(eid[:, :], 1, NT), bcast(topf[:, :, k], 2, E), ALU.is_equal).then_inc(q.router, 1)
            v.wait_ge(q.router, 3)
            v.tensor_tensor(M[:, 0:NT, :], oh[:, 0, :, :], oh[:, 1, :, :], ALU.add).then_inc(q.kept, 1)

        def router_rank(p):
            p.wait_ge(q.kept, 1)
            p.matmul(P[6][:, 0:NT * E + E], before[:, :], M[:, :, :], start=True, stop=False, skip_group_check=True)
            for k in range(1, NT + 1):
                t = p.matmul(P[6][:, E * k:E * (NT + 1)], ones[:, :], M[:, 0:NT + 1 - k, :], start=False, stop=(k == NT),
                             skip_group_check=True)
            t.then_inc(q.rank_psum, 1)

        def router_steps(v, done):
            steps = [done]

            def step(ins):
                ins.then_inc(q.router, 1)
                steps[0] += 1
                v.wait_ge(q.router, steps[0])
            return step

        def router_weights(v):
            step = router_steps(v, 3)
            v.wait_ge(q.eneg, 1)
            step(v.tensor_scalar(prob[:, :, :], prob[:, :, :], 1.0, None, ALU.add))
            step(v.reciprocal(prob[:, :, :], prob[:, :, :]))
            step(v.tensor_tensor(psum2[:, :], prob[:, 0, :], prob[:, 1, :], ALU.add))
            step(v.tensor_scalar(psum2[:, :], psum2[:, :], 1e-6, None, ALU.add))
            step(v.reciprocal(psum2[:, :], psum2[:, :]))
            step(v.tensor_tensor(wt[:, :, :], prob[:, :, :], bcast(psum2[:, :], 1, TOPK), ALU.mult))

        def router_ranks(v):
            step = router_steps(v, 9)
            v.wait_ge(q.rank_psum, 1)
            step(v.tensor_tensor(rank[:, :, :], P[6][:, 0:NT * E].rearrange("p (j e) -> p j e", e=E), bcast(carry[:, :], 1, NT), ALU.add))
            step(v.tensor_tensor(carry[:, :], P[6][:, NT * E:NT * E + E], carry[:, :], ALU.add))
            for k in range(TOPK):
                step(v.tensor_tensor(pick[:, k, :, :], oh[:, k, :, :], rank[:, :, :], ALU.mult))
            step(v.tensor_reduce(r[:, :, :], pick[:, :, :, :], AX.X, ALU.add))

        def router_slots(v):
            step = router_steps(v, 14)
            step(v.tensor_scalar(valid[:, :, :], r[:, :, :], float(CAP), None, ALU.is_lt))
            step(v.scalar_tensor_tensor(slot[:, :, :], topf[:, :, :].rearrange("p j k -> p k j"), float(CAP), r[:, :, :], ALU.mult, ALU.add))
            step(v.tensor_scalar(drop[:, :, :], valid[:, :, :], -float(4 * SLOTS), float(4 * SLOTS), ALU.mult, ALU.add))
            step(v.tensor_tensor(slot[:, :, :], slot[:, :, :], drop[:, :, :], ALU.add))

        def router_place(v):
            step = router_steps(v, 18)
            step(v.tensor_copy(slot_s[:, :, :], slot[:, :, :]))
            step(v.tensor_scalar(slot_g[:, :, :], slot[:, :, :], float(SLOTS - 1), None, ALU.min))
            v.tensor_tensor(wt[:, :, :], wt[:, :, :], valid[:, :, :], ALU.mult).then_inc(q.slots_ready, 1)

        def router_scatter(g):
            g.wait_ge(q.slots_ready, 1)
            for k in range(TOPK):
                for j in range(NT):
                    g.indirect_dma_start(out=dr["slots_in"], out_offset=bass.IndirectOffsetOnAxis(ap=slot_s[:, k, j:j + 1], axis=0),
                                         in_=norm2.h[:, j, :], in_offset=None,
                                         bounds_check=SLOTS - 1, oob_is_err=False).then_inc(scattered, 16)

        def router_store(s, i):
            s.wait_ge(q.slots_ready, 1)
            s.dma_start(dr["slot_g"][i], slot_g[:, :, :].rearrange("p k j -> p (k j)")).then_inc(q.stored, 16)
            s.dma_start(dr["wt"][i], wt[:, :, :].rearrange("p k j -> p (k j)")).then_inc(q.stored, 16)

        def keys(p, n, halves):
            p.wait_ge(q.hT_ready, 2 * n)
            for m in halves:
                for u in range(2):
                    p.matmul(P[m][:, :], wk[:, u, 128 * m:128 * m + 128], hT0[:, u, :], start=(u == 0), stop=(u == 1))

        with nc.Block() as block:
            @block.sync
            def _(s):
                s.dma_start(xin[:, :, :], x_rows[0]).then_inc(q.x_in, 16)
                load_weights(s)
                s.wait_ge(loads.a_w, 16 * NLOAD)

            @block.vector
            def _(v):
                v.wait_ge(q.x_in, 16)
                norm0.vector(v, q, xin, 0)
                constants(v)

            @block.gpsimd
            def _(g):
                for m in (norm0, norm, norm2):
                    g.memset(m.power[:, :], -0.5).then_inc(loads.a_const, 1)
                g.wait_ge(loads.a_const, 3)
                norm0.gpsimd(g, q, 0)
                selectors(g)

            @block.tensor
            def _(p):
                norm0.tensor(p, q, 0, P[6:8], ident)
                p.wait_ge(loads.a_w, 16 * NLOAD)
                keys(p, 1, (0, 1))

            @block.scalar
            def _(a):
                norm0.scalar(a, q, 0, P[6:8], hT0)
        clear(nc, q)
        clear(nc, loads)

        def group(i, first):
            N1 = 0 if first else 1
            with nc.Block() as block:
                @block.sync
                def _(s):
                    for u in range(2):
                        s.dma_start(ctxT[:, u, :, :], ctx_cols[i, u]).then_inc(q.ctx_in, 16)
                    s.dma_start(amask[:, :, :], mask_rows[i]).then_inc(q.ctx_in, 16)
                    if first:
                        for a in range(SLOTS // 1024):
                            s.dma_start(slot_rows[a], zeros[:, :]).then_inc(q.zeroed, 16)
                    else:
                        s.dma_start(y_rows[i - 1], x2[:, :, :]).then_inc(q.x2_stored, 16)
                        router_store(s, i - 1)
                    s.wait_ge(q.x1_ready, NB)
                    s.dma_start(xin[:, :, :], x_rows[(i + 1) % NG]).then_inc(q.next_in, 16)
                    if first:
                        s.wait_ge(q.zeroed, 16 * (SLOTS // 1024))
                    else:
                        s.wait_ge(q.x2_stored, 16)
                        s.wait_ge(q.stored, 32)
                    s.wait_ge(q.next_in, 16)

                @block.gpsimd
                def _(g):
                    if not first:
                        norm2.gpsimd(g, q, 0)
                    for n, (b, u) in enumerate(((0, 1), (1, 0), (1, 1))):
                        if n == 0:
                            g.wait_ge(q.pk_ready, 2)
                        g.tensor_tensor(kbd[:, b, u, :, :], bcast(pk[:, u, S * b:S * b + S], 1, 8), bcast(headsel[:, :], 2, S),
                                        ALU.mult).then_inc(q.kbd1_ready, 1)
                    for j in range(NT):
                        g.tensor_tensor(xin[:, j, :], xin[:, j, :], bo[:, :], ALU.add).then_inc(q.xb_ready, 1)
                    g.wait_ge(q.xk_ready, 1)
                    for b in range(NB):
                        for u in range(2):
                            g.tensor_tensor(xkbd[:, b, u, :, :], bcast(xk[:, u, b, :], 1, 8), bcast(headsel[:, :], 2, S2),
                                            ALU.mult).then_inc(q.xkbd_ready, 1)
                    if not first:
                        router_scatter(g)

                    def less_maximum(j):
                        g.wait_ge(q.Lm_ready, j + 1)
                        if j >= 3:
                            g.wait_ge(q.pt_psum, 4 * (j - 2))
                        g.tensor_tensor(L2[:, j % 3, :, :], L[:, j % 3, :, :],
                                        bcast(Lm[:, j, :], 2, S2), ALU.subtract).then_inc(q.L2_ready, 1)

                    norm.gpsimd(g, q, N1, range(0, 2))
                    less_maximum(0)
                    norm.gpsimd(g, q, N1 + 1, range(2, 4))
                    less_maximum(1)
                    norm0.gpsimd(g, q, N1 + 2)
                    for j in range(2, NT):
                        less_maximum(j)
                    if not first:
                        g.wait_ge(scattered, 16 * TOPK * NT * i)
                        g.tensor_tensor(left[:, :], norm.power[:, 0:1], norm.power[:, 0:1], ALU.add)

                @block.tensor
                def _(p):
                    def to_tokens(n, b):
                        p.wait_ge(q.oT_ready, 8 * n + 4 * b + 4)
                        for j in (2 * b, 2 * b + 1):
                            for u in range(4):
                                t = p.transpose(P[6 + j % 2][:, 128 * u:128 * u + 128], oT[:, u, 128 * j:128 * j + 128], ident)
                            t.then_inc(q.tok_psum, 1)

                    def to_columns(n, b):
                        p.wait_ge(q.at_ready, NT * n + 2 * b + 2)
                        for j in (2 * b, 2 * b + 1):
                            for u in range(2):
                                t = p.transpose(P[6][:, S * u + 128 * (j % 2):S * u + 128 * (j % 2) + 128], at[:, j, 128 * u:128 * u + 128], ident)
                        t.then_inc(q.aT_psum, 1)

                    def project(n, b):
                        p.wait_ge(q.aT_ready, NB * n + b + 1)
                        w = wo if n == 0 else xwo
                        for j in (2 * b, 2 * b + 1):
                            for u in range(2):
                                t = p.matmul(P[7][:, D * (j % 2):D * (j % 2) + D], aT[:, u, 128 * j:128 * j + 128],
                                             w[:, u, :], start=(u == 0), stop=(u == 1))
                        t.then_inc(q.proj_psum, 1)

                    def turn_norm(b):
                        p.wait_ge(q.ln_h, NT * N1 + 2 * b + 2)
                        for j in (2 * b, 2 * b + 1):
                            for u in range(2):
                                t = p.transpose(P[6][:, S * u + 128 * (j % 2):S * u + 128 * (j % 2) + 128], norm.h[:, j, 128 * u:128 * u + 128], ident)
                        t.then_inc(q.xh_psum, 1)

                    def x_queries(b):
                        p.wait_ge(q.xh_ready, b + 1)
                        p.wait_ge(q.x1_ready, b + 1)
                        for m in range(2):
                            for u in range(2):
                                t = p.matmul(P[7][:, S * m:S * m + S], xwq[:, u, 128 * m:128 * m + 128], hT[:, u, S * b:S * b + S],
                                             start=(u == 0), stop=(u == 1))
                        t.then_inc(q.xq_psum, 1)

                    for m in range(2):
                        for u in range(2):
                            t = p.matmul(P[2 + m][:, :], wq[:, u, 128 * m:128 * m + 128], hT0[:, u, :], start=(u == 0), stop=(u == 1))
                        t.then_inc(q.q_psum, 1)
                    for j in range(NT):
                        for u in range(2):
                            t = p.matmul(P[6 + j // 2][:, D * (j % 2):D * (j % 2) + D], hT0[:, u, 128 * j:128 * j + 128], wv[:, u, :],
                                         start=(u == 0), stop=(u == 1))
                        t.then_inc(q.v_psum, 1)
                    p.wait_ge(q.ctx_in, 48)
                    for m in range(2):
                        for u in range(2):
                            t = p.matmul(P[4][:, 154 * m:154 * m + 154], xwk[:, u, 128 * m:128 * m + 128],
                                         ctxT[:, u, :, :].rearrange("p b k -> p (b k)"), start=(u == 0), stop=(u == 1))
                    t.then_inc(q.xk_psum, 1)
                    for b in range(NB):
                        for u in range(2):
                            t = p.matmul(P[5][0:S2, D * b:D * b + D], ctxT[:, u, b, :], xwv[:, u, :], start=(u == 0), stop=(u == 1))
                    t.then_inc(q.xv_psum, 1)
                    p.wait_ge(q.pk_ready, 2)
                    p.wait_ge(q.pq_ready, 2)

                    def lin_values(m):
                        b, u = m // 4, m % 4
                        if m >= 2:
                            p.wait_ge(q.oT_ready, m - 1)
                        for s in range(2):
                            for hh in range(4):
                                n = 4 * m + hh
                                p.wait_ge(q.A_ready, n + 1)
                                cols = slice(0, 256) if s == 0 else slice(256, 384)
                                t = p.matmul(P[4 + m % 2][32 * hh:32 * hh + 32, 128 * s:256], vpad[:, 2 * b + s, 4 * u + hh, :],
                                             A[:, n % 8, cols], start=(s == 0), stop=(s == 1), tile_position=(0, 32 * hh),
                                             skip_group_check=True)
                        t.then_inc(q.o_psum, 1)

                    for n in range(NB * H + 2):
                        if n < NB * H:
                            b, h = n // H, n % H
                            u = h // 8
                            if n == 0:
                                p.wait_ge(q.kbd_ready, 1)
                            elif h % 8 == 0:
                                p.wait_ge(q.kbd1_ready, 2 * b + u)
                            if n >= 4:
                                p.wait_ge(q.A_ready, n - 3)
                            p.matmul(P[n % 4][:, 0:256], kbd[:, b, u, h % 8, 0:128], pq[:, u, S * b:S * b + S], start=True, stop=True)
                            p.matmul(P[n % 4][:, 256:384], kbd[:, b, u, h % 8, 128:256], pq[:, u, S * b + 128:S * b + 256],
                                     start=True, stop=True).then_inc(q.s_psum, 1)
                        if n == 4:
                            p.wait_ge(q.v_ready, NT)
                            p.wait_ge(q.xk_ready, 1)
                            p.wait_ge(q.xv_ready, NB)
                            if not first:
                                norm2.tensor(p, q, 0, P[4:6], ident)
                        if n == 5 and not first:
                            p.wait_ge(q.hT_ready, 2)
                            router_logits(p)
                        if n == 7 and not first:
                            router_turn(p)
                        if n == 12 and not first:
                            router_rank(p)
                        if n >= 5 and n % 4 == 1:
                            lin_values((n - 5) // 4)
                        if n == 19:
                            if not first:
                                p.wait_ge(q.slots_ready, 1)
                            to_tokens(0, 0)
                        if n == 23:
                            to_columns(0, 0)
                        if n == 25:
                            project(0, 0)
                        if n == 30:
                            turn_norm(0)
                        if n == 32:
                            x_queries(0)
                    p.wait_ge(q.A_ready, NB * H)

                    def x_scores(j):
                        for u in range(4):
                            n = 4 * j + u
                            if n >= 4:
                                p.wait_ge(q.L_ready, n - 3)
                            p.matmul(P[n % 4][:, 0:308], xqT[:, u // 2, 128 * j:128 * j + 128],
                                     xkbd[:, j // 2, u // 2, 4 * (u % 2):4 * (u % 2) + 4, :].rearrange("p h k -> p (h k)"),
                                     start=True, stop=True).then_inc(q.l_psum, 1)

                    def x_turn(j):
                        p.wait_ge(q.exp_ready, j + 1)
                        for u in range(4):
                            n = 4 * j + u
                            if n >= 2:
                                p.wait_ge(q.PT_ready, n - 1)
                            for hh in range(4):
                                t = p.transpose(P[4 + n % 2][0:S2, 128 * hh:128 * hh + 128], L2[:, j % 3, 4 * u + hh, :], ident)
                            t.then_inc(q.pt_psum, 1)

                    def x_values(b):
                        p.wait_ge(q.PT_ready, 8 * b + 8)
                        for u in range(4):
                            m = 4 * b + u
                            if m >= 2:
                                p.wait_ge(q.oT_ready, 8 + m - 1)
                            for hh in range(4):
                                t = p.matmul(P[6 + m % 2][32 * hh:32 * hh + 32, 0:256], xvpad[:, b, 4 * u + hh, :],
                                             PT[:, b, 4 * u + hh, :], start=True, stop=True, tile_position=(0, 32 * hh))
                            t.then_inc(q.o_psum, 1)

                    p.wait_ge(q.xq_ready, 1)
                    p.wait_ge(q.xkbd_ready, 4)
                    x_scores(0)
                    to_tokens(0, 1)
                    x_scores(1)
                    to_columns(0, 1)
                    project(0, 1)
                    x_turn(0)
                    turn_norm(1)
                    x_queries(1)
                    x_turn(1)
                    p.wait_ge(q.xq_ready, 2)
                    x_scores(2)
                    x_values(0)
                    x_scores(3)
                    to_tokens(1, 0)
                    x_turn(2)
                    to_columns(1, 0)
                    x_turn(3)
                    project(1, 0)
                    p.wait_ge(q.PT_ready, 16)
                    norm0.tensor(p, q, N1, P[4:6], ident, NT * (N1 + 1))
                    p.wait_ge(q.x2_ready, 1)
                    x_values(1)
                    p.wait_ge(q.L_ready, 16)
                    keys(p, N1 + 1, (0,))
                    to_tokens(1, 1)
                    keys(p, N1 + 1, (1,))
                    to_columns(1, 1)
                    project(1, 1)

                @block.scalar
                def _(a):
                    for m in range(2):
                        a.activation(ek[:, m, :], P[m][:, :], ACT.Exp).then_inc(q.ek_ready, 1)
                    for m in range(2):
                        a.wait_ge(q.q_psum, m + 1)
                        a.activation(eq[:, m, :], P[2 + m][:, :], ACT.Exp).then_inc(q.eq_ready, 1)
                    for j in range(NT):
                        a.wait_ge(q.v_psum, 2 * (j // 2) + 2)
                        a.activation(vpad[:, j, :, 0:HD], P[6 + j // 2][:, D * (j % 2):D * (j % 2) + D].rearrange("p (h d) -> p h d", d=HD),
                                     ACT.Copy).then_inc(q.v_ready, 1)
                    a.wait_ge(q.xk_psum, 1)
                    a.activation(xk[:, :, :, :].rearrange("p c b k -> p (c b k)"), P[4][:, 0:308], ACT.Copy).then_inc(q.xk_ready, 1)
                    a.wait_ge(q.xv_psum, 1)
                    for b in range(NB):
                        a.activation(xvpad[:, b, :, 0:HD], P[5][0:S2, D * b:D * b + D].rearrange("p (h d) -> p h d", d=HD),
                                     ACT.Copy).then_inc(q.xv_ready, 1)
                    if not first:
                        norm2.scalar(a, q, 0, P[4:6], hT)

                    def keep_columns(n, b):
                        a.wait_ge(q.aT_psum, NB * n + b + 1)
                        a.activation(aT[:, :, S * b:S * b + S], P[6][:, :].rearrange("p (c t) -> p c t", c=2), ACT.Copy).then_inc(q.aT_ready, 1)

                    def keep_norm(b):
                        a.wait_ge(q.xh_psum, b + 1)
                        a.activation(hT[:, :, S * b:S * b + S], P[6][:, :].rearrange("p (c t) -> p c t", c=2), ACT.Copy).then_inc(q.xh_ready, 1)

                    def keep_queries(b):
                        a.wait_ge(q.xq_psum, b + 1)
                        a.activation(xqT[:, :, S * b:S * b + S], P[7][:, :].rearrange("p (c t) -> p c t", c=2), ACT.Copy,
                                     scale=HD ** -0.5).then_inc(q.xq_ready, 1)

                    if not first:
                        router_keep(a)
                    for m in range(8):
                        if m == 1 and not first:
                            router_scalar(a)
                        if m == 7:
                            keep_norm(0)
                            keep_queries(0)
                        a.wait_ge(q.o_psum, m + 1)
                        a.activation(oT[:, m % 4, S * (m // 4):S * (m // 4) + S], P[4 + m % 2][:, 0:256], ACT.Copy).then_inc(q.oT_ready, 1)
                        if m == 4:
                            keep_columns(0, 0)

                    def outputs(b):
                        for u in range(4):
                            m = 4 * b + u
                            a.wait_ge(q.o_psum, 8 + m + 1)
                            a.activation(oT[:, u, S * b:S * b + S], P[6 + m % 2][:, 0:256], ACT.Copy).then_inc(q.oT_ready, 1)

                    def exponents(j):
                        a.wait_ge(q.L2_ready, j + 1)
                        a.activation(L2[:, j % 3, :, :], L2[:, j % 3, :, :], ACT.Exp).then_inc(q.exp_ready, 1)

                    def by_key(j):
                        for u in range(4):
                            n = 4 * j + u
                            a.wait_ge(q.pt_psum, n + 1)
                            a.activation(PT[:, j // 2, 4 * u:4 * u + 4, 128 * (j % 2):128 * (j % 2) + 128],
                                         P[4 + n % 2][0:S2, :].rearrange("p (h t) -> p h t", h=4), ACT.Copy).then_inc(q.PT_ready, 1)

                    keep_columns(0, 1)
                    exponents(0)
                    by_key(0)
                    keep_norm(1)
                    exponents(1)
                    keep_queries(1)
                    by_key(1)
                    outputs(0)
                    exponents(2)
                    by_key(2)
                    keep_columns(1, 0)
                    exponents(3)
                    by_key(3)
                    norm0.scalar(a, q, N1, P[4:6], hT0)
                    outputs(1)
                    keep_columns(1, 1)

                @block.vector
                def _(v):
                    def divide(n, b, eps):
                        for j in (2 * b, 2 * b + 1):
                            v.wait_ge(q.tok_psum, NT * n + j + 1)
                            o = P[6 + j % 2][:, :].rearrange("p (h d) -> p h d", d=32)
                            v.tensor_scalar(den[:, j, :], o[:, :, HD], eps, None, ALU.add).then_inc(q.den_ready, 1)
                            v.wait_ge(q.den_ready, NT * n + j + 1)
                            v.reciprocal(rden[:, j, :], den[:, j, :]).then_inc(q.rden_ready, 1)
                            v.wait_ge(q.rden_ready, NT * n + j + 1)
                            v.tensor_tensor(at[:, j, :].rearrange("p (h d) -> p h d", d=HD), o[:, :, 0:HD],
                                            bcast(rden[:, j, :], 2, HD), ALU.mult).then_inc(q.at_ready, 1)

                    def add_stream(n, b, out, stream, done):
                        v.wait_ge(q.proj_psum, NB * n + b + 1)
                        v.tensor_tensor(out[:, 2 * b:2 * b + 2, :], P[7][:, :].rearrange("p (j n) -> p j n", j=2),
                                        stream[:, 2 * b:2 * b + 2, :], ALU.add).then_inc(done, 1)

                    def norm_moments(b):
                        v.wait_ge(q.x1_ready, b + 1)
                        norm.moments(v, q, x1, N1 + b, range(2 * b, 2 * b + 2), NT * N1 + 2 * b)

                    if not first:
                        norm2.moments(v, q, x2, 0)
                    for e, e_ready, e_min, e_pos, pos_ready, bank in ((ek, q.ek_ready, q.ek_min, pk, q.pk_ready, 0),
                                                                      (eq, q.eq_ready, q.eq_min, pq, q.pq_ready, 2)):
                        for m in range(2):
                            v.wait_ge(e_ready, m + 1)
                            v.tensor_scalar(e[:, m, :], e[:, m, :], 1.0, None, ALU.min).then_inc(e_min, 1)
                            v.wait_ge(e_min, m + 1)
                            v.scalar_tensor_tensor(e_pos[:, m, :], P[bank + m][:, :], 0.0, e[:, m, :], ALU.max, ALU.add).then_inc(pos_ready, 1)
                    v.wait_ge(q.pk_ready, 1)
                    v.tensor_tensor(kbd[:, 0, 0, :, :], bcast(pk[:, 0, 0:S], 1, 8), bcast(headsel[:, :], 2, S), ALU.mult).then_inc(q.kbd_ready, 1)
                    if not first:
                        norm2.scale(v, q, x2, 0)
                    for n in range(NB * H):
                        v.wait_ge(q.s_psum, n + 1)
                        if n >= 8:
                            v.wait_ge(q.o_psum, n // 4 - 1)
                        v.tensor_tensor(A[:, n % 8, :], P[n % 4][:, 0:384], causal[:, :], ALU.mult).then_inc(q.A_ready, 1)
                        if not first:
                            if n == 7:
                                router_largest(v)
                            if n == 8:
                                router_choose(v)
                            if n == 11:
                                router_weights(v)
                            if n == 13:
                                router_ranks(v)
                            if n == 14:
                                router_slots(v)
                            if n == 15:
                                router_place(v)
                        if n == 20:
                            divide(0, 0, DEN_EPS)
                        if n == 25:
                            v.wait_ge(q.xb_ready, NT)
                            add_stream(0, 0, x1, xin, q.x1_ready)
                        if n == 26:
                            norm_moments(0)
                        if n == 28:
                            norm.scale(v, q, x1, N1, range(0, 2))
                    def masked(j):
                        for u in range(4):
                            n = 4 * j + u
                            v.wait_ge(q.l_psum, n + 1)
                            if u == 0 and j >= 3:
                                v.wait_ge(q.L2_ready, j - 2)
                            v.tensor_tensor(L[:, j % 3, 4 * u:4 * u + 4, :], P[n % 4][:, 0:308].rearrange("p (h k) -> p h k", h=4),
                                            bcast(amask[:, j, :], 1, 4), ALU.add).then_inc(q.L_ready, 1)
                        v.wait_ge(q.L_ready, 4 * j + 4)
                        v.tensor_reduce(Lm[:, j, :], L[:, j % 3, :, :], AX.X, ALU.max).then_inc(q.Lm_ready, 1)

                    masked(0)
                    divide(0, 1, DEN_EPS)
                    masked(1)
                    add_stream(0, 1, x1, xin, q.x1_ready)
                    norm_moments(1)
                    norm.scale(v, q, x1, N1 + 1, range(2, 4))
                    v.wait_ge(q.next_in, 16)
                    norm0.moments(v, q, xin, N1 + 2, range(NT), NT * (N1 + 1))
                    masked(2)
                    masked(3)
                    divide(1, 0, 0.0)
                    norm0.scale(v, q, xin, N1 + 2)
                    if not first:
                        v.wait_ge(q.x2_stored, 16)
                    add_stream(1, 0, x2, x1, q.x2_ready)
                    divide(1, 1, 0.0)
                    add_stream(1, 1, x2, x1, q.x2_ready)
            clear(nc, q)

        group(0, True)
        with nc.Fori(1, NG) as i:
            group(i, False)

        with nc.Block() as block:
            @block.vector
            def _(v):
                norm2.vector(v, q, x2, 0)
                router_largest(v)
                router_choose(v)
                router_weights(v)
                router_ranks(v)
                router_slots(v)
                router_place(v)

            @block.tensor
            def _(p):
                norm2.tensor(p, q, 0, P[0:2], ident)
                p.wait_ge(q.hT_ready, 2)
                router_logits(p)
                router_turn(p)
                router_rank(p)

            @block.scalar
            def _(a):
                norm2.scalar(a, q, 0, P[0:2], hT)
                router_keep(a)
                router_scalar(a)

            @block.gpsimd
            def _(g):
                norm2.gpsimd(g, q, 0)
                router_scatter(g)
                g.wait_ge(scattered, 16 * TOPK * NT * NG)

            @block.sync
            def _(s):
                s.dma_start(y_rows[NG - 1], x2[:, :, :]).then_inc(q.x2_stored, 16)
                router_store(s, NG - 1)
                s.wait_ge(q.x2_stored, 16)
                s.wait_ge(q.stored, 32)
        clear(nc, q)


def experts(nc, ctx, c, io, dr):
    st = ExitStack()
    with st:
        def sb(name, shape, dt=F32):
            return st.enter_context(nc.sbuf_tensor("b_" + name, shape, dt))
        P = c.banks
        ident = c.ident[:, :]
        RT = CAP // 128
        HC = CAP // 2
        w1 = [sb(f"w1_{k}", [128, 2, FF0]) for k in range(2)]
        w2 = [sb(f"w2_{k}", [128, 4, D]) for k in range(2)]
        X = [sb(f"X_{k}", [128, RT, D]) for k in range(2)]
        XT = [sb(f"XT_{k}", [128, 2, CAP]) for k in range(2)]
        G = sb("G", [128, 4, CAP])
        Y = [sb(f"Y_{k}", [128, RT, D]) for k in range(2)]
        NE = 4
        W = [sb(f"w_rows_{k}", [128, FF1 * D // 128 // BLK, BLK]) for k in range(3)]
        Wi = sb("w_int", [128, FF1 * D // 128 // BLK, BLK], I16)
        wa = sb("w_amax", [128, FF1 * D // 128 // BLK])
        wi = sb("w_inv", [128, FF1 * D // 128 // BLK])
        WT = [w[:, :, :].rearrange("p c n -> p (c n)") for w in (c.wuT, c.wgT, c.wdT)]
        w1_d = io["L0_ffn_w1"].rearrange("e (c p) f -> e p c f", p=128)
        w2_d = io["L0_ffn_w2"].rearrange("e (c p) d -> e p c d", p=128)
        in_d = dr["slots_in"].rearrange("(e j p) d -> e p j d", p=128, j=RT)
        out_d = dr["slots_out"].rearrange("(e j p) d -> e p j d", p=128, j=RT)

        def load(s, e, k, done):
            s.dma_start(w1[k][:, :, :], w1_d[e]).then_inc(done, 16)
            s.dma_start(w2[k][:, :, :], w2_d[e]).then_inc(done, 16)
            s.dma_start(X[k][:, :, :], in_d[e]).then_inc(done, 16)

        q = signals(nc, st, "b_first b_in1 b_in2 b_in3 b_in4 xT_psum xT_ready g_psum g_ready y_psum y_ready b_out0 b_out1 b_out2 b_out3 "
                            "w_in w_steps wt_psum wt_ready")

        def by_width(p, k, n):
            for j in range(RT):
                if j >= 2 or n:
                    p.wait_ge(q.xT_ready, RT * n + j - 1)
                for u in range(2):
                    t = p.transpose(P[j % 2][:, 128 * u:128 * u + 128], X[k % 2][:, j, 128 * u:128 * u + 128], ident)
                t.then_inc(q.xT_psum, 1)

        def keep_width(v, k, n):
            for j in range(RT):
                v.wait_ge(q.xT_psum, RT * n + j + 1)
                if k >= 2 and j == 0:
                    v.wait_ge(q.g_psum, 8 * (k - 1))
                v.tensor_copy(XT[k % 2][:, :, 128 * j:128 * j + 128],
                              P[j % 2][:, 0:256].rearrange("p (c t) -> p c t", c=2)).then_inc(q.xT_ready, 1)

        with nc.Block() as block:
            @block.sync
            def _(s):
                load(s, 0, 0, q.b_first)

            @block.tensor
            def _(p):
                p.wait_ge(q.b_first, 48)
                by_width(p, 0, 0)

            @block.vector
            def _(v):
                keep_width(v, 0, 0)
        clear(nc, q)

        arrived = (None, q.b_in1, q.b_in2, q.b_in3, q.b_in4)
        left = (q.b_out1, q.b_out2, q.b_out3)

        def turn(e0, first):
            with nc.Block() as block:
                @block.sync
                def _(s):
                    load(s, e0 + 1, 1, arrived[1])
                    if first:
                        for k, (name, r) in enumerate((("L1_ffn_w_up", FC), ("L1_ffn_w_gate", FC), ("L1_ffn_w_down", D // 128))):
                            s.dma_start(W[k][:, :, :].rearrange("p a b -> p (a b)").rearrange("p (r n) -> p r n", r=r),
                                        io[name].rearrange("(r p) n -> p r n", p=128)).then_inc(q.w_in, 16)
                    if not first:
                        s.dma_start(out_d[e0 - 1], Y[1][:, :, :]).then_inc(q.b_out0, 16)
                    for k in range(NE):
                        s.wait_ge(q.y_ready, RT * (k + 1))
                        if k + 2 <= NE:
                            load(s, (e0 + k + 2) % E, k % 2, arrived[k + 2])
                        if k < NE - 1:
                            s.dma_start(out_d[e0 + k], Y[k % 2][:, :, :]).then_inc(left[k], 16)
                    for k in range(1, NE + 1):
                        s.wait_ge(arrived[k], 48)
                    for k in range(NE - 1):
                        s.wait_ge(left[k], 16)
                    if not first:
                        s.wait_ge(q.b_out0, 16)

                @block.tensor
                def _(p):
                    def weight_turned(k):
                        w = W[k][:, :, :].rearrange("p a b -> p (a b)")
                        nr = FC if k < 2 else D // 128
                        ncol = 2 * FC // nr
                        p.wait_ge(q.w_steps, 6 * (k + 1))
                        p.wait_ge(q.xT_ready, RT * (k + 1))
                        for n in range(2 * FC):
                            col, r = n // nr, n % nr
                            if n == 8:
                                p.wait_ge(q.wt_ready, 3 * k + 1)
                            t = p.transpose(P[(n // 4) % 2][:, 128 * (n % 4):128 * (n % 4) + 128],
                                            w[:, 128 * (ncol * r + col):128 * (ncol * r + col) + 128], ident)
                            if n % 4 == 3:
                                t.then_inc(q.wt_psum, 1)

                    for k in range(NE):
                        if k:
                            p.wait_ge(q.xT_ready, RT * k)
                        for n in range(8):
                            f, m = n // 2, n % 2
                            if n >= 2 or k:
                                p.wait_ge(q.g_ready, 8 * k + n - 1)
                            for u in range(2):
                                t = p.matmul(P[2 + n % 2][:, 0:HC], w1[k % 2][:, u, 128 * f:128 * f + 128], XT[k % 2][:, u, HC * m:HC * m + HC],
                                             start=(u == 0), stop=(u == 1))
                            t.then_inc(q.g_psum, 1)
                        p.wait_ge(arrived[k + 1], 48)
                        if first and k:
                            p.wait_ge(q.wt_ready, 3 * k)
                        by_width(p, k + 1, k)
                        p.wait_ge(q.g_ready, 8 * (k + 1))
                        for j in range(RT):
                            n = RT * k + j
                            if n >= 4:
                                p.wait_ge(q.y_ready, n - 3)
                            for f in range(4):
                                t = p.matmul(P[4 + n % 4][:, 0:D], G[:, f, 128 * j:128 * j + 128], w2[k % 2][:, f, :], start=(f == 0), stop=(f == 3))
                            t.then_inc(q.y_psum, 1)
                        if first and k < 3:
                            weight_turned(k)

                @block.scalar
                def _(a):
                    for k in range(NE):
                        for n in range(8):
                            f, m = n // 2, n % 2
                            a.wait_ge(q.g_psum, 8 * k + n + 1)
                            if k and n == 0:
                                a.wait_ge(q.y_psum, RT * k)
                            a.activation(G[:, f, HC * m:HC * m + HC], P[2 + n % 2][:, 0:HC], ACT.Gelu).then_inc(q.g_ready, 1)
                        if first and k < 3:
                            for m in range(3):
                                a.wait_ge(q.wt_psum, 3 * k + m + 1)
                                a.activation(WT[k][:, 512 * m:512 * m + 512], P[m % 2][:, :], ACT.Copy).then_inc(q.wt_ready, 1)

                @block.vector
                def _(v):
                    def quantise_weight(k):
                        n = [6 * k]

                        def step(ins):
                            ins.then_inc(q.w_steps, 1)
                            n[0] += 1
                            v.wait_ge(q.w_steps, n[0])

                        v.wait_ge(q.w_in, 48)
                        step(v.tensor_reduce(wa[:, :], W[k][:, :, :], AX.X, ALU.max, apply_absolute_value=True))
                        step(v.tensor_scalar(wa[:, :], wa[:, :], 1.0 / WMAX, 1e-12, ALU.mult, ALU.max))
                        step(v.reciprocal(wi[:, :], wa[:, :]))
                        step(v.tensor_tensor(Wi[:, :, :], W[k][:, :, :], bcast(wi[:, :], 2, BLK), ALU.mult))
                        step(v.tensor_scalar(Wi[:, :, :], Wi[:, :, :], WMAX, -WMAX - 1.0, ALU.min, ALU.max))
                        step(v.tensor_tensor(W[k][:, :, :], Wi[:, :, :], bcast(wa[:, :], 2, BLK), ALU.mult))

                    for k in range(NE):
                        keep_width(v, k + 1, k)
                        if first and k < 3:
                            quantise_weight(k)
                        for j in range(RT):
                            n = RT * k + j
                            v.wait_ge(q.y_psum, n + 1)
                            if j == 0 and k >= 2:
                                v.wait_ge(left[k - 2], 16)
                            if j == 0 and k == 1 and not first:
                                v.wait_ge(q.b_out0, 16)
                            v.tensor_copy(Y[k % 2][:, j, :], P[4 + n % 4][:, 0:D]).then_inc(q.y_ready, 1)
            clear(nc, q)

        turn(0, True)
        with nc.Fori(1, E // NE) as i:
            turn(NE * i, False)
        with nc.Block() as block:
            @block.sync
            def _(s):
                s.dma_start(out_d[E - 1], Y[1][:, :, :]).then_inc(q.b_out0, 16)
                s.wait_ge(q.b_out0, 16)
        clear(nc, q)


def layer1(nc, ctx, c, io, dr):
    st = ExitStack()
    with st:
        def sb(name, shape, dt=F32):
            return st.enter_context(nc.sbuf_tensor("c_" + name, shape, dt))
        P = c.banks
        ident = c.ident[:, :]
        HW = H1 * HD1
        NP = H1 // 2
        wq = sb("wq", [128, 2, HW])
        wdn = sb("wdn", [128, 2, LR])
        wku = sb("wku", [128, HW])
        wvu = sb("wvu", [128, HW])
        wo = sb("wo", [128, NP, D])
        xwq, xwk, xwv, xwo = (sb(n, [128, 2, D]) for n in ("xwq", "xwk", "xwv", "xwo"))
        bq, bqs, bk = (sb(n, [128, 2]) for n in ("bq", "bqs", "bk"))
        bv = sb("bv", [128, D])
        bo = sb("bo", [128, D])
        imask = sb("imask", [128, NB, S2], I32)
        keep = sb("keep", [128, NB, S2])
        pen = sb("pen", [128, NB, S2])

        norm0, norm, norm2 = Norm(nc, st, "c0"), Norm(nc, st, "c1"), Norm(nc, st, "c2")
        slot = sb("slot", [128, TOPK * NT], I32)
        wt = sb("wt", [128, TOPK * NT])
        rows = sb("rows", [128, TOPK, NT, D])
        arrived = sb("arrived", [128, 1])
        xin = sb("xin", [128, NT, D])
        x3 = sb("x3", [128, NT, D])
        x3_next = sb("x3_next", [128, NT, D])
        x4 = sb("x4", [128, NT, D])
        x5 = sb("x5", [128, NT, D])
        hT0 = sb("hT0", [128, 2, T])
        hT = sb("hT", [128, 2, T])
        qT = sb("qT", [128, NP, T])
        latT = sb("latT", [128, T])
        kz = sb("kz", [128, H1, T])
        vs = sb("vs", [128, NT, HW])
        nmax = sb("nmax", [128, NB * H1, 2])
        sums = sb("sums", [128, NB * H1, 2])
        rsum = sb("rsum", [128, NB * H1, 2])
        pr = sb("pr", [128, 4, 2, S])
        PT = sb("PT", [128, 4, 2, S])
        aT = sb("aT", [128, NP, T])
        ctxT = sb("ctxT", [128, 2, NB, S2])
        xqT = sb("xqT", [128, 2, T])
        xkT = sb("xkT", [128, 2, NB, S2])
        xv = sb("xv", [S2, NB, D])
        L = sb("L", [128, NT, S2])
        xm = sb("xm", [128, NT])
        xs = sb("xs", [128, NT])
        xr = sb("xr", [128, NT])
        xPT = sb("xPT", [S2, T])
        xaT = sb("xaT", [128, 2, T])
        amax = sb("amax", [128, 1])

        weights = ((wq[:, :, :], io["L1_attn_Wq"].rearrange("(c p) n -> p c n", p=128)),
                   (wdn[:, :, :], io["L1_attn_Wkv_down"].rearrange("(c p) n -> p c n", p=128)),
                   (wo[:, :, :], io["L1_attn_Wo"].rearrange("(c p) n -> p c n", p=128)),
                   (xwq[:, :, :], io["L1_xattn_Wq"].rearrange("(c p) n -> p c n", p=128)),
                   (xwk[:, :, :], io["L1_xattn_Wk"].rearrange("(c p) n -> p c n", p=128)),
                   (xwv[:, :, :], io["L1_xattn_Wv"].rearrange("(c p) n -> p c n", p=128)),
                   (xwo[:, :, :], io["L1_xattn_Wo"].rearrange("(c p) n -> p c n", p=128)),
                   (wku[0:LR, :], io["L1_attn_Wk_up"]),
                   (wvu[0:LR, :], io["L1_attn_Wv_up"]),
                   (bv[:, :], io["L1_xattn_bv"].unsqueeze(0).broadcast_to([128, D])),
                   (bo[:, :], io["L1_xattn_bo"].unsqueeze(0).broadcast_to([128, D])),
                   (imask[:, :, :], io["mask_SxS2_ik0"].rearrange("(j p) k -> p j k", p=128)))
        NLOAD = len(weights) + 4

        def load_weights(s):
            for dst, src in weights:
                s.dma_start(dst, src).then_inc(loads.c_w, 16)
            for dst, src in ((bq, io["L1_xattn_bq"]), (bk, io["L1_xattn_bk"])):
                for u in range(2):
                    s.dma_start(dst[:, u:u + 1], src[128 * u:128 * u + 128].unsqueeze(1)).then_inc(loads.c_w, 16)

        def constants(v):
            v.memset(wku[LR:128, :], 0.0)
            v.memset(wvu[LR:128, :], 0.0)
            v.memset(latT[LR:128, :], 0.0)
            v.memset(kz[:, :, :], 0.0)
            v.memset(c.amax[:, :], 0.0)

        def masks(v):
            v.wait_ge(loads.c_w, 16 * NLOAD)
            v.tensor_scalar(bqs[:, :], bq[:, :], HD ** -0.5, None, ALU.mult)
            v.tensor_scalar(keep[:, :, :], imask[:, :, :], 0.0, None, ALU.not_equal).then_inc(loads.c_dve, 1)
            v.wait_ge(loads.c_dve, 4)
            v.tensor_scalar(pen[:, :, :], keep[:, :, :], 1.0, 1e9, ALU.subtract, ALU.mult)

        q = signals(nc, st, "r_in x_in ctx_in rows_in mixed ln_stats ln_moments ln_var ln_rstd ln_h hT_psum hT_ready xh_psum xh_ready q_psum qT_ready "
                         "lat_ready k_psum kz_ready v_psum v_ready s_psum nmax_ready exp_ready rsum_ready pr_ready pt_psum PT_ready "
                         "a_psum aT_ready proj_psum x4_ready xb_ready xk_psum xv_psum xk_ready xv_ready xq_psum xq_ready l_psum "
                         "L_kept L_ready xm_ready xe_ready xr_ready xp_ready xpt_psum xPT_ready xa_psum xaT_ready xproj_psum "
                         "x5_ready amax_part amax_ready stored")
        gathered = c.gathered
        x5_rows = dr["x_c"].rearrange("(i j p) n -> i p j n", p=128, j=NT)
        NH = NB * H1
        SB = (0, 1, 6, 7)
        KB = (7, 6, 0, 1)
        QB = (4, 5, 2, 3)

        def fetch(s, i):
            s.dma_start(slot[:, :], dr["slot_g"][i]).then_inc(q.r_in, 16)
            s.dma_start(wt[:, :], dr["wt"][i]).then_inc(q.x_in, 16)
            s.dma_start(xin[:, :, :], dr["x_a"].rearrange("(i j p) n -> i p j n", p=128, j=NT)[i]).then_inc(q.x_in, 16)

        def gather(g):
            g.wait_ge(q.r_in, 16)
            for k in range(TOPK):
                for j in range(NT):
                    g.indirect_dma_start(out=rows[:, k, j, :], out_offset=None, in_=dr["slots_out"],
                                         in_offset=bass.IndirectOffsetOnAxis(ap=slot[:, NT * k + j:NT * k + j + 1], axis=0),
                                         bounds_check=SLOTS - 1, oob_is_err=False).then_inc(gathered, 16)

        def gathers_done(g, n):
            g.wait_ge(gathered, 16 * TOPK * NT * n)
            g.tensor_tensor(arrived[:, :], norm.power[:, 0:1], norm.power[:, 0:1], ALU.add).then_inc(q.rows_in, 1)

        def mix(v, x3, m):
            k, j = m // NT, m % NT
            if m == 0:
                v.wait_ge(q.x_in, 32)
                v.wait_ge(q.rows_in, 1)
            if k:
                v.wait_ge(q.mixed, m - NT + 1)
            v.scalar_tensor_tensor(x3[:, j, :], rows[:, k, j, :], wt[:, NT * k + j:NT * k + j + 1],
                                   x3[:, j, :] if k else xin[:, j, :], ALU.mult, ALU.add).then_inc(q.mixed, 1)

        def last_norm(v):
            norm2.vector(v, q, x5, 0)
            v.wait_ge(q.ln_h, NT)
            v.tensor_reduce(amax[:, :], norm2.h[:, :, :].rearrange("p j n -> p (j n)"), AX.X, ALU.max, apply_absolute_value=True).then_inc(q.amax_part, 1)
            v.wait_ge(q.amax_part, 1)
            v.tensor_tensor(c.amax[:, :], c.amax[:, :], amax[:, :], ALU.max).then_inc(q.amax_ready, 1)

        def keep_input(a, i):
            a.wait_ge(q.hT_psum, 1)
            for u in range(2):
                a.activation(c.hT_all[:, u, bass.ts(i, T)], P[u][:, :], ACT.Copy).then_inc(q.hT_ready, 1)

        def latent_ahead(p):
            for u in range(2):
                p.matmul(P[6][0:LR, :], wdn[:, u, :], hT0[:, u, :], start=(u == 0), stop=(u == 1))

        def queries_ahead(p, m):
            for u in range(2):
                p.matmul(P[QB[m]][:, :], wq[:, u, 128 * m:128 * m + 128], hT0[:, u, :], start=(u == 0), stop=(u == 1))

        loads = signals(nc, st, "c_w c_dve")
        with nc.Block() as block:
            @block.sync
            def _(s):
                fetch(s, 0)
                load_weights(s)
                s.wait_ge(loads.c_w, 16 * NLOAD)

            @block.gpsimd
            def _(g):
                for m in (norm0, norm, norm2):
                    g.memset(m.power[:, :], -0.5).then_inc(loads.c_dve, 1)
                gather(g)
                g.wait_ge(loads.c_dve, 3)
                gathers_done(g, 1)
                norm0.gpsimd(g, q, 0)

            @block.vector
            def _(v):
                constants(v)
                for m in range(2 * NT):
                    mix(v, x3, m)
                v.wait_ge(q.mixed, 2 * NT)
                norm0.vector(v, q, x3, 0)
                masks(v)

            @block.tensor
            def _(p):
                norm0.tensor(p, q, 0, P[4:6], ident)
                p.wait_ge(loads.c_w, 16 * NLOAD)
                p.wait_ge(q.hT_ready, 2)
                latent_ahead(p)
                for m in range(2):
                    queries_ahead(p, m)

            @block.scalar
            def _(a):
                norm0.scalar(a, q, 0, P[4:6], hT0)
        clear(nc, q)
        clear(nc, loads)

        def group(i, first):
            N1 = 0 if first else 1
            with nc.Block() as block:
                @block.sync
                def _(s):
                    fetch(s, (i + 1) % NG)
                    if not first:
                        s.dma_start(x5_rows[i - 1], x5[:, :, :]).then_inc(q.stored, 16)
                    for u in range(2):
                        s.dma_start(ctxT[:, u, :, :], io["ctxT"].rearrange("(i b) (c p) k -> i c p b k", b=NB, p=128)[i, u]).then_inc(q.ctx_in, 16)
                    s.wait_ge(q.x_in, 32)
                    if not first:
                        s.wait_ge(q.stored, 16)

                @block.gpsimd
                def _(g):
                    if not first:
                        norm2.gpsimd(g, q, 0)
                    gather(g)
                    for n in range(NH):
                        if n == NH // 2:
                            gathers_done(g, i + 2)
                        g.wait_ge(q.rsum_ready, n + 1)
                        for u in range(2):
                            g.tensor_scalar(pr[:, n % 4, u, :], pr[:, n % 4, u, :], rsum[:, n, u:u + 1], 1.0,
                                            ALU.mult, ALU.mult).then_inc(q.pr_ready, 1)
                    norm0.gpsimd(g, q, N1)
                    norm.gpsimd(g, q, N1 + 1, range(0, 2))
                    norm.gpsimd(g, q, N1 + 2, range(2, 4))
                    g.wait_ge(q.ln_h, NT * (N1 + 2))
                    for j in range(NT):
                        g.tensor_tensor(x4[:, j, :], x4[:, j, :], bo[:, :], ALU.add).then_inc(q.xb_ready, 1)

                @block.tensor
                def _(p):
                    for m in range(2, NP):
                        for u in range(2):
                            t = p.matmul(P[QB[m]][:, :], wq[:, u, 128 * m:128 * m + 128], hT0[:, u, :], start=(u == 0), stop=(u == 1))
                        t.then_inc(q.q_psum, 1)
                    p.wait_ge(q.lat_ready, 1)
                    for m in range(NP):
                        if m == 2 and not first:
                            norm2.tensor(p, q, 0, P[0:2], ident)
                            p.wait_ge(q.hT_ready, 2)
                        p.matmul(P[KB[m]][:, :], wku[:, 128 * m:128 * m + 128], latT[:, :], start=True, stop=True).then_inc(q.k_psum, 1)
                    for j in range(NT):
                        p.wait_ge(q.qT_ready, j + 1)
                        p.matmul(P[QB[j]][:, :], latT[:, 128 * j:128 * j + 128], wvu[:, :], start=True, stop=True).then_inc(q.v_psum, 1)
                    p.wait_ge(q.kz_ready, H1)

                    def scores(n):
                        b, h = n // H1, n % H1
                        if n >= 4:
                            p.wait_ge(q.exp_ready, 2 * (n - 3))
                        for u in range(2):
                            t = p.matmul(P[SB[n % 4]][:, S * u:S * u + S], qT[:, h // 2, S * b + 128 * u:S * b + 128 * u + 128],
                                         kz[:, h, S * b:S * b + S], start=True, stop=True)
                        t.then_inc(q.s_psum, 1)

                    def turn(n):
                        p.wait_ge(q.pr_ready, 2 * n + 2)
                        if n == 0:
                            p.wait_ge(q.v_ready, NT)
                        if n >= 2:
                            p.wait_ge(q.PT_ready, n - 1)
                        for k in range(2):
                            for u in range(2):
                                t = p.transpose(P[2 + n % 2][:, S * k + 128 * u:S * k + 128 * u + 128],
                                                pr[:, n % 4, u, 128 * k:128 * k + 128], ident)
                        t.then_inc(q.pt_psum, 1)

                    def values(m):
                        b, g = m // NP, m % NP
                        p.wait_ge(q.PT_ready, 2 * m + 2)
                        if m == 0:
                            p.wait_ge(q.v_ready, NT)
                        if m >= 2:
                            p.wait_ge(q.aT_ready, m - 1)
                        for k in range(2):
                            for e in range(2):
                                h = 2 * g + e
                                t = p.matmul(P[4 + m % 2][HD1 * e:HD1 * e + HD1, 0:S], vs[:, 2 * b + k, HD1 * h:HD1 * h + HD1],
                                             PT[:, (2 * m + e) % 4, k, :], start=(k == 0), stop=(k == 1),
                                             tile_position=(0, HD1 * e), skip_group_check=True)
                        t.then_inc(q.a_psum, 1)

                    def project(b):
                        p.wait_ge(q.aT_ready, NP * (b + 1))
                        for j in (2 * b, 2 * b + 1):
                            for m in range(NP):
                                t = p.matmul(P[6 + b][:, D * (j % 2):D * (j % 2) + D], aT[:, m, 128 * j:128 * j + 128], wo[:, m, :],
                                             start=(m == 0), stop=(m == NP - 1))
                        t.then_inc(q.proj_psum, 1)

                    for n in range(NH + 4):
                        if n < NH:
                            scores(n)
                        if 0 <= n - 3 < NH:
                            turn(n - 3)
                        if n == NH + 2:
                            p.wait_ge(q.exp_ready, 2 * (NH - 1))
                            project(0)
                        if n >= 5 and n % 2:
                            values((n - 5) // 2)
                    p.wait_ge(q.ctx_in, 32)
                    p.wait_ge(q.PT_ready, NH)
                    for m in range(2):
                        for u in range(2):
                            t = p.matmul(P[2][:, 154 * m:154 * m + 154], xwk[:, u, 128 * m:128 * m + 128],
                                         ctxT[:, u, :, :].rearrange("p b k -> p (b k)"), start=(u == 0), stop=(u == 1))
                    t.then_inc(q.xk_psum, 1)
                    for b in range(NB):
                        for u in range(2):
                            t = p.matmul(P[3][0:S2, D * b:D * b + D], ctxT[:, u, b, :], xwv[:, u, :], start=(u == 0), stop=(u == 1))
                    t.then_inc(q.xv_psum, 1)
                    project(1)
                    p.wait_ge(q.exp_ready, 2 * NH)

                    def turn_norm(b):
                        p.wait_ge(q.ln_h, NT * (N1 + 1) + 2 * b + 2)
                        for j in (2 * b, 2 * b + 1):
                            for u in range(2):
                                t = p.transpose(P[2 * b][:, S * u + 128 * (j % 2):S * u + 128 * (j % 2) + 128], norm.h[:, j, 128 * u:128 * u + 128], ident)
                        t.then_inc(q.xh_psum, 1)

                    def x_queries(b):
                        p.wait_ge(q.xh_ready, b + 1)
                        for m in range(2):
                            for u in range(2):
                                t = p.matmul(P[2 * b + 1][:, S * m:S * m + S], xwq[:, u, 128 * m:128 * m + 128], hT[:, u, S * b:S * b + S],
                                             start=(u == 0), stop=(u == 1))
                        t.then_inc(q.xq_psum, 1)

                    def x_scores(b):
                        p.wait_ge(q.xq_ready, 2 * b + 2)
                        for j in (2 * b, 2 * b + 1):
                            for u in range(2):
                                t = p.matmul(P[2 * b][:, S2 * (j % 2):S2 * (j % 2) + S2], xqT[:, u, 128 * j:128 * j + 128], xkT[:, u, b, :],
                                             start=(u == 0), stop=(u == 1))
                        t.then_inc(q.l_psum, 1)

                    def x_turn(b):
                        p.wait_ge(q.xp_ready, 2 * b + 2)
                        for j in (2 * b, 2 * b + 1):
                            t = p.transpose(P[2 * b + 1][0:S2, 128 * (j % 2):128 * (j % 2) + 128], L[:, j, :], ident)
                        t.then_inc(q.xpt_psum, 1)

                    def x_values(b):
                        p.wait_ge(q.xPT_ready, b + 1)
                        for u in range(2):
                            t = p.matmul(P[2 * b][:, S * u:S * u + S], xv[:, b, 128 * u:128 * u + 128], xPT[:, S * b:S * b + S], start=True, stop=True)
                        t.then_inc(q.xa_psum, 1)

                    def x_project(b):
                        p.wait_ge(q.xaT_ready, b + 1)
                        for j in (2 * b, 2 * b + 1):
                            for u in range(2):
                                t = p.matmul(P[2 * b + 1][:, D * (j % 2):D * (j % 2) + D], xaT[:, u, 128 * j:128 * j + 128], xwo[:, u, :],
                                             start=(u == 0), stop=(u == 1))
                        t.then_inc(q.xproj_psum, 1)

                    turn_norm(0)
                    norm0.tensor(p, q, N1, P[4:6], ident)
                    x_queries(0)
                    p.wait_ge(q.xk_ready, 2)
                    p.wait_ge(q.xv_ready, NB)
                    turn_norm(1)
                    x_scores(0)
                    p.wait_ge(q.hT_ready, 2 * (N1 + 1))
                    p.wait_ge(q.x4_ready, 1)
                    latent_ahead(p)
                    x_queries(1)
                    queries_ahead(p, 0)
                    x_scores(1)
                    x_turn(0)
                    x_values(0)
                    queries_ahead(p, 1)
                    x_turn(1)
                    x_project(0)
                    x_values(1)
                    x_project(1)

                @block.scalar
                def _(a):
                    a.activation(latT[0:LR, :], P[6][0:LR, :], ACT.Copy).then_inc(q.lat_ready, 1)
                    for m in range(NP):
                        if m >= 2:
                            a.wait_ge(q.q_psum, m - 1)
                        a.activation(qT[:, m, :], P[QB[m]][:, :], ACT.Copy, scale=HD1 ** -0.5).then_inc(q.qT_ready, 1)
                    if not first:
                        keep_input(a, i - 1)
                    for j in range(NT):
                        a.wait_ge(q.v_psum, j + 1)
                        a.activation(vs[:, j, :], P[QB[j]][:, :], ACT.Copy).then_inc(q.v_ready, 1)

                    def heads(m):
                        a.wait_ge(q.a_psum, m + 1)
                        a.activation(aT[:, m % NP, S * (m // NP):S * (m // NP) + S], P[4 + m % 2][:, 0:S], ACT.Copy).then_inc(q.aT_ready, 1)

                    for n in range(NH):
                        a.wait_ge(q.nmax_ready, n + 1)
                        if n >= 4:
                            a.wait_ge(q.pt_psum, n - 3)
                        for u in range(2):
                            a.activation(pr[:, n % 4, u, :], P[SB[n % 4]][:, S * u:S * u + S], ACT.Exp, bias=nmax[:, n, u:u + 1],
                                         accum_out=sums[:, n, u:u + 1]).then_inc(q.exp_ready, 1)
                        if n >= 7 and n % 2:
                            heads((n - 7) // 2)
                    heads(NH // 2 - 3)
                    heads(NH // 2 - 2)
                    heads(NH // 2 - 1)
                    a.wait_ge(q.xk_psum, 1)
                    for m in range(2):
                        a.activation(xkT[:, m, :, :].rearrange("p b k -> p (b k)"), P[2][:, 154 * m:154 * m + 154], ACT.Identity,
                                     bias=bk[:, m:m + 1]).then_inc(q.xk_ready, 1)

                    def keep_norm(b):
                        a.wait_ge(q.xh_psum, b + 1)
                        a.activation(hT[:, :, S * b:S * b + S], P[2 * b][:, :].rearrange("p (c t) -> p c t", c=2), ACT.Copy).then_inc(q.xh_ready, 1)

                    def keep_queries(b):
                        a.wait_ge(q.xq_psum, b + 1)
                        for m in range(2):
                            a.activation(xqT[:, m, S * b:S * b + S], P[2 * b + 1][:, S * m:S * m + S], ACT.Identity, bias=bqs[:, m:m + 1],
                                         scale=HD ** -0.5).then_inc(q.xq_ready, 1)

                    def exponents(b):
                        a.wait_ge(q.xm_ready, b + 1)
                        for j in (2 * b, 2 * b + 1):
                            a.activation(L[:, j, :], L[:, j, :], ACT.Exp, bias=xm[:, j:j + 1], accum_out=xs[:, j:j + 1]).then_inc(q.xe_ready, 1)

                    def by_key(b):
                        a.wait_ge(q.xpt_psum, b + 1)
                        a.activation(xPT[:, S * b:S * b + S], P[2 * b + 1][0:S2, 0:S], ACT.Copy).then_inc(q.xPT_ready, 1)

                    def keep_heads(b):
                        a.wait_ge(q.xa_psum, b + 1)
                        a.activation(xaT[:, :, S * b:S * b + S], P[2 * b][:, :].rearrange("p (c t) -> p c t", c=2), ACT.Copy).then_inc(q.xaT_ready, 1)

                    keep_norm(0)
                    norm0.scalar(a, q, N1, P[4:6], hT0)
                    keep_queries(0)
                    keep_norm(1)
                    exponents(0)
                    keep_queries(1)
                    by_key(0)
                    keep_heads(0)
                    exponents(1)
                    a.activation(x3[:, :, :], x3_next[:, :, :], ACT.Copy)
                    by_key(1)
                    keep_heads(1)

                @block.vector
                def _(v):
                    if not first:
                        last_norm(v)
                    for m in range(NP):
                        v.wait_ge(q.k_psum, m + 1)
                        for e in range(2):
                            rows_ = slice(HD1 * e, HD1 * e + HD1)
                            v.tensor_copy(kz[rows_, 2 * m + e, :], P[KB[m]][rows_, :]).then_inc(q.kz_ready, 1)

                    def maxima(n):
                        v.wait_ge(q.s_psum, n + 1)
                        v.tensor_reduce(nmax[:, n, :], P[SB[n % 4]][:, :].rearrange("p (u k) -> p u k", u=2), AX.X, ALU.max,
                                        negate=True).then_inc(q.nmax_ready, 1)

                    def invert(n):
                        v.wait_ge(q.exp_ready, 2 * n + 2)
                        v.reciprocal(rsum[:, n, :], sums[:, n, :]).then_inc(q.rsum_ready, 1)

                    def by_key(n):
                        v.wait_ge(q.pt_psum, n + 1)
                        if n >= 4:
                            v.wait_ge(q.a_psum, n // 2 - 1)
                        v.tensor_copy(PT[:, n % 4, :, :].rearrange("p k t -> p (k t)"), P[2 + n % 2][:, :]).then_inc(q.PT_ready, 1)

                    for n in range(NH + 3):
                        if n < NH:
                            maxima(n)
                        if 0 <= n - 1 < NH:
                            invert(n - 1)
                        if n >= 3:
                            by_key(n - 3)
                        if 0 <= n - 9 < 2 * NT:
                            mix(v, x3_next, n - 9)
                    v.wait_ge(q.mixed, 2 * NT)
                    norm0.vector(v, q, x3_next, N1)
                    v.wait_ge(q.xv_psum, 1)
                    for b in range(NB):
                        v.tensor_tensor(xv[:, b, :], P[3][0:S2, D * b:D * b + D], bv[0:S2, :], ALU.add).then_inc(q.xv_ready, 1)
                    for b in range(NB):
                        own = slice(2 * b, 2 * b + 2)
                        v.wait_ge(q.proj_psum, b + 1)
                        v.tensor_tensor(x4[:, own, :], P[6 + b][:, :].rearrange("p (j n) -> p j n", j=2), x3[:, own, :], ALU.add).then_inc(q.x4_ready, 1)
                        v.wait_ge(q.x4_ready, b + 1)
                        norm.moments(v, q, x4, N1 + 1 + b, range(2 * b, 2 * b + 2), NT * (N1 + 1) + 2 * b)
                        norm.scale(v, q, x4, N1 + 1 + b, range(2 * b, 2 * b + 2))

                    def masked(b):
                        own = slice(2 * b, 2 * b + 2)
                        v.wait_ge(q.l_psum, b + 1)
                        l = P[2 * b][:, 0:2 * S2].rearrange("p (r k) -> p r k", r=2)
                        v.tensor_tensor(L[:, own, :], l, keep[:, :, :], ALU.mult).then_inc(q.L_kept, 1)
                        v.wait_ge(q.L_kept, b + 1)
                        v.tensor_tensor(L[:, own, :], L[:, own, :], pen[:, :, :], ALU.add).then_inc(q.L_ready, 1)
                        v.wait_ge(q.L_ready, b + 1)
                        v.tensor_reduce(xm[:, own], L[:, own, :], AX.X, ALU.max, negate=True).then_inc(q.xm_ready, 1)

                    def normalised(b):
                        own = slice(2 * b, 2 * b + 2)
                        v.wait_ge(q.xe_ready, 2 * b + 2)
                        v.reciprocal(xr[:, own], xs[:, own]).then_inc(q.xr_ready, 1)
                        v.wait_ge(q.xr_ready, b + 1)
                        for j in (2 * b, 2 * b + 1):
                            v.tensor_scalar(L[:, j, :], L[:, j, :], xr[:, j:j + 1], None, ALU.mult).then_inc(q.xp_ready, 1)

                    def add_stream(b):
                        own = slice(2 * b, 2 * b + 2)
                        v.wait_ge(q.xproj_psum, b + 1)
                        v.tensor_tensor(x5[:, own, :], P[2 * b + 1][:, :].rearrange("p (j n) -> p j n", j=2), x4[:, own, :], ALU.add).then_inc(q.x5_ready, 1)

                    masked(0)
                    normalised(0)
                    masked(1)
                    normalised(1)
                    v.wait_ge(q.xb_ready, NT)
                    if not first:
                        v.wait_ge(q.stored, 16)
                    add_stream(0)
                    add_stream(1)
            clear(nc, q)

        group(0, True)
        with nc.Fori(1, NG) as i:
            group(i, False)

        with nc.Block() as block:
            @block.sync
            def _(s):
                s.dma_start(x5_rows[NG - 1], x5[:, :, :]).then_inc(q.stored, 16)
                s.wait_ge(q.stored, 16)

            @block.vector
            def _(v):
                last_norm(v)

            @block.gpsimd
            def _(g):
                norm2.gpsimd(g, q, 0)

            @block.tensor
            def _(p):
                norm2.tensor(p, q, 0, P[0:2], ident)

            @block.scalar
            def _(a):
                keep_input(a, NG - 1)
        clear(nc, q)


def feed_forward(nc, ctx, c, io, dr, out):
    st = ExitStack()
    with st:
        def sb(name, shape, dt=F32):
            return st.enter_context(nc.sbuf_tensor("d_" + name, shape, dt))
        P = c.banks
        ident = c.ident[:, :]
        NTOK = B * S
        wuT, wgT, wdT = c.wuT, c.wgT, c.wdT
        raw = sb("raw", [128, FC, NTOK])
        mx = sb("mx", [128, 1])
        amx = sb("amx", [128, 1])
        pcur = sb("pcur", [128, 8])
        gmx = [sb(f"gmx_{n}", [128, 1]) for n in range(2)]
        cur = sb("cur", [128, 4 * FC])
        cur1 = sb("cur1", [128, 1])
        scale = {k: sb("scale_" + k, [128, 1]) for k in "xugao"}
        inv = {k: sb("inv_" + k, [128, 1]) for k in "xugao"}
        unit = {k: sb("unit_" + k, [128, 1]) for k in "ao"}


        def make_scales(*kinds, zeroed=(mx,)):
            with ExitStack() as once:
                q = signals(nc, once, "all_max scale_steps")
                with nc.Block() as block:
                    @block.gpsimd
                    def _(g):
                        for n, (k, src, unit, factors) in enumerate(kinds):
                            g.partition_all_reduce(gmx[n][:, :], src[:, :], 128, RMAX).then_inc(q.all_max, 1)

                    @block.vector
                    def _(v):
                        steps = [0]

                        def step(ins):
                            ins.then_inc(q.scale_steps, 1)
                            steps[0] += 1
                            v.wait_ge(q.scale_steps, steps[0])

                        for n, (k, src, unit, factors) in enumerate(kinds):
                            if unit is not None:
                                step(v.tensor_scalar(unit[:, :], factors[0], factors[1], None, ALU.mult))
                            v.wait_ge(q.all_max, n + 1)
                            if unit is not None:
                                step(v.tensor_scalar(gmx[n][:, :], gmx[n][:, :], unit[:, :], None, ALU.mult))
                            step(v.tensor_scalar(scale[k][:, :], gmx[n][:, :], 1.0 / QMAX, 1e-12, ALU.mult, ALU.max))
                            step(v.reciprocal(inv[k][:, :], scale[k][:, :]))
                            if unit is not None:
                                step(v.tensor_scalar(inv[k][:, :], inv[k][:, :], unit[:, :], None, ALU.mult))
                        for m in zeroed:
                            v.memset(m[:, :], 0.0)
                clear(nc, q)

        def quantise_input():
            with ExitStack() as once:
                q = signals(nc, once, "xi_ready xq_ready")
                xi = raw[:, 0:1, :].bitcast(I16)
                with nc.Block() as block:
                    @block.scalar
                    def _(a):
                        part = xi[:, 0, 0:NTOK]
                        a.activation(part, c.hT_all[:, 0, :], ACT.Copy, scale=inv["x"][:, :]).then_inc(q.xi_ready, 1)
                        a.wait_ge(q.xi_ready, 1)
                        a.activation(c.hT_all[:, 0, :], part, ACT.Copy, scale=scale["x"][:, :])

                    @block.vector
                    def _(v):
                        part = xi[:, 0, NTOK:2 * NTOK]
                        v.tensor_scalar(part, c.hT_all[:, 1, :], inv["x"][:, :], None, ALU.mult).then_inc(q.xq_ready, 1)
                        v.wait_ge(q.xq_ready, 1)
                        v.tensor_scalar(c.hT_all[:, 1, :], part, scale["x"][:, :], None, ALU.mult)
                clear(nc, q)

        TP = T // 2
        NPC = 8

        def carve(tiles, width):
            room = c.hT_all[:, :, :].rearrange("p c t -> p (c t)")
            at, out = 0, {}
            for k, dt in tiles:
                words = FC * width // (1 if dt == F32 else 2)
                part = room[:, at:at + words]
                out[k] = (part if dt == F32 else part.bitcast(dt)).rearrange("p (f t) -> p f t", f=FC)
                at += words
            assert at <= 2 * B * S
            return out

        K = 4

        def bank_magnitude(v, n, ready, done):
            v.wait_ge(ready, n + 1)
            v.tensor_reduce(cur[:, n:n + 1], P[n % 8][:, :], AX.X, ALU.max, apply_absolute_value=True).then_inc(done, 1)

        def running(v, src, count, part, into, total, done):
            v.wait_ge(part, count)
            v.tensor_reduce(cur1[:, :], src[:, 0:count], AX.X, ALU.max).then_inc(total, 1)
            v.wait_ge(total, 1)
            v.tensor_tensor(into[:, :], into[:, :], cur1[:, :], ALU.max).then_inc(done, 1)

        def products(p, i, wT, cur_ready, r_psum):
            for n in range(K * FC):
                k, f = n // FC, n % FC
                if n >= 8:
                    p.wait_ge(cur_ready, n - 7)
                for u in range(2):
                    t = p.matmul(P[n % 8][:, :], wT[:, u, 128 * f:128 * f + 128], c.hT_all[:, u, bass.ts(K * i + k, T)],
                                 start=(u == 0), stop=(u == 1))
                t.then_inc(r_psum, 1)

        def keep_product(a, i, n, r_psum, raw_ready):
            a.wait_ge(r_psum, n + 1)
            a.activation(raw[:, n % FC, bass.ts(K * i + n // FC, T)], P[n % 8][:, :], ACT.Copy).then_inc(raw_ready, 1)

        make_scales(("x", c.amax, None, None))
        quantise_input()

        with ExitStack() as once:
            q = signals(nc, once, "g_psum_d graw_ready gcur_ready gcur_total gcur_done")
            with nc.Fori(0, NG // K) as i:
                with nc.Block() as block:
                    @block.vector
                    def _(v):
                        for n in range(K * FC):
                            bank_magnitude(v, n, q.graw_ready, q.gcur_ready)
                        running(v, cur, K * FC, q.gcur_ready, mx, q.gcur_total, q.gcur_done)

                    @block.tensor
                    def _(p):
                        products(p, i, wgT, q.gcur_ready, q.g_psum_d)

                    @block.scalar
                    def _(a):
                        for n in range(K * FC):
                            keep_product(a, i, n, q.g_psum_d, q.graw_ready)
                clear(nc, q)
        make_scales(("g", mx, None, None), zeroed=(mx, amx))
        gi = sb("gate_int", [128, FC, NTOK], I16)

        with ExitStack() as once:
            q = signals(nc, once, "u_psum_d uraw_ready ucur_ready ucur_total ucur_done gi_ready sig_ready sq_ready sq1_ready act_ready act_part act_total act_done")
            sig = (wgT[:, :, :].rearrange("p c n -> p (c n)").rearrange("p (f t) -> p f t", f=FC),
                   once.enter_context(nc.sbuf_tensor("sig_1", [128, FC, TP], F32)))
            sq = [once.enter_context(nc.sbuf_tensor(f"sig_int_{k}", [128, FC, TP], U16)) for k in range(2)]
            with nc.Fori(0, NG // K) as i:
                with nc.Block() as block:
                    @block.vector
                    def _(v):
                        def activate(n, done, between):
                            part = sig[n % 2][:, :, :]
                            v.wait_ge(done, n // 2 + 1)
                            v.tensor_tensor(part, sq[n % 2][:, :, :], gi[:, :, bass.ts(NPC * i + n, TP)], ALU.mult).then_inc(q.act_ready, 1)
                            between()
                            v.wait_ge(q.act_ready, n + 1)
                            v.tensor_reduce(pcur[:, n:n + 1], part, AX.XY, ALU.max, apply_absolute_value=True).then_inc(q.act_part, 1)

                        def banks(k, fs):
                            for f in fs:
                                bank_magnitude(v, FC * k + f, q.uraw_ready, q.ucur_ready)

                        for k in range(K):
                            v.wait_ge(q.sig_ready, 2 * k + 1)
                            if k:
                                v.wait_ge(q.act_ready, 2 * k - 1)
                            v.tensor_scalar(sq[0][:, :, :], sig[0][:, :, :], 65536.0, None, ALU.mult).then_inc(q.sq_ready, 1)
                            if k:
                                banks(k - 1, (4, ))
                            activate(2 * k, q.sq_ready, (lambda: banks(k - 1, (5, ))) if k else (lambda: None))
                            activate(2 * k + 1, q.sq1_ready, lambda: banks(k, (0, )))
                            banks(k, (1, 2, 3))
                        banks(K - 1, (4, 5))
                        running(v, cur, K * FC, q.ucur_ready, mx, q.ucur_total, q.ucur_done)
                        v.wait_ge(q.ucur_done, 1)
                        v.wait_ge(q.act_part, NPC)
                        v.tensor_reduce(cur1[:, :], pcur[:, 0:NPC], AX.X, ALU.max).then_inc(q.act_total, 1)
                        v.wait_ge(q.act_total, 1)
                        v.tensor_tensor(amx[:, :], amx[:, :], cur1[:, :], ALU.max).then_inc(q.act_done, 1)

                    @block.tensor
                    def _(p):
                        products(p, i, wuT, q.ucur_ready, q.u_psum_d)

                    @block.scalar
                    def _(a):
                        for k in range(K):
                            for n in (2 * k, 2 * k + 1):
                                part = gi[:, :, bass.ts(NPC * i + n, TP)]
                                a.activation(part, raw[:, :, bass.ts(NPC * i + n, TP)], ACT.Copy, scale=inv["g"][:, :]).then_inc(q.gi_ready, 1)
                                if n >= 2:
                                    a.wait_ge(q.act_part, n - 1)
                                a.wait_ge(q.gi_ready, n + 1)
                                a.activation(sig[n % 2][:, :, :], part, ACT.Sigmoid, scale=scale["g"][:, :]).then_inc(q.sig_ready, 1)
                            if k:
                                a.wait_ge(q.act_ready, 2 * k)
                            a.wait_ge(q.sig_ready, 2 * k + 2)
                            a.activation(sq[1][:, :, :], sig[1][:, :, :], ACT.Copy, scale=65536.0).then_inc(q.sq1_ready, 1)
                            for n in range(FC * k, FC * k + FC):
                                keep_product(a, i, n, q.u_psum_d, q.uraw_ready)
                clear(nc, q)
        make_scales(("u", mx, None, None), ("a", amx, unit["a"], (scale["g"][:, :], 1.0 / 65536.0)))

        with ExitStack() as once:
            q = signals(nc, once, "sg_ready sr_ready ui_ready ai_ready prod_ready p_part p_total p_done")
            tl = carve([(n + str(k), dt) for k in range(2) for n, dt in (("sig", F32), ("sq", U16), ("ui", I16), ("ai", I16))], TP)
            with nc.Fori(0, NTOK // (TP * NPC)) as i:
                with nc.Block() as block:
                    @block.vector
                    def _(v):
                        def magnitude(n):
                            v.wait_ge(q.prod_ready, n + 1)
                            v.tensor_reduce(pcur[:, n:n + 1], raw[:, :, bass.ts(NPC * i + n, TP)], AX.XY, ALU.max,
                                            apply_absolute_value=True).then_inc(q.p_part, 1)

                        for n in range(NPC):
                            k = n % 2
                            v.wait_ge(q.sr_ready, n + 1)
                            if n >= 2:
                                v.wait_ge(q.prod_ready, n - 1)
                            v.scalar_tensor_tensor(tl[f"ai{k}"], tl[f"sq{k}"], inv["a"][:, :], gi[:, :, bass.ts(NPC * i + n, TP)],
                                                   ALU.mult, ALU.mult).then_inc(q.ai_ready, 1)
                            if n:
                                magnitude(n - 1)
                            v.wait_ge(q.ui_ready, n + 1)
                            v.wait_ge(q.ai_ready, n + 1)
                            v.tensor_tensor(raw[:, :, bass.ts(NPC * i + n, TP)], tl[f"ai{k}"], tl[f"ui{k}"], ALU.mult).then_inc(q.prod_ready, 1)
                        magnitude(NPC - 1)
                        running(v, pcur, NPC, q.p_part, mx, q.p_total, q.p_done)

                    @block.scalar
                    def _(a):
                        for n in range(NPC):
                            k = n % 2
                            if n >= 2:
                                a.wait_ge(q.sr_ready, n - 1)
                            a.activation(tl[f"sig{k}"], gi[:, :, bass.ts(NPC * i + n, TP)], ACT.Sigmoid, scale=scale["g"][:, :]).then_inc(q.sg_ready, 1)
                            if n >= 2:
                                a.wait_ge(q.prod_ready, n - 1)
                            a.activation(tl[f"ui{k}"], raw[:, :, bass.ts(NPC * i + n, TP)], ACT.Copy, scale=inv["u"][:, :]).then_inc(q.ui_ready, 1)
                            a.wait_ge(q.sg_ready, n + 1)
                            a.activation(tl[f"sq{k}"], tl[f"sig{k}"], ACT.Copy, scale=65536.0).then_inc(q.sr_ready, 1)
                clear(nc, q)
        make_scales(("o", mx, unit["o"], (scale["a"][:, :], scale["u"][:, :])))

        with ExitStack() as once:
            q = signals(nc, once, "xf_in0 xf_in1 xf_in2 xf_in3 oi_ready of_ready y_psum y_ready y_out")
            pieces = [(0, 0), (0, 1)] + [(k, None) for k in range(1, K)]
            arrived = (q.xf_in0, q.xf_in1, q.xf_in2, q.xf_in3)
            tl = carve((("of0", F32), ("of1", F32), ("oi", I16)), T)
            room = gi[:, :, :].rearrange("p f t -> p (f t)").bitcast(F32)
            xin = [room[:, NT * D * k:NT * D * k + NT * D].rearrange("p (j n) -> p j n", j=NT) for k in range(K)]
            with nc.Fori(0, NG // K) as i:
                with nc.Block() as block:
                    @block.sync
                    def _(s):
                        for k in range(K):
                            s.dma_start(xin[k], dr["x_c"].rearrange("(i j p) n -> i p j n", p=128, j=NT)[K * i + k]).then_inc(arrived[k], 16)
                        for k in range(K):
                            s.wait_ge(q.y_ready, NT * (k + 1))
                            s.dma_start(out.rearrange("(i j p) n -> i p j n", p=128, j=NT)[K * i + k], xin[k]).then_inc(q.y_out, 16)
                        s.wait_ge(q.y_out, 16 * K)

                    def part(tile, half):
                        return tile if half is None else tile[:, :, TP * half:TP * half + TP]

                    @block.scalar
                    def _(a):
                        for n, (k, half) in enumerate(pieces):
                            if n >= 2:
                                a.wait_ge(q.of_ready, n)
                            r = raw[:, :, bass.ts(K * i + k, T)] if half is None else raw[:, :, bass.ts(NPC * i + half, TP)]
                            a.activation(part(tl["oi"], half), r, ACT.Copy, scale=inv["o"][:, :]).then_inc(q.oi_ready, 1)

                    @block.vector
                    def _(v):
                        def scale_back(n):
                            k, half = pieces[n]
                            v.wait_ge(q.oi_ready, n + 1)
                            if k >= 2:
                                v.wait_ge(q.y_psum, NT * (k - 1))
                            v.tensor_scalar(part(tl[f"of{k % 2}"], half), part(tl["oi"], half), scale["o"][:, :], None, ALU.mult).then_inc(q.of_ready, 1)

                        for n in range(3):
                            scale_back(n)
                        for k in range(K):
                            v.wait_ge(arrived[k], 16)
                            for j in range(NT):
                                n = NT * k + j
                                v.wait_ge(q.y_psum, n + 1)
                                v.tensor_tensor(xin[k][:, j, :], P[n % 8][:, 0:D], xin[k][:, j, :], ALU.add).then_inc(q.y_ready, 1)
                            if k + 2 < K:
                                scale_back(k + 3)

                    @block.tensor
                    def _(p):
                        for k in range(K):
                            for j in range(NT):
                                n = NT * k + j
                                p.wait_ge(q.of_ready, k + 2 if k else 1 + j // 2)
                                if n >= 8:
                                    p.wait_ge(q.y_ready, n - 7)
                                for f in range(FC):
                                    t = p.matmul(P[n % 8][:, 0:D], tl[f"of{k % 2}"][:, f, 128 * j:128 * j + 128], wdT[:, f, :],
                                                 start=(f == 0), stop=(f == FC - 1))
                                t.then_inc(q.y_psum, 1)
                clear(nc, q)


class Common:
    pass


def program(nc, io, dr, out):
    ctx = ExitStack()
    with ctx:
        c = Common()
        c.banks = [ctx.enter_context(nc.psum_tensor(f"bank{k}", [128, 512], F32)) for k in range(8)]
        c.scattered = ctx.enter_context(nc.semaphore("scattered"))
        c.gathered = ctx.enter_context(nc.semaphore("gathered"))
        c.ident = ctx.enter_context(nc.sbuf_tensor("ident", [128, 128], F32))
        with ExitStack() as once:
            q = signals(nc, once, "ident_made")
            with nc.Block() as block:
                @block.gpsimd
                def _(g):
                    g.memset(c.ident[:, :], 0.0).then_inc(q.ident_made, 1)
                    g.wait_ge(q.ident_made, 1)
                    g.affine_select(out=c.ident[:, :], in_=c.ident[:, :], pattern=[[-1, 128]], base=0, channel_multiplier=1,
                                    compare_op=ALU.not_equal, fill=1.0).then_inc(q.ident_made, 1)
            clear(nc, q)
        layer0(nc, ctx, c, io, dr)
        c.wuT = ctx.enter_context(nc.sbuf_tensor("wuT", [128, 2, FF1], F32))
        c.wgT = ctx.enter_context(nc.sbuf_tensor("wgT", [128, 2, FF1], F32))
        c.wdT = ctx.enter_context(nc.sbuf_tensor("wdT", [128, FC, D], F32))
        experts(nc, ctx, c, io, dr)
        c.hT_all = ctx.enter_context(nc.sbuf_tensor("hT_all", [128, 2, B * S], F32))
        c.amax = ctx.enter_context(nc.sbuf_tensor("amax_all", [128, 1], F32))
        layer1(nc, ctx, c, io, dr)
        feed_forward(nc, ctx, c, io, dr, out)


def kernel(**inputs):
    import numpy as _np
    import concourse.bacc as _bacc
    from concourse import mybir as _mybir
    from concourse.bass_utils import run_bass_kernel_spmd as _run

    t = {k: _np.asarray(v) for k, v in inputs.items()}
    lay = {k: v for k, v in t.items()}
    lay["x"] = t["x"].reshape(B * S, D)
    lay["ctxT"] = t["ctx_1024"].transpose(0, 2, 1)
    lay["mask_Bx1xSxS2_ff0"] = t["mask_Bx1xSxS2_ff0"].reshape(B * S, S2)
    del lay["ctx_1024"]
    for k in ("L0_attn_Wq", "L0_attn_Wk", "L0_attn_Wv", "L0_attn_Wo", "L0_ffn_gate_w", "L1_attn_Wq",
              "L1_attn_Wkv_down", "L1_attn_Wk_up", "L1_attn_Wv_up", "L1_attn_Wo"):
        lay[k] = t[k].T
    for k in ("wq", "wk", "wv"):
        lay["L0_xattn_" + k] = t["L0_xattn_" + k].reshape(D, D)
    lay["L0_xattn_wo"] = t["L0_xattn_wo"].reshape(D, D)

    nc = _bacc.Bacc("TRN2", target_bir_lowering=False, num_devices=1)
    arrays, io = {}, {}
    for k, v in lay.items():
        arrays[k] = _np.ascontiguousarray(v)
        io[k] = nc.dram_tensor(k, v.shape, _mybir.dt.from_np(v.dtype), kind="ExternalInput").ap()
    f32, i32 = _mybir.dt.float32, _mybir.dt.int32
    dr = {}
    for k, shape, dt in (("x_a", (B * S, D), f32), ("x_c", (B * S, D), f32), ("slots_in", (SLOTS, D), f32),
                         ("slots_out", (SLOTS, D), f32), ("slot_g", (NG, 128, TOPK * NT), i32),
                         ("wt", (NG, 128, TOPK * NT), f32)):
        dr[k] = nc.dram_tensor("t_" + k, shape, dt, kind="Internal").ap()
    out = nc.dram_tensor("out", (B * S, D), f32, kind="ExternalOutput").ap()
    program(nc, io, dr, out)
    r = _run(nc, [arrays], core_ids=[0])
    return r.results[0]["out"].reshape(B, S, D)
```
